# Optimizing a Trainium2 kernel written in Bass

```python
import numpy as np
import jax
import jax.numpy as jnp

def _softmax(x, axis=-1):
    return jax.nn.softmax(x, axis=axis)

def _gelu(x):
    return jax.nn.gelu(x, approximate=True)

def _silu(x):
    return jax.nn.silu(x)

def _sigmoid(x):
    return jax.nn.sigmoid(x)

def _layernorm(x, axis=-1, eps=1e-05):
    m = jnp.mean(x, axis=axis, keepdims=True)
    v = jnp.var(x, axis=axis, keepdims=True)
    return (x - m) / jnp.sqrt(v + eps)

def _scatter_add(tgt, idx, src, axis=0):
    return tgt.at[idx].add(src)

def _segment_sum(src, seg, n):
    return jax.ops.segment_sum(src, seg, n)
kernel_name = 'mk_flamingo_gated_d4_seqx_r8_226008'

def setup_inputs(seed: int=0):
    np.random.seed(seed)
    _w = jnp.asarray

    def _rec_inputs():
        import jax
        import jax.numpy as jnp
        _rk = jax.random.key(seed)
        x = -0.0005857 + 0.9999 * jax.random.normal(jax.random.fold_in(_rk, 1), (64, 64, 128), jnp.float32)
        _lenS = 64 - jax.random.randint(jax.random.fold_in(_rk, 7), (64,), 0, max(1, 64 // 4) + 1, jnp.int32)
        _lenS2 = 64 - jax.random.randint(jax.random.fold_in(_rk, 8), (64,), 0, max(1, 64 // 4) + 1, jnp.int32)
        _ctx_1024P = jax.random.normal(jax.random.fold_in(_rk, 11), (64, 16, 128), jnp.float32)
        _ctx_1024c = jax.random.dirichlet(jax.random.fold_in(_rk, 511), 0.3 * jnp.ones((16,), jnp.float32), (64, 64))
        _ctx_1024t = jnp.einsum('bsk,bkd->bsd', _ctx_1024c, _ctx_1024P)
        _ctx_1024t = _ctx_1024t * jax.lax.rsqrt(jnp.mean(jnp.square(_ctx_1024t)) + 1e-12) * 0.953939
        ctx_1024 = -0.000264403 + 1.00002 * (_ctx_1024t + 0.3 * jax.random.normal(jax.random.fold_in(_rk, 611), (64, 64, 128), jnp.float32))
        fside_1xSxS2_0 = 0.000675642 + 1.00031 * jax.random.normal(jax.random.fold_in(_rk, 12), (1, 64, 64), jnp.float32)
        _g = jax.random.normal(jax.random.fold_in(_rk, 9001), (2, 4), jnp.float32)
        _g = jnp.sign(_g) * jnp.maximum(jnp.abs(_g), 1.0) + (_g == 0) * 1.0
        g_xattn = _g[0]
        g_ffn = _g[1]
        return (x, ctx_1024, fside_1xSxS2_0, g_xattn, g_ffn)
    x, ctx_1024, fside_1xSxS2_0, g_xattn, g_ffn = _rec_inputs()

    def _L0_xattn_setup():
        import jax, jax.numpy as jnp
        import numpy as np
        D_MODEL = 128
        N_HEADS = 16
        D_K = D_MODEL // N_HEADS
        key = jax.random.key(seed)
        ks = jax.random.split(key, 12)
        B, S, D = (2, 256, D_MODEL)
        lim = 1.0 / np.sqrt(D)

        def lin(k):
            kw, kb = jax.random.split(k)
            W = jax.random.uniform(kw, (D, D), jnp.float32, -lim, lim)
            b = jax.random.uniform(kb, (D,), jnp.float32, -lim, lim)
            return (W, b)
        wq, bq = lin(ks[0])
        wk, bk = lin(ks[1])
        wv, bv = lin(ks[2])
        wo, bo = lin(ks[3])
        return {'query': jax.random.normal(ks[4], (B, S, D), jnp.float32), 'key': jax.random.normal(ks[5], (B, S, D), jnp.float32), 'value': jax.random.normal(ks[6], (B, S, D), jnp.float32), 'wq': wq, 'bq': bq, 'wk': wk, 'bk': bk, 'wv': wv, 'bv': bv, 'wo': wo, 'bo': bo, 'time_decay': jnp.float32(0.1)}
    _L0_xattn_all = _L0_xattn_setup()
    _L0_xattn_in = {k: v for k, v in _L0_xattn_all.items() if k in ('wq', 'bq', 'wk', 'bk', 'wv', 'bv', 'wo', 'bo', 'time_decay')}
    del _L0_xattn_all

    def _L0_ffn_setup():
        import jax, jax.numpy as jnp
        import numpy as np
        HID = 128
        NH = 16
        NKV = 4
        HD = HID // NH
        E = 8
        TOPK = 2
        FFN = 256
        EPS = 1e-05
        THETA = 10000.0

        def _rmsnorm(x, w):
            var = jnp.mean(x * x, axis=-1, keepdims=True)
            return x * jax.lax.rsqrt(var + EPS) * w

        def _rope_tables(S):
            inv_freq = 1.0 / THETA ** (jnp.arange(0, HD, 2, dtype=jnp.float32) / HD)
            freqs = jnp.arange(S, dtype=jnp.float32)[:, None] * inv_freq[None, :]
            emb = jnp.concatenate([freqs, freqs], axis=-1)
            return (jnp.cos(emb), jnp.sin(emb))

        def _apply_rope(t, cos, sin):
            t1, t2 = jnp.split(t, 2, axis=-1)
            rot = jnp.concatenate([-t2, t1], axis=-1)
            return t * cos[None, :, None, :] + rot * sin[None, :, None, :]
        key = jax.random.key(seed)
        ks = jax.random.split(key, 6)
        B, S = (1, 256)
        x = jax.random.normal(ks[0], (B, S, HID), dtype=jnp.float32)
        wqkv = jax.random.normal(ks[1], ((NH + 2 * NKV) * HD, HID), dtype=jnp.float32) * 0.02
        wo = jax.random.normal(ks[2], (HID, NH * HD), dtype=jnp.float32) * 0.02
        gate_w = jax.random.normal(ks[3], (E, HID), dtype=jnp.float32) * 0.02
        w13 = jax.random.normal(ks[4], (E, 2 * FFN, HID), dtype=jnp.float32) * 0.02
        w2 = jax.random.normal(ks[5], (E, HID, FFN), dtype=jnp.float32) * 0.02
        return {'x': x, 'ln1_w': jnp.ones((HID,), jnp.float32), 'ln2_w': jnp.ones((HID,), jnp.float32), 'wqkv': wqkv, 'wo': wo, 'gate_w': gate_w, 'w13': w13, 'w2': w2}
    _L0_ffn_all = _L0_ffn_setup()
    _L0_ffn_in = {k: v for k, v in _L0_ffn_all.items() if k in ('ln1_w', 'ln2_w', 'wqkv', 'wo', 'gate_w', 'w13', 'w2')}
    del _L0_ffn_all

    def _L1_xattn_setup():
        import jax, jax.numpy as jnp
        import numpy as np
        D_MODEL = 128
        N_HEADS = 16
        D_K = D_MODEL // N_HEADS
        WINDOW = 128
        NEG = -1000000000.0
        key = jax.random.key(seed)
        ks = jax.random.split(key, 11)
        B, S = (2, 256)
        scale = 1.0 / np.sqrt(D_MODEL)
        inp = {'Q': jax.random.normal(ks[0], (B, S, D_MODEL), jnp.float32), 'K': jax.random.normal(ks[1], (B, S, D_MODEL), jnp.float32), 'V': jax.random.normal(ks[2], (B, S, D_MODEL), jnp.float32), 'Wq': jax.random.normal(ks[3], (D_MODEL, D_MODEL), jnp.float32) * scale, 'bq': jnp.zeros((D_MODEL,), jnp.float32), 'Wk': jax.random.normal(ks[4], (D_MODEL, D_MODEL), jnp.float32) * scale, 'bk': jnp.zeros((D_MODEL,), jnp.float32), 'Wv': jax.random.normal(ks[5], (D_MODEL, D_MODEL), jnp.float32) * scale, 'bv': jnp.zeros((D_MODEL,), jnp.float32), 'Wo': jax.random.normal(ks[6], (D_MODEL, D_MODEL), jnp.float32) * scale, 'bo': jnp.zeros((D_MODEL,), jnp.float32)}
        return inp
    _L1_xattn_all = _L1_xattn_setup()
    _L1_xattn_in = {k: v for k, v in _L1_xattn_all.items() if k in ('Wq', 'bq', 'Wk', 'bk', 'Wv', 'bv', 'Wo', 'bo')}
    del _L1_xattn_all

    def _L1_ffn_setup():
        import jax, jax.numpy as jnp
        import numpy as np
        B, S, D = (4, 256, 128)
        E, F = (8, 512)
        key = jax.random.key(seed)
        ks = jax.random.split(key, 5)
        x = jax.random.normal(ks[0], (B, S, D), dtype=jnp.float32)
        switch_w = jax.random.normal(ks[1], (D, E), dtype=jnp.float32) * D ** (-0.5)
        switch_b = jnp.zeros((E,), dtype=jnp.float32)
        w1 = jax.random.normal(ks[2], (E, D, F), dtype=jnp.float32) * D ** (-0.5)
        b1 = jnp.zeros((E, F), dtype=jnp.float32)
        w2 = jax.random.normal(ks[3], (E, F, D), dtype=jnp.float32) * F ** (-0.5)
        b2 = jnp.zeros((E, D), dtype=jnp.float32)
        return {'x': x, 'switch_w': switch_w, 'switch_b': switch_b, 'w1': w1, 'b1': b1, 'w2': w2, 'b2': b2}
    _L1_ffn_all = _L1_ffn_setup()
    _L1_ffn_in = {k: v for k, v in _L1_ffn_all.items() if k in ('switch_w', 'switch_b', 'w1', 'b1', 'w2', 'b2')}
    del _L1_ffn_all

    def _L2_xattn_setup():
        import jax, jax.numpy as jnp
        import numpy as np
        import math
        D = 128
        B, S = (8, 256)

        def _proj(x, W1, b1, W2, b2):
            h = jnp.einsum('bsd,od->bso', x, W1) + b1
            return jnp.einsum('bsd,od->bso', h, W2) + b2
        key = jax.random.key(seed)
        ks = jax.random.split(key, 8)
        q = jax.random.normal(ks[0], (B, S, D), dtype=jnp.float32)
        k = jax.random.normal(ks[1], (B, S, D), dtype=jnp.float32)
        v1 = jax.random.normal(ks[2], (B, S, D), dtype=jnp.float32)
        mask = jax.random.normal(ks[3], (1, S, S), dtype=jnp.float32)
        lim = 1.0 / math.sqrt(D)
        W1 = jax.random.uniform(ks[4], (D, D), jnp.float32, -lim, lim)
        b1 = jax.random.uniform(ks[5], (D,), jnp.float32, -lim, lim)
        W2 = jax.random.uniform(ks[6], (D, D), jnp.float32, -lim, lim)
        b2 = jax.random.uniform(ks[7], (D,), jnp.float32, -lim, lim)
        return {'q': q, 'k': k, 'v1': v1, 'mask': mask, 'W1': W1, 'b1': b1, 'W2': W2, 'b2': b2}
    _L2_xattn_all = _L2_xattn_setup()
    _L2_xattn_in = {k: v for k, v in _L2_xattn_all.items() if k in ('W1', 'b1', 'W2', 'b2')}
    del _L2_xattn_all

    def _L2_ffn_setup():
        import jax, jax.numpy as jnp
        import numpy as np
        D_MODEL, D_FF, D2, DL = (128, 512, 64, 64)
        D1 = D_FF // D2
        BATCH, SEQ = (2, 128)
        KERNEL_SCALE = D2 ** 0.5
        key = jax.random.key(seed)
        ks = jax.random.split(key, 7)
        xav = lambda k, shape, fan: jax.random.normal(k, shape, jnp.float32) * (2.0 / sum(fan)) ** 0.5
        x = jax.random.normal(ks[0], (BATCH, SEQ, D_MODEL), jnp.float32)
        m1 = xav(ks[1], (D_MODEL, DL), (D_MODEL, DL))
        m2 = xav(ks[2], (DL, D1, D2), (DL, D_FF))
        mb = jax.random.normal(ks[3], (D1, D2), jnp.float32)
        w1 = xav(ks[4], (D_MODEL, D1, D2), (D_MODEL, D_FF))
        w2 = xav(ks[5], (D2, D1, D_MODEL), (D_FF, D_MODEL)) * KERNEL_SCALE
        b2 = jax.random.normal(ks[6], (D_MODEL,), jnp.float32)
        return {'x': x, 'm1': m1, 'm2': m2, 'mb': mb, 'w1': w1, 'w2': w2, 'b2': b2}
    _L2_ffn_all = _L2_ffn_setup()
    _L2_ffn_in = {k: v for k, v in _L2_ffn_all.items() if k in ('m1', 'm2', 'mb', 'w1', 'w2', 'b2')}
    del _L2_ffn_all

    def _L3_xattn_setup():
        import jax, jax.numpy as jnp
        import numpy as np
        D_MODEL = 128
        NUM_HEAD = 16
        key = jax.random.key(seed)
        ks = jax.random.split(key, 11)
        B, S, D = (2, 256, D_MODEL)
        s = 0.02
        return {'Q': jax.random.normal(ks[0], (B, S, D), jnp.float32), 'K': jax.random.normal(ks[1], (B, S, D), jnp.float32), 'V': jax.random.normal(ks[2], (B, S, D), jnp.float32), 'Wq': jax.random.normal(ks[3], (D, D), jnp.float32) * s, 'bq': jnp.zeros((D,), jnp.float32), 'Wk': jax.random.normal(ks[4], (D, D), jnp.float32) * s, 'bk': jnp.zeros((D,), jnp.float32), 'Wv': jax.random.normal(ks[5], (D, D), jnp.float32) * s, 'bv': jnp.zeros((D,), jnp.float32), 'Wo': jax.random.normal(ks[6], (D, D), jnp.float32) * s, 'bo': jnp.zeros((D,), jnp.float32)}
    _L3_xattn_all = _L3_xattn_setup()
    _L3_xattn_in = {k: v for k, v in _L3_xattn_all.items() if k in ('Wq', 'bq', 'Wk', 'bk', 'Wv', 'bv', 'Wo', 'bo')}
    del _L3_xattn_all

    def _L3_ffn_setup():
        import jax, jax.numpy as jnp
        import numpy as np
        HIDDEN = 128
        N_EXPERTS = 32
        MOE_I = 64
        N_GROUP = 4
        TOPK_GROUP = 2
        TOP_K = 6
        N_LOCAL_GROUPS = 16
        ANCHOR_I = 32
        SHARED_I = 64
        ROUTED_SCALE = 0.2
        ANCHOR_ALPHA = 0.1
        BATCH, SEQ = (1, 128)

        def _moe_forward(hidden_states, gate_weight, gate_bias, w_gate, w_up, w_down, shared_w_gate, shared_w_up, shared_w_down, anchor_w_gate, anchor_w_up, anchor_w_down):
            B, S, H = hidden_states.shape
            x = hidden_states.reshape(-1, H)
            T = x.shape[0]
            E = gate_weight.shape[0]
            L = anchor_w_gate.shape[0]
            logits = x @ gate_weight.T
            scores = jax.nn.sigmoid(logits)
            sc = scores + gate_bias
            grp = sc.reshape(T, N_GROUP, E // N_GROUP)
            group_scores = jax.lax.top_k(grp, 2)[0].sum(-1)
            _, gidx = jax.lax.top_k(group_scores, TOPK_GROUP)
            gmask = jax.nn.one_hot(gidx, N_GROUP, dtype=sc.dtype).sum(1)
            emask = jnp.repeat(gmask, E // N_GROUP, axis=1)
            masked = jnp.where(emask > 0, sc, -jnp.inf)
            _, topidx = jax.lax.top_k(masked, TOP_K)
            tw = jnp.take_along_axis(scores, topidx, axis=-1)
            tw = tw / (tw.sum(-1, keepdims=True) + 1e-20) * ROUTED_SCALE
            g = jnp.einsum('th,ehi->tei', x, w_gate)
            u = jnp.einsum('th,ehi->tei', x, w_up)
            eo = jnp.einsum('tei,eih->teh', jax.nn.silu(g) * u, w_down)
            cw = (jax.nn.one_hot(topidx, E, dtype=x.dtype) * tw[..., None]).sum(1)
            routed = jnp.einsum('te,teh->th', cw, eo)
            shared = jax.nn.silu(x @ shared_w_gate) * (x @ shared_w_up) @ shared_w_down
            lg = topidx[:, 0] // (E // L)
            ag = jnp.einsum('th,lhi->tli', x, anchor_w_gate)
            au = jnp.einsum('th,lhi->tli', x, anchor_w_up)
            ao = jnp.einsum('tli,lih->tlh', jax.nn.silu(ag) * au, anchor_w_down)
            acw = jax.nn.one_hot(lg, L, dtype=x.dtype)
            anchor = jnp.einsum('tl,tlh->th', acw, ao)
            out = routed + shared + ANCHOR_ALPHA * anchor
            return out.reshape(B, S, H)
        key = jax.random.key(seed)
        ks = jax.random.split(key, 13)
        s = 0.02
        return {'hidden_states': jax.random.normal(ks[0], (BATCH, SEQ, HIDDEN), jnp.float32), 'gate_weight': s * jax.random.normal(ks[1], (N_EXPERTS, HIDDEN), jnp.float32), 'gate_bias': s * jax.random.normal(ks[2], (N_EXPERTS,), jnp.float32), 'w_gate': s * jax.random.normal(ks[3], (N_EXPERTS, HIDDEN, MOE_I), jnp.float32), 'w_up': s * jax.random.normal(ks[4], (N_EXPERTS, HIDDEN, MOE_I), jnp.float32), 'w_down': s * jax.random.normal(ks[5], (N_EXPERTS, MOE_I, HIDDEN), jnp.float32), 'shared_w_gate': s * jax.random.normal(ks[6], (HIDDEN, SHARED_I), jnp.float32), 'shared_w_up': s * jax.random.normal(ks[7], (HIDDEN, SHARED_I), jnp.float32), 'shared_w_down': s * jax.random.normal(ks[8], (SHARED_I, HIDDEN), jnp.float32), 'anchor_w_gate': s * jax.random.normal(ks[9], (N_LOCAL_GROUPS, HIDDEN, ANCHOR_I), jnp.float32), 'anchor_w_up': s * jax.random.normal(ks[10], (N_LOCAL_GROUPS, HIDDEN, ANCHOR_I), jnp.float32), 'anchor_w_down': s * jax.random.normal(ks[11], (N_LOCAL_GROUPS, ANCHOR_I, HIDDEN), jnp.float32)}
    _L3_ffn_all = _L3_ffn_setup()
    _L3_ffn_in = {k: v for k, v in _L3_ffn_all.items() if k in ('gate_weight', 'gate_bias', 'w_gate', 'w_up', 'w_down', 'shared_w_gate', 'shared_w_up', 'shared_w_down', 'anchor_w_gate', 'anchor_w_up', 'anchor_w_down')}
    del _L3_ffn_all
    return {'x': x, 'ctx_1024': ctx_1024, 'fside_1xSxS2_0': fside_1xSxS2_0, 'g_xattn': g_xattn, 'g_ffn': g_ffn, 'L0_xattn_wq': _L0_xattn_in['wq'], 'L0_xattn_bq': _L0_xattn_in['bq'], 'L0_xattn_wk': _L0_xattn_in['wk'], 'L0_xattn_bk': _L0_xattn_in['bk'], 'L0_xattn_wv': _L0_xattn_in['wv'], 'L0_xattn_bv': _L0_xattn_in['bv'], 'L0_xattn_wo': _L0_xattn_in['wo'], 'L0_xattn_bo': _L0_xattn_in['bo'], 'L0_xattn_time_decay': _L0_xattn_in['time_decay'], 'L0_ffn_ln1_w': _L0_ffn_in['ln1_w'], 'L0_ffn_ln2_w': _L0_ffn_in['ln2_w'], 'L0_ffn_wqkv': _L0_ffn_in['wqkv'], 'L0_ffn_wo': _L0_ffn_in['wo'], 'L0_ffn_gate_w': _L0_ffn_in['gate_w'], 'L0_ffn_w13': _L0_ffn_in['w13'], 'L0_ffn_w2': _L0_ffn_in['w2'], 'L1_xattn_Wq': _L1_xattn_in['Wq'], 'L1_xattn_bq': _L1_xattn_in['bq'], 'L1_xattn_Wk': _L1_xattn_in['Wk'], 'L1_xattn_bk': _L1_xattn_in['bk'], 'L1_xattn_Wv': _L1_xattn_in['Wv'], 'L1_xattn_bv': _L1_xattn_in['bv'], 'L1_xattn_Wo': _L1_xattn_in['Wo'], 'L1_xattn_bo': _L1_xattn_in['bo'], 'L1_ffn_switch_w': _L1_ffn_in['switch_w'], 'L1_ffn_switch_b': _L1_ffn_in['switch_b'], 'L1_ffn_w1': _L1_ffn_in['w1'], 'L1_ffn_b1': _L1_ffn_in['b1'], 'L1_ffn_w2': _L1_ffn_in['w2'], 'L1_ffn_b2': _L1_ffn_in['b2'], 'L2_xattn_W1': _L2_xattn_in['W1'], 'L2_xattn_b1': _L2_xattn_in['b1'], 'L2_xattn_W2': _L2_xattn_in['W2'], 'L2_xattn_b2': _L2_xattn_in['b2'], 'L2_ffn_m1': _L2_ffn_in['m1'], 'L2_ffn_m2': _L2_ffn_in['m2'], 'L2_ffn_mb': _L2_ffn_in['mb'], 'L2_ffn_w1': _L2_ffn_in['w1'], 'L2_ffn_w2': _L2_ffn_in['w2'], 'L2_ffn_b2': _L2_ffn_in['b2'], 'L3_xattn_Wq': _L3_xattn_in['Wq'], 'L3_xattn_bq': _L3_xattn_in['bq'], 'L3_xattn_Wk': _L3_xattn_in['Wk'], 'L3_xattn_bk': _L3_xattn_in['bk'], 'L3_xattn_Wv': _L3_xattn_in['Wv'], 'L3_xattn_bv': _L3_xattn_in['bv'], 'L3_xattn_Wo': _L3_xattn_in['Wo'], 'L3_xattn_bo': _L3_xattn_in['bo'], 'L3_ffn_gate_weight': _L3_ffn_in['gate_weight'], 'L3_ffn_gate_bias': _L3_ffn_in['gate_bias'], 'L3_ffn_w_gate': _L3_ffn_in['w_gate'], 'L3_ffn_w_up': _L3_ffn_in['w_up'], 'L3_ffn_w_down': _L3_ffn_in['w_down'], 'L3_ffn_shared_w_gate': _L3_ffn_in['shared_w_gate'], 'L3_ffn_shared_w_up': _L3_ffn_in['shared_w_up'], 'L3_ffn_shared_w_down': _L3_ffn_in['shared_w_down'], 'L3_ffn_anchor_w_gate': _L3_ffn_in['anchor_w_gate'], 'L3_ffn_anchor_w_up': _L3_ffn_in['anchor_w_up'], 'L3_ffn_anchor_w_down': _L3_ffn_in['anchor_w_down']}

def reference(x, ctx_1024, fside_1xSxS2_0, g_xattn, g_ffn, L0_xattn_wq, L0_xattn_bq, L0_xattn_wk, L0_xattn_bk, L0_xattn_wv, L0_xattn_bv, L0_xattn_wo, L0_xattn_bo, L0_xattn_time_decay, L0_ffn_ln1_w, L0_ffn_ln2_w, L0_ffn_wqkv, L0_ffn_wo, L0_ffn_gate_w, L0_ffn_w13, L0_ffn_w2, L1_xattn_Wq, L1_xattn_bq, L1_xattn_Wk, L1_xattn_bk, L1_xattn_Wv, L1_xattn_bv, L1_xattn_Wo, L1_xattn_bo, L1_ffn_switch_w, L1_ffn_switch_b, L1_ffn_w1, L1_ffn_b1, L1_ffn_w2, L1_ffn_b2, L2_xattn_W1, L2_xattn_b1, L2_xattn_W2, L2_xattn_b2, L2_ffn_m1, L2_ffn_m2, L2_ffn_mb, L2_ffn_w1, L2_ffn_w2, L2_ffn_b2, L3_xattn_Wq, L3_xattn_bq, L3_xattn_Wk, L3_xattn_bk, L3_xattn_Wv, L3_xattn_bv, L3_xattn_Wo, L3_xattn_bo, L3_ffn_gate_weight, L3_ffn_gate_bias, L3_ffn_w_gate, L3_ffn_w_up, L3_ffn_w_down, L3_ffn_shared_w_gate, L3_ffn_shared_w_up, L3_ffn_shared_w_down, L3_ffn_anchor_w_gate, L3_ffn_anchor_w_up, L3_ffn_anchor_w_down):
    import jax
    import jax.numpy as jnp

    def _L0_xattn_ref(query, key, value, wq, bq, wk, bk, wv, bv, wo, bo, time_decay):
        import jax, jax.numpy as jnp
        import numpy as np
        D_MODEL = 128
        N_HEADS = 16
        D_K = D_MODEL // N_HEADS
        B, S, D = query.shape
        H, Dk = (N_HEADS, D_K)

        def proj(x, W, b):
            y = jnp.einsum('bsd,ed->bse', x, W) + b
            return y.reshape(B, S, H, Dk).transpose(0, 2, 1, 3)
        Q = proj(query, wq, bq)
        K = proj(key, wk, bk)
        V = proj(value, wv, bv)
        scores = jnp.einsum('bhqd,bhkd->bhqk', Q, K) / jnp.sqrt(jnp.float32(Dk))
        pos = jnp.arange(S, dtype=jnp.float32)
        decay = -time_decay * jnp.abs(pos[:, None] - pos[None, :])
        scores = scores + decay[None, None, :, :]
        attn = jax.nn.softmax(scores, axis=-1)
        ctx = jnp.einsum('bhqk,bhkd->bhqd', attn, V)
        ctx = ctx.transpose(0, 2, 1, 3).reshape(B, S, D)
        out = jnp.einsum('bsd,ed->bse', ctx, wo) + bo
        return out

    def _L0_ffn_ref(x, ln1_w, ln2_w, wqkv, wo, gate_w, w13, w2):
        import jax, jax.numpy as jnp
        import numpy as np
        HID = 128
        NH = 16
        NKV = 4
        HD = HID // NH
        E = 8
        TOPK = 2
        FFN = 256
        EPS = 1e-05
        THETA = 10000.0

        def _rmsnorm(x, w):
            var = jnp.mean(x * x, axis=-1, keepdims=True)
            return x * jax.lax.rsqrt(var + EPS) * w

        def _rope_tables(S):
            inv_freq = 1.0 / THETA ** (jnp.arange(0, HD, 2, dtype=jnp.float32) / HD)
            freqs = jnp.arange(S, dtype=jnp.float32)[:, None] * inv_freq[None, :]
            emb = jnp.concatenate([freqs, freqs], axis=-1)
            return (jnp.cos(emb), jnp.sin(emb))

        def _apply_rope(t, cos, sin):
            t1, t2 = jnp.split(t, 2, axis=-1)
            rot = jnp.concatenate([-t2, t1], axis=-1)
            return t * cos[None, :, None, :] + rot * sin[None, :, None, :]
        B, S, _ = x.shape
        h = _rmsnorm(x, ln1_w)
        qkv = jnp.einsum('bsh,oh->bso', h, wqkv)
        q = qkv[..., :NH * HD].reshape(B, S, NH, HD)
        k = qkv[..., NH * HD:(NH + NKV) * HD].reshape(B, S, NKV, HD)
        v = qkv[..., (NH + NKV) * HD:].reshape(B, S, NKV, HD)
        cos, sin = _rope_tables(S)
        q = _apply_rope(q, cos, sin)
        k = _apply_rope(k, cos, sin)
        groups = NH // NKV
        k = jnp.repeat(k, groups, axis=2)
        v = jnp.repeat(v, groups, axis=2)
        scale = HD ** (-0.5)
        scores = jnp.einsum('bqhd,bkhd->bhqk', q, k) * scale
        causal = jnp.tril(jnp.ones((S, S), dtype=bool))
        scores = jnp.where(causal[None, None], scores, jnp.finfo(scores.dtype).min)
        probs = jax.nn.softmax(scores, axis=-1)
        attn = jnp.einsum('bhqk,bkhd->bqhd', probs, v).reshape(B, S, NH * HD)
        x = x + jnp.einsum('bso,ho->bsh', attn, wo)
        h = _rmsnorm(x, ln2_w).reshape(-1, HID)
        T = h.shape[0]
        logits = jnp.einsum('th,eh->te', h, gate_w)
        rprobs = jax.nn.softmax(logits.astype(jnp.float32), axis=-1)
        topw, topi = jax.lax.top_k(rprobs, TOPK)
        topw = topw / jnp.sum(topw, axis=-1, keepdims=True)
        wfull = jnp.zeros((T, E), jnp.float32).at[jnp.arange(T)[:, None], topi].set(topw)
        wfull = wfull.astype(h.dtype)
        out = jnp.zeros((T, HID), h.dtype)
        for e in range(E):
            w1 = w13[e, :FFN]
            w3 = w13[e, FFN:]
            g = jax.nn.silu(h @ w1.T) * (h @ w3.T)
            out = out + jnp.einsum('tf,hf->th', g, w2[e]) * wfull[:, e:e + 1]
        return x + out.reshape(B, S, HID)

    def _L1_xattn_ref(Q, K, V, Wq, bq, Wk, bk, Wv, bv, Wo, bo):
        import jax, jax.numpy as jnp
        import numpy as np
        D_MODEL = 128
        N_HEADS = 16
        D_K = D_MODEL // N_HEADS
        WINDOW = 128
        NEG = -1000000000.0
        B, S, _ = Q.shape
        q = Q @ Wq + bq
        k = K @ Wk + bk
        v = V @ Wv + bv
        q = q.reshape(B, S, N_HEADS, D_K).transpose(0, 2, 1, 3)
        k = k.reshape(B, S, N_HEADS, D_K).transpose(0, 2, 1, 3)
        v = v.reshape(B, S, N_HEADS, D_K).transpose(0, 2, 1, 3)
        scores = jnp.einsum('bhqd,bhkd->bhqk', q, k) / jnp.sqrt(jnp.float32(D_K))
        rel = jnp.arange(S)[None, :] - jnp.arange(S)[:, None]
        win = (rel >= -WINDOW) & (rel <= WINDOW)
        scores = jnp.where(win[None, None], scores, NEG)
        probs = jax.nn.softmax(scores, axis=-1)
        out = jnp.einsum('bhqk,bhkd->bhqd', probs, v)
        out = out.transpose(0, 2, 1, 3).reshape(B, S, D_MODEL)
        return out @ Wo + bo

    def _L1_ffn_ref(x, switch_w, switch_b, w1, b1, w2, b2):
        import jax, jax.numpy as jnp
        import numpy as np
        B, S, D = (4, 256, 128)
        E, F = (8, 512)
        b, s, d = x.shape
        t = x.reshape(-1, d)
        logits = t @ switch_w + switch_b
        route_prob = jax.nn.softmax(logits, axis=-1)
        route_prob_max = jnp.max(route_prob, axis=-1)
        routes = jnp.argmax(route_prob, axis=-1)
        out = jnp.zeros_like(t)
        n_experts = w1.shape[0]
        for e in range(n_experts):
            h = jax.nn.gelu(t @ w1[e] + b1[e])
            y = h @ w2[e] + b2[e]
            mask = (routes == e)[:, None]
            out = jnp.where(mask, y, out)
        out = out * route_prob_max[:, None]
        return out.reshape(b, s, d)

    def _L2_xattn_ref(q, k, v1, mask, W1, b1, W2, b2):
        import jax, jax.numpy as jnp
        import numpy as np
        import math
        D = 128
        B, S = (8, 256)

        def _proj(x, W1, b1, W2, b2):
            h = jnp.einsum('bsd,od->bso', x, W1) + b1
            return jnp.einsum('bsd,od->bso', h, W2) + b2
        qp = _proj(q, W1, b1, W2, b2)
        kp = _proj(k, W1, b1, W2, b2)
        scale = 1.0 / math.sqrt(qp.shape[-1])
        qk = jnp.einsum('bqd,bkd->bqk', qp, kp) * scale
        qk = qk + mask
        attn = jax.nn.softmax(qk, axis=-1)
        return jnp.einsum('bqk,bkd->bqd', attn, v1)

    def _L2_ffn_ref(x, m1, m2, mb, w1, w2, b2):
        import jax, jax.numpy as jnp
        import numpy as np
        D_MODEL, D_FF, D2, DL = (128, 512, 64, 64)
        D1 = D_FF // D2
        BATCH, SEQ = (2, 128)
        KERNEL_SCALE = D2 ** 0.5
        x_shape = x.shape
        xf = x.reshape(-1, x_shape[-1])
        d1 = w1.shape[1]
        lr = xf @ m1
        mask_logits = jnp.einsum('bl,lxy->bxy', lr, m2) + mb
        quant_mask = jnp.argmax(mask_logits, axis=-1)
        w1p = jnp.transpose(w1, (1, 2, 0))
        w2p = jnp.transpose(w2, (1, 0, 2))
        j = jnp.arange(d1)[None, :]
        w = w1p[j, quant_mask]
        mid = jnp.einsum('ai,aji->aj', xf, w)
        relu = jax.nn.relu(mid)
        v = w2p[j, quant_mask]
        res = jnp.einsum('ai,aij->aj', relu, v) + b2
        return res.reshape(x_shape)

    def _L3_xattn_ref(Q, K, V, Wq, bq, Wk, bk, Wv, bv, Wo, bo):
        import jax, jax.numpy as jnp
        import numpy as np
        D_MODEL = 128
        NUM_HEAD = 16
        b, s, d = Q.shape
        h = NUM_HEAD
        hd = d // h
        q = (Q @ Wq.T + bq).reshape(b, s, h, hd)
        k = (K @ Wk.T + bk).reshape(b, s, h, hd)
        v = (V @ Wv.T + bv).reshape(b, s, h, hd)
        atten = jnp.einsum('bqhd,bkhd->bhqk', q, k) / jnp.sqrt(jnp.float32(hd))
        atten = jax.nn.softmax(atten, axis=3)
        out = jnp.einsum('bhqk,bkhv->bqhv', atten, v).reshape(b, s, d)
        return out @ Wo.T + bo

    def _L3_ffn_ref(hidden_states, gate_weight, gate_bias, w_gate, w_up, w_down, shared_w_gate, shared_w_up, shared_w_down, anchor_w_gate, anchor_w_up, anchor_w_down):
        import jax, jax.numpy as jnp
        import numpy as np
        HIDDEN = 128
        N_EXPERTS = 32
        MOE_I = 64
        N_GROUP = 4
        TOPK_GROUP = 2
        TOP_K = 6
        N_LOCAL_GROUPS = 16
        ANCHOR_I = 32
        SHARED_I = 64
        ROUTED_SCALE = 0.2
        ANCHOR_ALPHA = 0.1
        BATCH, SEQ = (1, 128)

        def _moe_forward(hidden_states, gate_weight, gate_bias, w_gate, w_up, w_down, shared_w_gate, shared_w_up, shared_w_down, anchor_w_gate, anchor_w_up, anchor_w_down):
            B, S, H = hidden_states.shape
            x = hidden_states.reshape(-1, H)
            T = x.shape[0]
            E = gate_weight.shape[0]
            L = anchor_w_gate.shape[0]
            logits = x @ gate_weight.T
            scores = jax.nn.sigmoid(logits)
            sc = scores + gate_bias
            grp = sc.reshape(T, N_GROUP, E // N_GROUP)
            group_scores = jax.lax.top_k(grp, 2)[0].sum(-1)
            _, gidx = jax.lax.top_k(group_scores, TOPK_GROUP)
            gmask = jax.nn.one_hot(gidx, N_GROUP, dtype=sc.dtype).sum(1)
            emask = jnp.repeat(gmask, E // N_GROUP, axis=1)
            masked = jnp.where(emask > 0, sc, -jnp.inf)
            _, topidx = jax.lax.top_k(masked, TOP_K)
            tw = jnp.take_along_axis(scores, topidx, axis=-1)
            tw = tw / (tw.sum(-1, keepdims=True) + 1e-20) * ROUTED_SCALE
            g = jnp.einsum('th,ehi->tei', x, w_gate)
            u = jnp.einsum('th,ehi->tei', x, w_up)
            eo = jnp.einsum('tei,eih->teh', jax.nn.silu(g) * u, w_down)
            cw = (jax.nn.one_hot(topidx, E, dtype=x.dtype) * tw[..., None]).sum(1)
            routed = jnp.einsum('te,teh->th', cw, eo)
            shared = jax.nn.silu(x @ shared_w_gate) * (x @ shared_w_up) @ shared_w_down
            lg = topidx[:, 0] // (E // L)
            ag = jnp.einsum('th,lhi->tli', x, anchor_w_gate)
            au = jnp.einsum('th,lhi->tli', x, anchor_w_up)
            ao = jnp.einsum('tli,lih->tlh', jax.nn.silu(ag) * au, anchor_w_down)
            acw = jax.nn.one_hot(lg, L, dtype=x.dtype)
            anchor = jnp.einsum('tl,tlh->th', acw, ao)
            out = routed + shared + ANCHOR_ALPHA * anchor
            return out.reshape(B, S, H)
        return _moe_forward(hidden_states, gate_weight, gate_bias, w_gate, w_up, w_down, shared_w_gate, shared_w_up, shared_w_down, anchor_w_gate, anchor_w_up, anchor_w_down)
    x = x + jnp.tanh(g_xattn[0]) * _L0_xattn_ref(_layernorm(x, axis=-1), ctx_1024, ctx_1024, L0_xattn_wq, L0_xattn_bq, L0_xattn_wk, L0_xattn_bk, L0_xattn_wv, L0_xattn_bv, L0_xattn_wo, L0_xattn_bo, L0_xattn_time_decay)
    x = x + jnp.tanh(g_ffn[0]) * _L0_ffn_ref(_layernorm(x, axis=-1), L0_ffn_ln1_w, L0_ffn_ln2_w, L0_ffn_wqkv, L0_ffn_wo, L0_ffn_gate_w, L0_ffn_w13, L0_ffn_w2)
    x = x + jnp.tanh(g_xattn[1]) * _L1_xattn_ref(_layernorm(x, axis=-1), ctx_1024, ctx_1024, L1_xattn_Wq, L1_xattn_bq, L1_xattn_Wk, L1_xattn_bk, L1_xattn_Wv, L1_xattn_bv, L1_xattn_Wo, L1_xattn_bo)
    x = x + jnp.tanh(g_ffn[1]) * _L1_ffn_ref(_layernorm(x, axis=-1), L1_ffn_switch_w, L1_ffn_switch_b, L1_ffn_w1, L1_ffn_b1, L1_ffn_w2, L1_ffn_b2)
    x = x + jnp.tanh(g_xattn[2]) * _L2_xattn_ref(_layernorm(x, axis=-1), ctx_1024, ctx_1024, fside_1xSxS2_0, L2_xattn_W1, L2_xattn_b1, L2_xattn_W2, L2_xattn_b2)
    x = x + jnp.tanh(g_ffn[2]) * _L2_ffn_ref(_layernorm(x, axis=-1), L2_ffn_m1, L2_ffn_m2, L2_ffn_mb, L2_ffn_w1, L2_ffn_w2, L2_ffn_b2)
    x = x + jnp.tanh(g_xattn[3]) * _L3_xattn_ref(_layernorm(x, axis=-1), ctx_1024, ctx_1024, L3_xattn_Wq, L3_xattn_bq, L3_xattn_Wk, L3_xattn_bk, L3_xattn_Wv, L3_xattn_bv, L3_xattn_Wo, L3_xattn_bo)
    x = x + jnp.tanh(g_ffn[3]) * _L3_ffn_ref(_layernorm(x, axis=-1), L3_ffn_gate_weight, L3_ffn_gate_bias, L3_ffn_w_gate, L3_ffn_w_up, L3_ffn_w_down, L3_ffn_shared_w_gate, L3_ffn_shared_w_up, L3_ffn_shared_w_down, L3_ffn_anchor_w_gate, L3_ffn_anchor_w_up, L3_ffn_anchor_w_down)
    return x

_drawn_inputs = setup_inputs


def setup_inputs(seed=0):
    import zlib

    import numpy as np

    out = dict(_drawn_inputs(seed))
    spreads = {'L0_ffn_ln1_w': (1.0, 0.2),
     'L0_ffn_ln2_w': (1.0, 0.2),
     'L1_xattn_bq': (0.0, 0.1),
     'L1_xattn_bk': (0.0, 0.8),
     'L1_xattn_bv': (0.0, 0.1),
     'L1_xattn_bo': (0.0, 0.1),
     'L1_ffn_switch_b': (0.0, 0.1),
     'L1_ffn_b1': (0.0, 0.1),
     'L1_ffn_b2': (0.0, 0.1),
     'L3_xattn_bq': (0.0, 0.8),
     'L3_xattn_bk': (0.0, 0.8),
     'L3_xattn_bv': (0.0, 0.633),
     'L3_xattn_bo': (0.0, 0.1)}
    factors = {'L0_xattn_bq': 4.866,
     'L0_xattn_bk': 8.0,
     'L3_xattn_Wq': 8.0,
     'L3_xattn_Wk': 8.0,
     'L3_xattn_Wv': 3.272,
     'L3_xattn_Wo': 2.717,
     'L3_ffn_gate_weight': 8.0,
     'L3_ffn_gate_bias': 8.0,
     'L3_ffn_w_gate': 8.0,
     'L3_ffn_w_up': 8.0,
     'L3_ffn_w_down': 8.0,
     'L3_ffn_shared_w_gate': 8.0,
     'L3_ffn_shared_w_up': 8.0,
     'L3_ffn_shared_w_down': 8.0,
     'L3_ffn_anchor_w_gate': 8.0,
     'L3_ffn_anchor_w_up': 8.0,
     'L3_ffn_anchor_w_down': 8.0}
    for name, (base, spread) in spreads.items():
        noise = np.random.default_rng([zlib.crc32(name.encode()), seed]).standard_normal(out[name].shape)
        drawn = base * np.exp(spread * noise) if base else spread * noise
        out[name] = jnp.asarray(drawn.astype(out[name].dtype))
    for name, factor in factors.items():
        out[name] = (out[name] * factor).astype(out[name].dtype)
    return out
```

```python
from contextlib import ExitStack

import numpy as np
import concourse.bass as bass
from concourse import mybir

F32 = mybir.dt.float32
ALU = mybir.AluOpType
ACT = mybir.ActivationFunctionType
AX_X = mybir.AxisListType.X

P = 128
D = 128
B, S = 64, 64
TILES = B * S // P
TPG = 4
GROUPS = TILES // TPG
GT = TPG * P
GB = GT // S
H, DK = 16, 8
PAIRS = H // 2
VW = DK + 1
EPS = 1e-5
E0, F0 = 8, 256
E1, F1 = 8, 512
D1, D2, DL = 8, 64, 64
E3, I3, G3, K3 = 32, 64, 4, 6
L3, A3 = 16, 32
SENT = -3.0e38
TAKEN = 3.0e38
LOW = -1.0e30


class Columns:

    def __init__(self, widths):
        self.at, self.width = {}, 0
        for name, n in widths:
            self.at[name] = (self.width, self.width + n)
            self.width += n

    def __call__(self, tile, name):
        a, b = self.at[name]
        return tile[:, a:b]


ATT = ("x0", "f0", "x1", "x3")
ATT_W = Columns([(f"{w}_{k}", D) for k in ATT for w in ("wq", "wk", "wv", "wo")]
                + [("wqs_f0", D), ("wks_f0", D), ("w1_x2", D), ("w2t_x2", D)]
                + [(f"{w}_{k}", 1) for k in ("x0", "x1", "x3") for w in ("bq", "bk", "bv")]
                + [("b1_x2", 1), ("b2_x2", 1), ("ln1", 1), ("ln2", 1), ("mask", S)]
                + [("gate0", E0), ("switch", E1), ("gate3", E3)])
ROWS = Columns([("bo_x0", D), ("bo_x1", D), ("bo_x3", D), ("b2_f2", D), ("g", 8), ("decay", 1),
                ("switch_b", E1), ("gate_bias", E3)])
CONST = Columns([("ident", P), ("head", H), ("dist", S), ("causal", S), ("qcos", S), ("qsin", S),
                 ("kcos", S), ("ksin", S), ("first", D2)])


def constants():
    c = np.zeros((P, CONST.width), np.float32)
    row = np.arange(P)
    CONST(c, "ident")[:] = np.eye(P)
    CONST(c, "head")[:] = row[:, None] // DK == np.arange(H)[None]
    q, k = row[:, None] % S, np.arange(S)[None]
    CONST(c, "dist")[:] = -np.abs(q - k)
    CONST(c, "causal")[:] = np.where(k <= q, 0.0, SENT)
    freq = (1.0 / 10000.0 ** (np.arange(0, DK, 2, dtype=np.float32) / DK)).astype(np.float32)
    angle = np.arange(S, dtype=np.float32)[None] * freq[row % (DK // 2)][:, None]
    sign = np.where(row % DK < DK // 2, -1.0, 1.0)[:, None]
    CONST(c, "kcos")[:] = np.cos(angle)
    CONST(c, "ksin")[:] = np.sin(angle) * sign
    CONST(c, "qcos")[:] = np.cos(angle) * DK ** -0.5
    CONST(c, "qsin")[:] = np.sin(angle) * sign * DK ** -0.5
    CONST(c, "first")[:] = D2 - np.arange(D2)[None]
    return c


def over_heads(table):
    return table.unsqueeze(1).broadcast_to([P, H, S])


def run_groups(eng, prologue, body, tail):
    prologue()
    body(0, 0, True, False)
    with eng.Fori(0, (GROUPS - 2) // 2) as j:
        body(j * 2 + 1, 1, False, False)
        body(j * 2 + 2, 0, False, False)
    body(GROUPS - 1, (GROUPS - 1) % 2, False, True)
    tail()


class Attention:


    def __init__(self, k, kind):
        self.k, self.kind = k, kind
        self.rope = kind == "f0"
        self.table = {"x0": k.decay, "f0": CONST(k.const, "causal")}.get(kind)
        nq = 2 if self.rope else 1
        self.s, self.past = k.signals(
            {n: GROUPS for n in ("stats", "rstd", "xn", "lnT", "hT", "kblk0", "kblk1", "aTp", "aT", "wo", "X")}
            | {n: nq * GROUPS for n in ("q", "QT", "k", "KT")} | {n: GROUPS for n in ("v", "V")}
            | {n: TILES for n in ("scores", "shifted", "exp", "pv", "attn")} | {n: 2 * TILES for n in ("pT", "PT")}
            | {n: 0 if self.rope else 8 * GROUPS for n in ("ctx0", "ctx1")})
        self.nq = 2 if self.rope else 1
        if self.rope:
            self.misc = {(0, "B"): "lnT", (0, "C"): "q", (1, "A"): "qs", (1, "B"): "k", (1, "C"): "ks",
                         (2, "A"): "v", (2, "B"): "aT", (3, "A"): "wo"}
        else:
            self.misc = {(0, "B"): "lnT", (0, "C"): "q", (1, "A"): "k", (1, "B"): "v", (2, "B"): "aT",
                         (3, "A"): "wo"}

    def w(self, name):
        return ATT_W(self.k.att_w, f"{name}_{self.kind}")

    def tensor(self, pe):
        k, s, past = self.k, self.s, self.past
        ident = CONST(k.const, "ident")
        misc = k.bank[7]

        def scores(t, c, gp, g):
            pe.wait_ge(s["QT"], past["QT"] + (g + 1) * self.nq)
            pe.wait_ge(s["kblk0"] if c < 2 else s["kblk1"], (past["kblk0"] if c < 2 else past["kblk1"]) + g + 1)
            if not (isinstance(t, int) and t < 2):
                pe.wait_ge(s["shifted"], past["shifted"] + t - 1)
            for n in range(2):
                for b in range(2):
                    at = c * P + b * S
                    last = pe.matmul(k.bank[2 * (c % 2) + n][b * S:(b + 1) * S, :],
                                     k.QT[gp][:, at:at + S],
                                     k.Kblk[c // 2][:, 2 * (c % 2) + b, n * 8:(n + 1) * 8, :],
                                     start=True, stop=True)
            last.then_inc(s["scores"], 1)

        def turn(t, c):
            pe.wait_ge(s["exp"], past["exp"] + t + 1)
            for half in range(2):
                if not (isinstance(t, int) and t < 1):
                    pe.wait_ge(s["PT"], past["PT"] + 2 * t - 1 + half)
                for p in range(4):
                    at = (half * 4 + p) * P
                    last = pe.transpose(k.bank[4 + half][:, p * P:(p + 1) * P],
                                        k.probs[c % 2][:, at:at + P], ident)
                last.then_inc(s["pT"], 1)

        def values(t, c, gp, g):
            pe.wait_ge(s["PT"], past["PT"] + 2 * t + 2)
            pe.wait_ge(s["V"], past["V"] + g + 1)
            if not (isinstance(t, int) and t < 1):
                pe.wait_ge(s["attn"], past["attn"] + t)
            for p in range(PAIRS):
                for b in range(2):
                    at = (2 * c + b) * PAIRS * 2 * VW + p * 2 * VW
                    last = pe.matmul(k.bank[6][b * S:(b + 1) * S, p * S:(p + 1) * S],
                                     k.PT[c % 2][:, p * P + b * S:p * P + (b + 1) * S],
                                     k.Vblk[gp][:, at:at + S], start=True, stop=True)
            last.then_inc(s["pv"], 1)

        def project(what, n, np_, first):
            if what == "lnT":
                pe.wait_ge(s["xn"], past["xn"] + n + 1)
                if first != "prologue":
                    pe.wait_ge(s["V"], past["V"] + n)
                if first is False:
                    pe.wait_ge(s["X"], past["X"] + n - 2)
                for c in range(TPG):
                    last = pe.transpose(misc[:, c * P:(c + 1) * P], k.xn[:, c, :], ident)
                last.then_inc(s["lnT"], 1)
            elif what in ("q", "qs"):
                pe.wait_ge(s["hT"], past["hT"] + n + 1)
                if what == "qs":
                    pe.wait_ge(s["QT"], past["QT"] + 2 * n + 1)
                w = self.w("wq") if what == "q" else self.w("wqs")
                pe.matmul(misc[:, :], w, k.hT[np_][:, :], start=True, stop=True).then_inc(s["q"], 1)
            elif what in ("k", "ks"):
                pe.wait_ge(s["QT"], past["QT"] + (n + 1) * self.nq)
                if not self.rope:
                    pe.wait_ge(s[f"ctx{np_}"], past[f"ctx{np_}"] + 8 * n + 16 - 8 * np_)
                if what == "ks":
                    pe.wait_ge(s["KT"], past["KT"] + 2 * n + 1)
                w = self.w("wk") if what == "k" else self.w("wks")
                src = k.hT[np_] if self.rope else k.ctxT[np_]
                pe.matmul(misc[:, :], w, src[:, :], start=True, stop=True).then_inc(s["k"], 1)
            elif what == "v":
                pe.wait_ge(s["KT"], past["KT"] + (n + 1) * self.nq)
                src = k.hT[np_] if self.rope else k.ctxT[np_]
                for b in range(GB):
                    for up in range(2):
                        last = pe.matmul(misc[up * S:(up + 1) * S, b * S:(b + 1) * S], src[:, b * S:(b + 1) * S],
                                         self.w("wv")[:, up * S:(up + 1) * S], start=True, stop=True)
                last.then_inc(s["v"], 1)

        def output(what, p, pp, before):
            if what == "aT":
                pe.wait_ge(s["attn"], past["attn"] + TPG * (p + 1))
                pe.wait_ge(*before)
                for c in range(TPG):
                    last = pe.transpose(misc[:, c * P:(c + 1) * P], k.attn[pp][:, c, :], ident)
                last.then_inc(s["aTp"], 1)
            else:
                pe.wait_ge(s["aT"], past["aT"] + p + 1)
                for c in range(TPG):
                    last = pe.matmul(misc[:, c * P:(c + 1) * P], k.aT[:, c * P:(c + 1) * P],
                                     k.wo[self.kind], start=True, stop=True)
                last.then_inc(s["wo"], 1)

        def place(c, where, g, gp, first, last):
            what = self.misc.get((c, where))
            if what in ("aT", "wo"):
                if not first:
                    before = (s["X"], past["X"] + g - 1) if last else (s["V"], past["V"] + g + 2)
                    output(what, g - 1, 1 - gp, before)
            elif what and not last:
                project(what, g + 1, 1 - gp, first)

        def prologue():
            for what in ("lnT", "q", "qs", "k", "ks", "v"):
                if self.rope or len(what) != 2:
                    project(what, 0, 0, "prologue")
            scores(0, 0, 0, 0)

        def body(g, gp, first, last):
            for c in range(TPG):
                t = g * TPG + c
                if c < 3:
                    scores(t + 1, c + 1, gp, g)
                elif not last:
                    scores(t + 1, 0, 1 - gp, g + 1)
                place(c, "A", g, gp, first, last)
                turn(t, c)
                place(c, "B", g, gp, first, last)
                if c > 0:
                    values(t - 1, c - 1, gp, g)
                elif not first:
                    values(t - 1, 3, 1 - gp, g - 1)
                place(c, "C", g, gp, first, last)

        def tail():
            values(TILES - 1, 3, (GROUPS - 1) % 2, GROUPS - 1)
            output("aT", GROUPS - 1, (GROUPS - 1) % 2, (s["X"], past["X"] + GROUPS - 1))
            output("wo", GROUPS - 1, (GROUPS - 1) % 2, None)

        run_groups(pe, prologue, body, tail)

    def scalar(self, act):
        k, s, past = self.k, self.s, self.past
        misc = k.bank[7]

        def evacuate(what, n, np_):
            if what == "lnT":
                act.wait_ge(s["lnT"], past["lnT"] + n + 1)
                act.activation(k.hT[np_][:, :], misc[:, :], ACT.Copy if not self.rope else ACT.Identity,
                               scale=1.0 if not self.rope else ATT_W(k.att_w, "ln1")).then_inc(s["hT"], 1)
            elif what == "q" and not self.rope:
                act.wait_ge(s["q"], past["q"] + n + 1)
                act.activation(k.QT[np_][:, :], misc[:, :], ACT.Identity, bias=k.bqs[self.kind],
                               scale=DK ** -0.5).then_inc(s["QT"], 1)
            elif what == "k" and not self.rope:
                act.wait_ge(s["k"], past["k"] + n + 1)
                if not (isinstance(n, int) and n < 1):
                    act.wait_ge(s["kblk0"], past["kblk0"] + n)
                act.activation(k.KT[:, :], misc[:, :], ACT.Identity, bias=self.w("bk")).then_inc(s["KT"], 1)
            elif what == "v":
                act.wait_ge(s["v"], past["v"] + n + 1)
                dst = k.Vblk[np_][:, 0:GB * PAIRS * 2 * VW].rearrange("p (b r x) -> p b r x", b=GB, r=PAIRS)
                src = misc[:, :].rearrange("p (b r x) -> p b r x", b=GB, r=PAIRS)
                for up in range(2):
                    last = act.activation(dst[up * S:(up + 1) * S, :, :, up * VW:up * VW + DK],
                                          src[up * S:(up + 1) * S], ACT.Copy)
                last.then_inc(s["V"], 1)

        def turned(t, c):
            for half in range(2):
                act.wait_ge(s["pT"], past["pT"] + 2 * t + 1 + half)
                if not (isinstance(t, int) and t < 2):
                    act.wait_ge(s["pv"], past["pv"] + t - 1)
                act.activation(k.PT[c % 2][:, half * GT:(half + 1) * GT], k.bank[4 + half][:, :],
                               ACT.Copy).then_inc(s["PT"], 1)

        def exp(t, c):
            act.wait_ge(s["shifted"], past["shifted"] + t + 1)
            act.activation(k.probs[c % 2][:, :], k.probs[c % 2][:, :], ACT.Exp).then_inc(s["exp"], 1)

        def block_keys(g, heads):
            act.wait_ge(s["KT"], past["KT"] + (g + 1) * self.nq)
            if not (isinstance(g, int) and g < 1):
                act.wait_ge(s["scores"], past["scores"] + TPG * g)
            src = k.KT[:, GT // 2:GT].rearrange("p (b n) -> p b n", b=4)
            for h in heads:
                last = act.activation(k.Kblk[1][:, :, h, :], src, ACT.Copy,
                                      scale=CONST(k.const, "head")[:, h:h + 1])
            if heads[-1] == H - 1:
                last.then_inc(s["kblk1"], 1)

        def output(p, before=None):
            act.wait_ge(s["aTp"], past["aTp"] + p + 1)
            if not (isinstance(p, int) and p < 1):
                act.wait_ge(s["wo"], past["wo"] + p)
            act.activation(k.aT[:, :], misc[:, :], ACT.Copy).then_inc(s["aT"], 1)

        def place(c, where, g, gp, first, last):
            what = self.misc.get((c, where))
            if what == "aT":
                if not first:
                    output(g - 1)
            elif what not in (None, "wo") and not last:
                evacuate(what, g + 1, 1 - gp)

        def prologue():
            for what in ("lnT", "q", "k", "v"):
                evacuate(what, 0, 0)
            exp(0, 0)
            block_keys(0, range(H))

        def body(g, gp, first, last):
            for c in range(TPG):
                t = g * TPG + c
                place(c, "A", g, gp, first, last)
                turned(t, c)
                if c == 0 and not first:
                    block_keys(g, range(8, 12))
                if c == 3 and not last:
                    block_keys(g + 1, range(0, 4))
                place(c, "B", g, gp, first, last)
                if c < 3 or not last:
                    exp(t + 1, (c + 1) % 2)
                place(c, "C", g, gp, first, last)
                if c == 0 and not first:
                    block_keys(g, range(12, 16))
                if c == 3 and not last:
                    block_keys(g + 1, range(4, 8))

        def tail():
            output(GROUPS - 1)

        run_groups(act, prologue, body, tail)

    def vector(self, dve):
        k, s, past = self.k, self.s, self.past
        misc = k.bank[7]

        def stats(n):
            layer_stats(dve, k, n, s["stats"])

        def normalise(n):
            dve.wait_ge(s["rstd"], past["rstd"] + n + 1)
            if not (isinstance(n, int) and n < 1):
                dve.wait_ge(s["lnT"], past["lnT"] + n)
            for c in range(TPG):
                x = k.X[:, bass.ds(n * TPG + c, 1), :]
                if self.rope:
                    h0 = k.XH[:, bass.ds(n * TPG + c, 1), :]
                    dve.tensor_scalar(h0, x, k.mv[:, c, 0:1], k.rstd[:, c:c + 1], ALU.subtract, ALU.mult)
                    dve.drain()
                    last = dve.tensor_scalar(k.xn[:, c, :], h0, k.rms[:, c:c + 1], 0.0, ALU.mult, ALU.add)
                else:
                    last = dve.tensor_scalar(k.xn[:, c, :], x, k.mv[:, c, 0:1], k.rstd[:, c:c + 1],
                                             ALU.subtract, ALU.mult)
            last.then_inc(s["xn"], 1)

        def shift(t, c):
            dve.wait_ge(s["scores"], past["scores"] + t + 1)
            if not (isinstance(t, int) and t < 2):
                dve.wait_ge(s["pT"], past["pT"] + 2 * (t - 1))
            sc = k.scores[c % 2]
            pr = k.probs[c % 2][:, :].rearrange("p (h n) -> p h n", h=H)
            if self.table is not None:
                dve.tensor_tensor(pr, sc, over_heads(self.table), ALU.add)
                dve.drain()
                sc = pr
            top = k.top[:, c % 2 * H:(c % 2 + 1) * H]
            dve.tensor_reduce(top, sc, AX_X, ALU.max)
            dve.drain()
            dve.tensor_tensor(pr, sc, top.unsqueeze(2).broadcast_to([P, H, S]),
                              ALU.subtract).then_inc(s["shifted"], 1)

        def divide(t, c, gp, g):
            dve.wait_ge(s["pv"], past["pv"] + t + 1)
            if not (isinstance(g, int) and g < 2):
                dve.wait_ge(s["aTp"], past["aTp"] + g - 1)
            pv = k.bank[6][:, :].rearrange("p (r x) -> p r x", r=PAIRS)[:, :, 0:2 * VW]\
                .rearrange("p r (u x) -> p r u x", u=2)
            dve.reciprocal(k.rsum[:, :], pv[:, :, :, DK])
            dve.drain()
            dve.tensor_tensor(k.attn[gp][:, c, :].rearrange("p (h x) -> p h x", h=H).rearrange("p (r u) x -> p r u x", u=2),
                              pv[:, :, :, 0:DK],
                              k.rsum[:, :].rearrange("p (r u) -> p r u", u=2).unsqueeze(3)
                              .broadcast_to([P, PAIRS, 2, DK]), ALU.mult).then_inc(s["attn"], 1)

        def rotate(what, n, np_):
            which = what[0]
            done, ready = which, which.upper() + "T"
            dst = (k.QT[np_] if which == "q" else k.KT)[:, :].rearrange("p (b n) -> p b n", b=GB)
            src = misc[:, :].rearrange("p (b n) -> p b n", b=GB)
            second = len(what) == 2
            dve.wait_ge(s[done], past[done] + 2 * n + 1 + second)
            if which == "k" and not second and not (isinstance(n, int) and n < 1):
                dve.wait_ge(s["kblk0"], past["kblk0"] + n)
                dve.wait_ge(s["kblk1"], past["kblk1"] + n)
            trig = CONST(k.const, which + ("sin" if second else "cos")).unsqueeze(1).broadcast_to([P, GB, S])
            if not second:
                dve.tensor_tensor(dst, src, trig, ALU.mult).then_inc(s[ready], 1)
            else:
                part = k.tmp[:, :].rearrange("p (b n) -> p b n", b=GB)
                dve.tensor_tensor(part, src, trig, ALU.mult)
                dve.drain()
                dve.tensor_tensor(dst, dst, part, ALU.add).then_inc(s[ready], 1)

        def residual(p):
            dve.wait_ge(s["wo"], past["wo"] + p + 1)
            prod = misc[:, :].rearrange("p (c n) -> p c n", c=TPG)
            if self.rope:
                xh = k.XH[:, bass.ds(p * TPG, TPG), :]
                dve.tensor_tensor(xh, prod, xh, ALU.add).then_inc(s["X"], 1)
            else:
                x = k.X[:, bass.ds(p * TPG, TPG), :]
                tmp = k.tmp[:, :].rearrange("p (c n) -> p c n", c=TPG)
                dve.tensor_tensor(tmp, prod, k.bo[self.kind].unsqueeze(1).broadcast_to([P, TPG, D]), ALU.add)
                dve.drain()
                dve.tensor_tensor(x, x, tmp, ALU.add).then_inc(s["X"], 1)

        def place(c, where, g, gp, last):
            what = self.misc.get((c, where))
            if self.rope and what in ("q", "qs", "k", "ks") and not last:
                rotate(what, g + 1, 1 - gp)

        def prologue():
            stats(0)
            normalise(0)
            if self.rope:
                for what in ("q", "qs", "k", "ks"):
                    rotate(what, 0, 0)
            shift(0, 0)

        def body(g, gp, first, last):
            for c in range(TPG):
                t = g * TPG + c
                if c == 0 and not last:
                    stats(g + 1)
                    normalise(g + 1)
                place(c, "A", g, gp, last)
                if c < 3 or not last:
                    shift(t + 1, (c + 1) % 2)
                place(c, "B", g, gp, last)
                if c > 0:
                    divide(t - 1, c - 1, gp, g)
                elif not first:
                    divide(t - 1, 3, 1 - gp, g - 1)
                place(c, "C", g, gp, last)
                if c == 3 and not first:
                    residual(g - 1)

        def tail():
            divide(TILES - 1, 3, (GROUPS - 1) % 2, GROUPS - 1)
            residual(GROUPS - 1)

        run_groups(dve, prologue, body, tail)

    def gpsimd(self, pool):
        k, s, past = self.k, self.s, self.past

        def block_keys(g):
            pool.wait_ge(s["KT"], past["KT"] + (g + 1) * self.nq)
            if not (isinstance(g, int) and g < 1):
                pool.wait_ge(s["scores"], past["scores"] + TPG * g - 2)
            pool.tensor_tensor(k.gate[:, 0:1], k.gate[:, 1:2], k.gate[:, 1:2], ALU.mult)
            src = k.KT[:, 0:GT // 2].rearrange("p (b n) -> p b n", b=4)
            for h in range(H):
                last = pool.tensor_scalar(k.Kblk[0][:, :, h, :], src, CONST(k.const, "head")[:, h:h + 1],
                                          k.zero[:, 0:1], ALU.mult, ALU.add)
            last.then_inc(s["kblk0"], 1)

        def prologue():
            layer_rstd(pool, k, 0, s, past, self.rope)
            block_keys(0)

        def body(g, gp, first, last):
            if not last:
                layer_rstd(pool, k, g + 1, s, past, self.rope)
                block_keys(g + 1)

        run_groups(pool, prologue, body, lambda: None)

    def sync(self, sp):
        k, s, past = self.k, self.s, self.past
        if self.rope:
            return

        def load(g, gp):
            if g >= 2:
                sp.wait_ge(s["v"], past["v"] + g - 1)
            sp.dma_start(k.ctxT[gp][:, :], k.ctxT_dram[:, bass.ds(g * GT, GT)]).then_inc(s[f"ctx{gp}"], 16)

        for g in range(GROUPS):
            load(g, g % 2)


def layer_stats(dve, k, n, done):
    for c in range(TPG):
        dve.bn_stats(k.bn[:, c, :], k.X[:, bass.ds(n * TPG + c, 1), :].rearrange("p a n -> p (a n)"))
    dve.drain()
    for c in range(TPG):
        dve.bn_aggr(k.mv[:, c, :], k.bn[:, c, :])
    dve.drain()
    dve.tensor_scalar(k.veps[:, :], k.mv[:, :, 1], EPS, None, ALU.add).then_inc(done, 1)


def layer_rstd(pool, k, n, s, past, rms=False):
    pool.wait_ge(s["stats"], past["stats"] + n + 1)
    last = pool.tensor_tensor(k.rstd[:, :], k.veps[:, :], k.minus_half[:, 0:TPG], ALU.pow)
    if rms:
        pool.drain()
        pool.tensor_tensor(k.rms[:, :], k.mv[:, :, 1], k.rstd[:, :], ALU.mult)
        pool.drain()
        pool.tensor_tensor(k.rms[:, :], k.rms[:, :], k.rstd[:, :], ALU.mult)
        pool.drain()
        pool.tensor_tensor(k.rms[:, :], k.rms[:, :], k.eps[:, 0:TPG], ALU.add)
        pool.drain()
        last = pool.tensor_tensor(k.rms[:, :], k.rms[:, :], k.minus_half[:, 0:TPG], ALU.pow)
    last.then_inc(s["rstd"], 1)


def run_loop(eng, count, body, tail):
    body(0, True)
    with eng.Fori(1, count) as j:
        body(j, False)
    tail()


def pe_gate(pe, k):
    pe.matmul(k.bank[7][0:1, GT - 1:GT], CONST(k.const, "ident")[:, 0:1], CONST(k.const, "ident")[:, 0:1],
              start=True, stop=True)


def at_least(eng, sem, value, base):
    if not (isinstance(value, int) and value < 1):
        eng.wait_ge(sem, base + value)


class WholeAttention:


    def __init__(self, k):
        self.k = k
        self.s, self.past = k.signals(
            {n: GROUPS for n in ("stats", "rstd", "xn", "lnT", "hT", "q", "QT", "k", "KT", "scores", "shifted", "exp",
                                 "pT", "PT", "out", "X")} | {n: 16 * GROUPS for n in ("ctx0", "ctx1")})

    def tensor(self, pe):
        k, s, past = self.k, self.s, self.past
        ident = CONST(k.const, "ident")

        def front(n, np_):
            pe.wait_ge(s["xn"], past["xn"] + n + 1)
            at_least(pe, s["hT"], n, past["hT"])
            for c in range(TPG):
                last = pe.transpose(k.bank[0][:, c * P:(c + 1) * P], k.xn[:, c, :], ident)
            last.then_inc(s["lnT"], 1)
            pe.wait_ge(s[f"ctx{np_}"], past[f"ctx{np_}"] + 16 * n + 32 - 16 * np_)
            at_least(pe, s["KT"], n, past["KT"])
            pe.matmul(k.bank[2][:, :], k.wc, k.ctxT[np_][:, :], start=True, stop=True).then_inc(s["k"], 1)
            pe.wait_ge(s["hT"], past["hT"] + n + 1)
            at_least(pe, s["QT"], n, past["QT"])
            pe.matmul(k.bank[1][:, :], k.wc, k.hT[0][:, :], start=True, stop=True).then_inc(s["q"], 1)

        def scores(n):
            pe.wait_ge(s["KT"], past["KT"] + n + 1)
            pe.wait_ge(s["QT"], past["QT"] + n + 1)
            at_least(pe, s["shifted"], n, past["shifted"])
            for c in range(TPG):
                for b in range(2):
                    at = c * P + b * S
                    last = pe.matmul(k.bank[3][b * S:(b + 1) * S, c * S:(c + 1) * S], k.QT[0][:, at:at + S],
                                     k.KT[:, at:at + S], start=True, stop=True)
            last.then_inc(s["scores"], 1)

        def back(g, gp):
            pe.wait_ge(s["exp"], past["exp"] + g + 1)
            at_least(pe, s["PT"], g, past["PT"])
            pe_gate(pe, k)
            for c in range(TPG):
                last = pe.transpose(k.bank[4][0:S, c * P:(c + 1) * P], k.soft[gp][:, c, :], ident)
            last.then_inc(s["pT"], 1)

        def multiply(g, gp):
            pe.wait_ge(s["PT"], past["PT"] + g + 1)
            at_least(pe, s["X"], g, past["X"])
            pe_gate(pe, k)
            for c in range(TPG):
                for b in range(2):
                    at = c * P + b * S
                    last = pe.matmul(k.bank[5][b * S:(b + 1) * S, c * P:(c + 1) * P], k.PT[0][0:S, at:at + S],
                                     k.ctxN[gp][:, 2 * c + b, :], start=True, stop=True)
            last.then_inc(s["out"], 1)

        def prologue():
            front(0, 0)
            scores(0)

        def body(g, gp, first, last):
            if not last:
                front(g + 1, 1 - gp)
            back(g, gp)
            if not last:
                scores(g + 1)
            multiply(g, gp)

        run_groups(pe, prologue, body, lambda: None)

    def scalar(self, act):
        k, s, past = self.k, self.s, self.past

        def front(n):
            act.wait_ge(s["lnT"], past["lnT"] + n + 1)
            at_least(act, s["q"], n, past["q"])
            act.activation(k.hT[0][:, :], k.bank[0][:, :], ACT.Copy).then_inc(s["hT"], 1)
            act.wait_ge(s["k"], past["k"] + n + 1)
            at_least(act, s["scores"], n, past["scores"])
            act.activation(k.KT[:, :], k.bank[2][:, :], ACT.Identity, bias=k.bc[:, 0:1]).then_inc(s["KT"], 1)
            act.wait_ge(s["q"], past["q"] + n + 1)
            act.activation(k.QT[0][:, :], k.bank[1][:, :], ACT.Identity, bias=k.bc[:, 1:2],
                           scale=D ** -0.5).then_inc(s["QT"], 1)

        def exp(n, np_):
            act.wait_ge(s["shifted"], past["shifted"] + n + 1)
            act.activation(k.soft[np_][:, :, :], k.soft[np_][:, :, :], ACT.Exp).then_inc(s["exp"], 1)

        def prologue():
            front(0)
            exp(0, 0)

        def body(g, gp, first, last):
            if not last:
                front(g + 1)
            act.wait_ge(s["pT"], past["pT"] + g + 1)
            at_least(act, s["out"], g, past["out"])
            act.activation(k.PT[0][0:S, 0:GT], k.bank[4][0:S, :], ACT.Copy).then_inc(s["PT"], 1)
            if not last:
                exp(g + 1, 1 - gp)

        run_groups(act, prologue, body, lambda: None)

    def vector(self, dve):
        k, s, past = self.k, self.s, self.past

        def normalise(n):
            layer_stats(dve, k, n, s["stats"])
            dve.wait_ge(s["rstd"], past["rstd"] + n + 1)
            at_least(dve, s["lnT"], n, past["lnT"])
            for c in range(TPG):
                last = dve.tensor_scalar(k.xn[:, c, :], k.X[:, bass.ds(n * TPG + c, 1), :], k.mv[:, c, 0:1],
                                         k.rstd[:, c:c + 1], ALU.subtract, ALU.mult)
            last.then_inc(s["xn"], 1)

        def shift(n, np_):
            dve.wait_ge(s["scores"], past["scores"] + n + 1)
            soft = k.soft[np_][:, :, :]
            sc = k.bank[3][:, 0:TPG * S].rearrange("p (c n) -> p c n", c=TPG)
            mask = ATT_W(k.att_w, "mask").unsqueeze(1).broadcast_to([P, TPG, S])
            dve.tensor_tensor(soft, sc, mask, ALU.add)
            dve.drain()
            dve.tensor_reduce(k.top[:, 0:TPG], soft, AX_X, ALU.max)
            dve.drain()
            dve.tensor_tensor(soft, soft, k.top[:, 0:TPG].unsqueeze(2).broadcast_to([P, TPG, S]),
                              ALU.subtract).then_inc(s["shifted"], 1)

        def add(g, gp):
            dve.wait_ge(s["exp"], past["exp"] + g + 1)
            dve.tensor_reduce(k.rsum[:, 0:TPG], k.soft[gp][:, :, :], AX_X, ALU.add)
            dve.drain()
            dve.reciprocal(k.rsum[:, 4:8], k.rsum[:, 0:TPG])
            dve.drain()
            dve.tensor_scalar(k.rsum[:, 8:12], k.rsum[:, 4:8], k.gates[:, 2:3], None, ALU.mult)
            dve.drain()
            dve.wait_ge(s["out"], past["out"] + g + 1)
            for c in range(TPG):
                x = k.X[:, bass.ds(g * TPG + c, 1), :]
                last = dve.scalar_tensor_tensor(out=x, in0=k.bank[5][:, c * P:(c + 1) * P].unsqueeze(1),
                                                scalar=k.rsum[:, 8 + c:9 + c], in1=x, op0=ALU.mult, op1=ALU.add)
            last.then_inc(s["X"], 1)

        def prologue():
            normalise(0)
            shift(0, 0)

        def body(g, gp, first, last):
            if not last:
                normalise(g + 1)
                shift(g + 1, 1 - gp)
            add(g, gp)

        run_groups(dve, prologue, body, lambda: None)

    def gpsimd(self, pool):
        k, s, past = self.k, self.s, self.past
        layer_rstd(pool, k, 0, s, past)
        with pool.Fori(1, GROUPS) as g:
            layer_rstd(pool, k, g, s, past)

    def sync(self, sp):
        k, s, past = self.k, self.s, self.past

        def load(g, gp):
            at_least(sp, s["k"], g - 1, past["k"])
            at_least(sp, s["out"], g - 1, past["out"])
            sp.dma_start(k.ctxT[gp][:, :], k.ctxT_dram[:, bass.ds(g * GT, GT)]).then_inc(s[f"ctx{gp}"], 16)
            sp.dma_start(k.ctxN[gp][:, :, :], k.ctxN_dram[:, bass.ds(g * GB, GB), :]).then_inc(s[f"ctx{gp}"], 16)

        for g in range(GROUPS):
            load(g, g % 2)


class Route:


    def __init__(self, k, kind):
        self.k, self.kind = k, kind
        own = ("w", "wTp", "wT", "bias", "X") if kind == "f1" else ()
        self.s, self.past = k.signals(
            {n: GROUPS for n in ("stats", "rstd", "xn", "lnT", "hT", "logits", "lg", "e", "exp") + own})
        self.E = {"f0": E0, "f1": E1, "f3": E3}[kind]
        self.gate = ATT_W(k.att_w, {"f0": "gate0", "f1": "switch", "f3": "gate3"}[kind])

    def tensor(self, pe):
        k, s, past = self.k, self.s, self.past
        ident = CONST(k.const, "ident")

        def front(n):
            pe.wait_ge(s["xn"], past["xn"] + n + 1)
            at_least(pe, s["hT"], n, past["hT"])
            for c in range(TPG):
                last = pe.transpose(k.bank[0][:, c * P:(c + 1) * P], k.xn[:, c, :], ident)
            last.then_inc(s["lnT"], 1)
            pe.wait_ge(s["hT"], past["hT"] + n + 1)
            at_least(pe, s["lg"], n, past["lg"])
            for c in range(TPG):
                last = pe.matmul(k.bank[1][:, c * self.E:(c + 1) * self.E], k.hT[0][:, c * P:(c + 1) * P],
                                 self.gate, start=True, stop=True)
            last.then_inc(s["logits"], 1)

        def bias(g):
            pe.wait_ge(s["w"], past["w"] + g + 1)
            at_least(pe, s["wT"], g, past["wT"])
            for c in range(TPG):
                last = pe.transpose(k.bank[2][0:E1, c * P:(c + 1) * P], k.wt[:, c, :], ident)
            last.then_inc(s["wTp"], 1)
            pe.wait_ge(s["wT"], past["wT"] + g + 1)
            at_least(pe, s["X"], g, past["X"])
            for c in range(TPG):
                last = pe.matmul(k.bank[3][:, c * P:(c + 1) * P], k.wtT[0:E1, c * P:(c + 1) * P], k.b2e[0:E1, :],
                                 start=True, stop=True)
            last.then_inc(s["bias"], 1)

        front(0)

        def body(g):
            front(g + 1)
            if self.kind == "f1":
                bias(g)

        with pe.Fori(0, GROUPS - 1) as g:
            body(g)
        if self.kind == "f1":
            bias(GROUPS - 1)

    def scalar(self, act):
        k, s, past = self.k, self.s, self.past

        def front(n):
            act.wait_ge(s["lnT"], past["lnT"] + n + 1)
            at_least(act, s["logits"], n, past["logits"])
            scale = ATT_W(k.att_w, "ln2") if self.kind == "f0" else 1.0
            fn = ACT.Identity if self.kind == "f0" else ACT.Copy
            act.activation(k.HT[:, bass.ds(n * GT, GT)], k.bank[0][:, :], fn, scale=scale)
            act.activation(k.hT[0][:, :], k.bank[0][:, :], fn, scale=scale).then_inc(s["hT"], 1)

        def exps(g):
            act.wait_ge(s["e"], past["e"] + g + 1)
            n = {"f0": 2, "f1": E1, "f3": E3}[self.kind]
            act.activation(k.ex[:, :, 0:n], k.ex[:, :, 0:n], ACT.Exp).then_inc(s["exp"], 1)

        def bias(g):
            act.wait_ge(s["wTp"], past["wTp"] + g + 1)
            at_least(act, s["bias"], g, past["bias"])
            act.activation(k.wtT[0:E1, :], k.bank[2][0:E1, :], ACT.Copy).then_inc(s["wT"], 1)

        front(0)

        def body(g, last):
            if not last:
                front(g + 1)
            exps(g)
            if self.kind == "f1":
                bias(g)

        with act.Fori(0, GROUPS - 1) as g:
            body(g, False)
        body(GROUPS - 1, True)

    def vector(self, dve):
        k, s, past = self.k, self.s, self.past
        E = self.E

        def step(ins):
            dve.drain()

        def normalise(n):
            if self.kind == "f0":
                for c in range(TPG):
                    dve.bn_stats(k.bn[:, c, :], k.XH[:, bass.ds(n * TPG + c, 1), :].rearrange("p a n -> p (a n)"))
                dve.drain()
                for c in range(TPG):
                    dve.bn_aggr(k.mv[:, c, :], k.bn[:, c, :])
                dve.drain()
                step(dve.tensor_tensor(k.veps[:, :], k.mv[:, :, 0], k.mv[:, :, 0], ALU.mult))
                step(dve.tensor_tensor(k.veps[:, :], k.veps[:, :], k.mv[:, :, 1], ALU.add))
                dve.tensor_scalar(k.veps[:, :], k.veps[:, :], EPS, None, ALU.add).then_inc(s["stats"], 1)
            else:
                layer_stats(dve, k, n, s["stats"])
            dve.wait_ge(s["rstd"], past["rstd"] + n + 1)
            at_least(dve, s["lnT"], n, past["lnT"])
            for c in range(TPG):
                if self.kind == "f0":
                    last = dve.tensor_scalar(k.xn[:, c, :], k.XH[:, bass.ds(n * TPG + c, 1), :],
                                             k.rstd[:, c:c + 1], 0.0, ALU.mult, ALU.add)
                else:
                    last = dve.tensor_scalar(k.xn[:, c, :], k.X[:, bass.ds(n * TPG + c, 1), :], k.mv[:, c, 0:1],
                                             k.rstd[:, c:c + 1], ALU.subtract, ALU.mult)
            last.then_inc(s["xn"], 1)

        def pick(rows, width, top, n, taken):
            dve.drain()
            for c in range(rows.shape[1]):
                dve.max(top[:, c, :], rows[:, c, 0:width])
            dve.drain()
            step(dve.memset(top[:, :, n:8], SENT))
            for c in range(rows.shape[1]):
                dve.match_replace(taken[:, c, 0:width], top[:, c, :], rows[:, c, 0:width], TAKEN)
            dve.drain()

        def route0(g):
            dve.drain()
            dve.wait_ge(s["logits"], past["logits"] + g + 1)
            dve.tensor_copy(k.lg[:, :, 0:E], k.bank[1][:, 0:TPG * E].rearrange("p (c e) -> p c e", c=TPG))\
                .then_inc(s["lg"], 1)
            dve.drain()
            for c in range(TPG):
                dve.max(k.t8[:, c, :], k.lg[:, c, 0:16])
            dve.drain()
            best = k.t8[:, :, 0:1].broadcast_to([P, TPG, 2])
            dve.tensor_tensor(k.ex[:, :, 0:2], k.t8[:, :, 0:2], best, ALU.subtract).then_inc(s["e"], 1)
            for n in range(2):
                step(dve.tensor_copy(k.m8[:, :, :], k.t8[:, :, :]))
                step(dve.memset(k.m8[:, :, n + 1:8], SENT))
                for c in range(TPG):
                    dve.match_replace(k.taken[:, c, 0:16], k.m8[:, c, :], k.lg[:, c, 0:16], TAKEN)
                dve.drain()
                step(dve.tensor_scalar(k.pk[:, n, :, 0:E], k.taken[:, :, 0:E], TAKEN, None, ALU.is_equal))
            step(dve.tensor_tensor(k.pk[:, 1, :, 0:E], k.pk[:, 1, :, 0:E], k.pk[:, 0, :, 0:E], ALU.subtract))
            dve.wait_ge(s["exp"], past["exp"] + g + 1)
            dve.tensor_reduce(k.sm[:, 0:TPG], k.ex[:, :, 0:2], AX_X, ALU.add)
            dve.drain()
            step(dve.reciprocal(k.sm[:, 4:8], k.sm[:, 0:TPG]))
            step(dve.tensor_scalar(k.sm[:, 8:12], k.sm[:, 4:8], k.gates[:, 4:5], None, ALU.mult))
            step(dve.tensor_tensor(k.ex[:, :, 0:2], k.ex[:, :, 0:2],
                                   k.sm[:, 8:12].unsqueeze(2).broadcast_to([P, TPG, 2]), ALU.mult))
            for n in range(2):
                step(dve.tensor_tensor(k.pk[:, n, :, 0:E], k.pk[:, n, :, 0:E],
                                       k.ex[:, :, n:n + 1].broadcast_to([P, TPG, E]), ALU.mult))
            dve.tensor_tensor(k.route[:, bass.ds(g * TPG, TPG), 0:E], k.pk[:, 0, :, 0:E], k.pk[:, 1, :, 0:E], ALU.add)
            x, xh = (v[:, bass.ds(g * TPG, TPG), :] for v in (k.X, k.XH))
            dve.scalar_tensor_tensor(out=x, in0=xh, scalar=k.gates[:, 4:5], in1=x, op0=ALU.mult, op1=ALU.add)

        def route1(g):
            dve.drain()
            dve.wait_ge(s["logits"], past["logits"] + g + 1)
            sb = ROWS(k.rows, "switch_b").unsqueeze(1).broadcast_to([P, TPG, E])
            dve.tensor_tensor(k.lg[:, :, 0:E], k.bank[1][:, 0:TPG * E].rearrange("p (c e) -> p c e", c=TPG), sb,
                              ALU.add).then_inc(s["lg"], 1)
            dve.drain()
            for c in range(TPG):
                dve.max(k.t8[:, c, :], k.lg[:, c, 0:16])
            dve.drain()
            dve.tensor_tensor(k.ex[:, :, 0:E], k.lg[:, :, 0:E], k.t8[:, :, 0:1].broadcast_to([P, TPG, E]),
                              ALU.subtract).then_inc(s["e"], 1)
            pick(k.lg, 16, k.t8, 1, k.taken)
            step(dve.tensor_scalar(k.pk[:, 0, :, 0:E], k.taken[:, :, 0:E], TAKEN, None, ALU.is_equal))
            dve.wait_ge(s["exp"], past["exp"] + g + 1)
            dve.tensor_reduce(k.sm[:, 0:TPG], k.ex[:, :, 0:E], AX_X, ALU.add)
            dve.drain()
            step(dve.reciprocal(k.sm[:, 4:8], k.sm[:, 0:TPG]))
            step(dve.tensor_scalar(k.sm[:, 8:12], k.sm[:, 4:8], k.gates[:, 5:6], None, ALU.mult))
            at_least(dve, s["wTp"], g, past["wTp"])
            dve.tensor_tensor(k.wt[:, :, :], k.pk[:, 0, :, 0:E],
                              k.sm[:, 8:12].unsqueeze(2).broadcast_to([P, TPG, E]), ALU.mult).then_inc(s["w"], 1)
            dve.drain()
            dve.tensor_copy(k.route[:, bass.ds(g * TPG, TPG), 0:E], k.wt[:, :, :])
            dve.wait_ge(s["bias"], past["bias"] + g + 1)
            x = k.X[:, bass.ds(g * TPG, TPG), :]
            dve.tensor_tensor(x, k.bank[3][:, :].rearrange("p (c n) -> p c n", c=TPG), x, ALU.add).then_inc(s["X"], 1)

        def route3(g):
            dve.drain()
            dve.wait_ge(s["logits"], past["logits"] + g + 1)
            dve.tensor_scalar(k.ex[:, :, 0:E], k.bank[1][:, 0:TPG * E].rearrange("p (c e) -> p c e", c=TPG), -1.0,
                              None, ALU.mult).then_inc(s["lg"], 1)
            dve.drain().then_inc(s["e"], 1)
            dve.wait_ge(s["exp"], past["exp"] + g + 1)
            dve.tensor_scalar(k.ex[:, :, 0:E], k.ex[:, :, 0:E], 1.0, None, ALU.add)
            dve.drain()
            step(dve.reciprocal(k.sg[:, :, :], k.ex[:, :, 0:E]))
            gb = ROWS(k.rows, "gate_bias").unsqueeze(1).broadcast_to([P, TPG, E])
            step(dve.tensor_tensor(k.sc[:, :, :], k.sg[:, :, :], gb, ALU.add))
            for c in range(TPG):
                for q in range(G3):
                    dve.max(k.g8[:, c, q, :], k.sc[:, c, q * 8:(q + 1) * 8])
            dve.drain()
            step(dve.tensor_tensor(k.lg[:, :, 0:G3], k.g8[:, :, :, 0], k.g8[:, :, :, 1], ALU.add))
            pick(k.lg, 16, k.t8, 2, k.taken)
            step(dve.tensor_scalar(k.gm[:, :, 0, :], k.taken[:, :, 0:G3], TAKEN, None, ALU.is_equal))
            step(dve.tensor_scalar(k.gm[:, :, 1, :], k.gm[:, :, 0, :], 1.0, -LOW, ALU.subtract, ALU.mult))
            for c in range(TPG):
                cand = k.cand[:, c, 0:E].rearrange("p (q e) -> p q e", q=G3)
                sc = k.sc[:, c, :].rearrange("p (q e) -> p q e", q=G3)
                dve.tensor_tensor(cand, sc, k.gm[:, c, 0, :].unsqueeze(2).broadcast_to([P, G3, 8]), ALU.mult)
            dve.drain()
            for c in range(TPG):
                cand = k.cand[:, c, 0:E].rearrange("p (q e) -> p q e", q=G3)
                dve.tensor_tensor(cand, cand, k.gm[:, c, 1, :].unsqueeze(2).broadcast_to([P, G3, 8]), ALU.add)
            dve.drain()
            pick(k.cand, E + 8, k.t8, K3, k.taken)
            step(dve.tensor_scalar(k.ex[:, :, 0:E], k.taken[:, :, 0:E], TAKEN, None, ALU.is_equal))
            step(dve.tensor_tensor(k.ex[:, :, 0:E], k.ex[:, :, 0:E], k.sg[:, :, :], ALU.mult))
            step(dve.tensor_reduce(k.sm[:, 0:TPG], k.ex[:, :, 0:E], AX_X, ALU.add))
            step(dve.tensor_scalar(k.sm[:, 0:TPG], k.sm[:, 0:TPG], 1e-20, None, ALU.add))
            step(dve.reciprocal(k.sm[:, 4:8], k.sm[:, 0:TPG]))
            step(dve.tensor_scalar(k.sm[:, 8:12], k.sm[:, 4:8], 0.2, k.gates[:, 7:8], ALU.mult, ALU.mult))
            dve.tensor_tensor(k.route[:, bass.ds(g * TPG, TPG), 0:E], k.ex[:, :, 0:E],
                              k.sm[:, 8:12].unsqueeze(2).broadcast_to([P, TPG, E]), ALU.mult)
            pick(k.cand, E + 8, k.t8, 1, k.taken)
            step(dve.tensor_scalar(k.ex[:, :, 0:E], k.taken[:, :, 0:E], TAKEN, k.alpha[:, 0:1], ALU.is_equal, ALU.mult))
            two = k.ex[:, :, 0:E].rearrange("p c (l u) -> p c l u", u=2)
            dve.tensor_tensor(k.anchor[:, bass.ds(g * TPG, TPG), :], two[:, :, :, 0], two[:, :, :, 1], ALU.add)

        route = {"f0": route0, "f1": route1, "f3": route3}[self.kind]
        dve.memset(k.lg[:, :, :], SENT)
        dve.memset(k.cand[:, :, :], SENT)
        dve.drain()
        normalise(0)
        with dve.Fori(0, GROUPS - 1) as g:
            normalise(g + 1)
            route(g)
        route(GROUPS - 1)

    def gpsimd(self, pool):
        k, s, past = self.k, self.s, self.past
        layer_rstd(pool, k, 0, s, past)
        with pool.Fori(1, GROUPS) as g:
            layer_rstd(pool, k, g, s, past)

    def sync(self, sp):
        pass


class Experts:


    def __init__(self, k, kind):
        self.k, self.kind = k, kind
        self.gated = kind == "f0"
        self.NF = (F0 if self.gated else F1) // P
        self.E = E0 if self.gated else E1
        self.up_w, self.down_w = k.experts[kind]
        n = GROUPS * self.E
        self.s, self.past = k.signals({"up": n * self.NF, "act": n * self.NF, "hid": n * self.NF * self.gated,
                                       "y": n, "X": n})

    def tensor(self, pe):
        k, s, past, NF, E = self.k, self.s, self.past, self.NF, self.E

        def up(g, e):
            i = g * E + e
            x = k.HT[:, bass.ds(g * GT, GT)]
            for f in range(NF):
                at_least(pe, s["hid"] if self.gated else s["act"], (i - 1) * NF + f + 1, (past["hid"] if self.gated else past["act"]))
                last = pe.matmul(k.bank[f][:, :], self.up_w[:, e, f * P:(f + 1) * P], x, start=True, stop=True)
                if self.gated:
                    last = pe.matmul(k.bank[2 + f][:, :], self.up_w[:, e, F0 + f * P:F0 + (f + 1) * P], x,
                                     start=True, stop=True)
                last.then_inc(s["up"], 1)

        def down(g, e):
            i = g * E + e
            pe.wait_ge(s["hid"] if self.gated else s["act"], (past["hid"] if self.gated else past["act"]) + (i + 1) * NF)
            at_least(pe, s["X"], i - 1, past["X"])
            for c in range(TPG):
                for f in range(NF):
                    last = pe.matmul(k.bank[4 + e % 2][:, c * P:(c + 1) * P], k.hid[e % 2][:, f, c * P:(c + 1) * P],
                                     self.down_w[:, e, f, :], start=(f == 0), stop=(f == NF - 1))
            last.then_inc(s["y"], 1)

        def body(g, first):
            for e in range(E):
                up(g, e)
                if e > 0:
                    down(g, e - 1)
                elif not first:
                    down(g - 1, E - 1)

        pe.wait_ge(k.loaded[self.kind], 16 * k.parts[self.kind])
        run_loop(pe, GROUPS, body, lambda: down(GROUPS - 1, E - 1))

    def scalar(self, act):
        k, s, past, NF, E = self.k, self.s, self.past, self.NF, self.E

        def body(g, first):
            for e in range(E):
                i = g * E + e
                for f in range(NF):
                    act.wait_ge(s["up"], past["up"] + i * NF + f + 1)
                    if self.gated:
                        at_least(act, s["hid"], (i - 1) * NF + f + 1, past["hid"])
                        act.activation(k.silu[:, f, :], k.bank[f][:, :], ACT.Silu).then_inc(s["act"], 1)
                    else:
                        at_least(act, s["y"], i - 1, past["y"])
                        act.activation(k.hid[e % 2][:, f, :], k.bank[f][:, :], ACT.Gelu_apprx_tanh,
                                       bias=k.b1e[:, e * NF + f:e * NF + f + 1]).then_inc(s["act"], 1)

        act.wait_ge(k.loaded[self.kind], 16 * k.parts[self.kind])
        run_loop(act, GROUPS, body, lambda: None)

    def vector(self, dve):
        k, s, past, NF, E = self.k, self.s, self.past, self.NF, self.E

        def add(g, e):
            i = g * E + e
            dve.drain()
            dve.wait_ge(s["y"], past["y"] + i + 1)
            for c in range(TPG):
                x = k.X[:, bass.ds(g * TPG + c, 1), :]
                w = k.route[:, bass.ds(g * TPG + c, 1), e:e + 1].rearrange("p a e -> p (a e)")
                last = dve.scalar_tensor_tensor(out=x, in0=k.bank[4 + e % 2][:, c * P:(c + 1) * P].unsqueeze(1),
                                                scalar=w, in1=x, op0=ALU.mult, op1=ALU.add)
            last.then_inc(s["X"], 1)

        def body(g, first):
            for e in range(E):
                i = g * E + e
                if self.gated:
                    for f in range(NF):
                        dve.wait_ge(s["act"], past["act"] + i * NF + f + 1)
                        at_least(dve, s["y"], i - 1, past["y"])
                        dve.tensor_tensor(k.hid[e % 2][:, f, :], k.bank[2 + f][:, :], k.silu[:, f, :],
                                          ALU.mult).then_inc(s["hid"], 1)
                if e > 0:
                    add(g, e - 1)
                elif not first:
                    add(g - 1, E - 1)

        run_loop(dve, GROUPS, body, lambda: add(GROUPS - 1, E - 1))

    def gpsimd(self, pool):
        pass

    def sync(self, sp):
        pass


class Choices:


    def __init__(self, k):
        self.k = k
        self.s, self.past = k.signals(
            {n: GROUPS for n in ("stats", "rstd", "xn", "lnT", "hT", "lr", "lrT")}
            | {n: TILES for n in ("logits", "mid", "eq", "ranked", "hid", "pT", "hidT", "out", "X")})

    def tensor(self, pe):
        k, s, past = self.k, self.s, self.past
        ident = CONST(k.const, "ident")

        def front(n, np_):
            pe.wait_ge(s["xn"], past["xn"] + n + 1)
            at_least(pe, s["hT"], n, past["hT"])
            for c in range(TPG):
                last = pe.transpose(k.bank[0][:, c * P:(c + 1) * P], k.xn[:, c, :], ident)
            last.then_inc(s["lnT"], 1)
            pe.wait_ge(s["hT"], past["hT"] + n + 1)
            at_least(pe, s["lrT"], n, past["lrT"])
            pe.matmul(k.bank[1][0:DL, :], k.m1, k.hT[np_][:, :], start=True, stop=True).then_inc(s["lr"], 1)

        def units(t, c, gp, g):
            pe.wait_ge(s["lrT"], past["lrT"] + g + 1)
            at_least(pe, s["hid"], t - 1 if not isinstance(t, int) else max(t - 1, 0), past["hid"])
            pe.matmul(k.bank[2 + c % 2][:, :], k.lrT[gp][:, c * P:(c + 1) * P], k.m2, start=True, stop=True)\
                .then_inc(s["logits"], 1)
            pe.matmul(k.bank[4 + c % 2][:, :], k.hT[gp][:, c * P:(c + 1) * P], k.w1c, start=True, stop=True)\
                .then_inc(s["mid"], 1)

        def turn(t, c):
            pe.wait_ge(s["hid"], past["hid"] + t + 1)
            at_least(pe, s["hidT"], t, past["hidT"])
            for f in range(4):
                last = pe.transpose(k.bank[6][:, f * P:(f + 1) * P], k.hidc[c % 2][:, f * P:(f + 1) * P], ident)
            last.then_inc(s["pT"], 1)

        def multiply(t, c):
            pe.wait_ge(s["hidT"], past["hidT"] + t + 1)
            at_least(pe, s["X"], t, past["X"])
            for f in range(4):
                last = pe.matmul(k.bank[7][:, 0:P], k.hidcT[:, f * P:(f + 1) * P], k.w2c[:, f, :], start=(f == 0),
                                 stop=(f == 3))
            last.then_inc(s["out"], 1)

        def prologue():
            front(0, 0)
            units(0, 0, 0, 0)

        def body(g, gp, first, last):
            for c in range(TPG):
                t = g * TPG + c
                if c < 3:
                    units(t + 1, c + 1, gp, g)
                elif not last:
                    units(t + 1, 0, 1 - gp, g + 1)
                turn(t, c)
                if c == 1 and not last:
                    front(g + 1, 1 - gp)
                multiply(t, c)

        pe.wait_ge(k.loaded["f2"], 16 * k.parts["f2"])
        run_groups(pe, prologue, body, lambda: None)

    def scalar(self, act):
        k, s, past = self.k, self.s, self.past

        def front(n, np_):
            act.wait_ge(s["lnT"], past["lnT"] + n + 1)
            act.activation(k.hT[np_][:, :], k.bank[0][:, :], ACT.Copy).then_inc(s["hT"], 1)
            act.wait_ge(s["lr"], past["lr"] + n + 1)
            act.activation(k.lrT[np_][0:DL, :], k.bank[1][0:DL, :], ACT.Copy).then_inc(s["lrT"], 1)

        def body(g, gp, first, last):
            for c in range(TPG):
                t = g * TPG + c
                act.wait_ge(s["pT"], past["pT"] + t + 1)
                at_least(act, s["out"], t, past["out"])
                act.activation(k.hidcT[:, :], k.bank[6][:, :], ACT.Copy).then_inc(s["hidT"], 1)
                if c == 1 and not last:
                    front(g + 1, 1 - gp)

        for lr in k.lrT:
            act.activation(lr[DL:DL + 1, :], k.onesrow[DL:DL + 1, :], ACT.Copy)
        act.drain()
        run_groups(act, lambda: front(0, 0), body, lambda: None)

    def vector(self, dve):
        k, s, past = self.k, self.s, self.past

        def normalise(n):
            layer_stats(dve, k, n, s["stats"])
            dve.wait_ge(s["rstd"], past["rstd"] + n + 1)
            at_least(dve, s["lnT"], n, past["lnT"])
            for c in range(TPG):
                last = dve.tensor_scalar(k.xn[:, c, :], k.X[:, bass.ds(n * TPG + c, 1), :], k.mv[:, c, 0:1],
                                         k.rstd[:, c:c + 1], ALU.subtract, ALU.mult)
            last.then_inc(s["xn"], 1)

        def blocks(ap):
            return ap.rearrange("p (j y) -> p j y", j=D1)

        def largest(t, c):
            dve.wait_ge(s["logits"], past["logits"] + t + 1)
            dve.tensor_reduce(k.top[:, 0:D1], blocks(k.bank[2 + c % 2][:, :]), AX_X, ALU.max)
            dve.drain()
            dve.tensor_tensor(blocks(k.eq[c % 2][:, :]), blocks(k.bank[2 + c % 2][:, :]),
                              k.top[:, 0:D1].unsqueeze(2).broadcast_to([P, D1, D2]), ALU.is_equal)
            dve.drain().then_inc(s["eq"], 1)

        def choose(t, c):
            dve.wait_ge(s["ranked"], past["ranked"] + t + 1)
            dve.tensor_reduce(k.top[:, 8:16], blocks(k.eq[c % 2][:, :]), AX_X, ALU.max)
            dve.drain()
            dve.tensor_tensor(blocks(k.eq[c % 2][:, :]), blocks(k.eq[c % 2][:, :]),
                              k.top[:, 8:16].unsqueeze(2).broadcast_to([P, D1, D2]), ALU.is_equal)
            dve.drain()
            dve.wait_ge(s["mid"], past["mid"] + t + 1)
            at_least(dve, s["pT"], t - 1 if not isinstance(t, int) else max(t - 1, 0), past["pT"])
            dve.scalar_tensor_tensor(out=k.hidc[c % 2][:, :], in0=k.bank[4 + c % 2][:, :], scalar=0.0,
                                     in1=k.eq[c % 2][:, :], op0=ALU.max, op1=ALU.mult).then_inc(s["hid"], 1)

        def add(t):
            dve.drain()
            dve.wait_ge(s["out"], past["out"] + t + 1)
            x = k.X[:, bass.ds(t, 1), :]
            dve.scalar_tensor_tensor(out=k.tmp[:, 0:P], in0=k.bank[7][:, 0:P], scalar=k.gates[:, 6:7], in1=k.b2c,
                                     op0=ALU.mult, op1=ALU.add)
            dve.drain().then_inc(s["X"], 1)
            dve.tensor_tensor(x, x, k.tmp[:, 0:P].unsqueeze(1), ALU.add)

        def prologue():
            normalise(0)
            largest(0, 0)
            choose(0, 0)

        def body(g, gp, first, last):
            for c in range(TPG):
                t = g * TPG + c
                if c < 3 or not last:
                    largest(t + 1, (c + 1) % 2)
                if c == 0 and not last:
                    normalise(g + 1)
                if c > 0 or not first:
                    add(t - 1)
                if c < 3 or not last:
                    choose(t + 1, (c + 1) % 2)

        run_groups(dve, prologue, body, lambda: add(TILES - 1))

    def gpsimd(self, pool):
        k, s, past = self.k, self.s, self.past

        def rank(t, c):
            pool.wait_ge(s["eq"], past["eq"] + t + 1)
            eq = k.eq[c % 2][:, :].rearrange("p (j y) -> p j y", j=D1)
            pool.tensor_tensor(eq, eq, CONST(k.const, "first").unsqueeze(1).broadcast_to([P, D1, D2]), ALU.mult)\
                .then_inc(s["ranked"], 1)

        def prologue():
            layer_rstd(pool, k, 0, s, past)
            rank(0, 0)

        def body(g, gp, first, last):
            for c in range(TPG):
                if c < 3 or not last:
                    rank(g * TPG + c + 1, (c + 1) % 2)
                if c == 0 and not last:
                    layer_rstd(pool, k, g + 1, s, past)

        run_groups(pool, prologue, body, lambda: None)

    def sync(self, sp):
        pass


class Mixture:

    CHUNKS = 6

    def __init__(self, k):
        self.k = k
        self.s, self.past = k.signals(
            {n: TILES * self.CHUNKS for n in ("up", "silu", "hid", "pT", "hidT", "out")} | {"x": TILES + 1, "X": TILES})
        self.chunks = [(k.w3g[:, n * 512:(n + 1) * 512], k.w3u[:, n * 512:(n + 1) * 512],
                        k.w3d[:, 4 * n:4 * n + 4, :], 512) for n in range(5)]
        self.chunks.append((k.w3g[:, 2560:2624], k.w3u[:, 2560:2624], k.w3d[:, 20:21, :], I3))

    def tensor(self, pe):
        k, s, past = self.k, self.s, self.past
        ident = CONST(k.const, "ident")

        def up(t, tp, n):
            i = t * self.CHUNKS + n
            gate, upw, _, width = self.chunks[n]
            if n == 0:
                pe.wait_ge(s["x"], past["x"] + t + 1)
            at_least(pe, s["hid"], i - 1, past["hid"])
            b = 2 * (n % 2)
            pe.matmul(k.bank[b][:, 0:width], k.hx[tp][:, :], gate, start=True, stop=True)
            pe.matmul(k.bank[b + 1][:, 0:width], k.hx[tp][:, :], upw, start=True, stop=True).then_inc(s["up"], 1)

        def turn(t, n):
            i = t * self.CHUNKS + n
            width = self.chunks[n][3]
            pe.wait_ge(s["hid"], past["hid"] + i + 1)
            at_least(pe, s["hidT"], i - 1, past["hidT"])
            for f in range(max(width // P, 1)):
                last = pe.transpose(k.bank[4 + n % 2][:, f * P:(f + 1) * P], k.hid3[n % 2][:, f * P:(f + 1) * P],
                                    ident)
            last.then_inc(s["pT"], 1)

        def down(t, tp, n):
            i = t * self.CHUNKS + n
            width = self.chunks[n][3]
            pe.wait_ge(s["hidT"], past["hidT"] + i + 1)
            if n == 0:
                at_least(pe, s["X"], t - 1, past["X"])
            for f in range(max(width // P, 1)):
                w = min(width, P)
                last = pe.matmul(k.bank[6 + tp][:, 0:P], k.hid3T[n % 2][0:w, f * P:(f + 1) * P],
                                 self.chunks[n][2][0:w, f, :], start=(n == 0 and f == 0),
                                 stop=(n == self.CHUNKS - 1))
            last.then_inc(s["out"], 1)

        def body(j, first):
            for u in range(2 * self.CHUNKS):
                t, n, tp = j * 2 + u // self.CHUNKS, u % self.CHUNKS, u // self.CHUNKS
                up(t, tp, n)
                if u >= 1:
                    turn(j * 2 + (u - 1) // self.CHUNKS, (u - 1) % self.CHUNKS)
                elif not first:
                    turn(j * 2 - 1, self.CHUNKS - 1)
                if u >= 2:
                    down(j * 2 + (u - 2) // self.CHUNKS, (u - 2) // self.CHUNKS, (u - 2) % self.CHUNKS)
                elif not first:
                    down(j * 2 - 1, 1, self.CHUNKS - 2 + u)

        def tail():
            turn(TILES - 1, self.CHUNKS - 1)
            down(TILES - 1, 1, self.CHUNKS - 2)
            down(TILES - 1, 1, self.CHUNKS - 1)

        pe.wait_ge(k.loaded["f3"], 16 * k.parts["f3"])
        run_loop(pe, TILES // 2, body, tail)

    def scalar(self, act):
        k, s, past = self.k, self.s, self.past

        def silu(t, n):
            i = t * self.CHUNKS + n
            width = self.chunks[n][3]
            act.wait_ge(s["up"], past["up"] + i + 1)
            at_least(act, s["hid"], i - 1, past["hid"])
            act.activation(k.silu3[n % 2][:, 0:width], k.bank[2 * (n % 2)][:, 0:width], ACT.Silu)\
                .then_inc(s["silu"], 1)

        def turned(t, n):
            i = t * self.CHUNKS + n
            w = min(self.chunks[n][3], P)
            act.wait_ge(s["pT"], past["pT"] + i + 1)
            at_least(act, s["out"], i - 1, past["out"])
            cols = GT if w == P else P
            act.activation(k.hid3T[n % 2][0:w, 0:cols], k.bank[4 + n % 2][0:w, 0:cols], ACT.Copy)\
                .then_inc(s["hidT"], 1)

        def body(j, first):
            for u in range(2 * self.CHUNKS):
                silu(j * 2 + u // self.CHUNKS, u % self.CHUNKS)
                if u >= 1:
                    turned(j * 2 + (u - 1) // self.CHUNKS, (u - 1) % self.CHUNKS)
                elif not first:
                    turned(j * 2 - 1, self.CHUNKS - 1)

        run_loop(act, TILES // 2, body, lambda: turned(TILES - 1, self.CHUNKS - 1))

    def vector(self, dve):
        k, s, past = self.k, self.s, self.past

        def weigh(t, n):
            i = t * self.CHUNKS + n
            width = self.chunks[n][3]
            dve.wait_ge(s["up"], past["up"] + i + 1)
            up = k.bank[2 * (n % 2) + 1][:, 0:width]
            part = k.up3[n % 2][:, 0:width]
            if n < 5:
                groups, src, lo = (8, k.route, 8 * n) if n < 4 else (L3, k.anchor, 0)
                w = src[:, bass.ds(t, 1), lo:lo + groups].rearrange("p a e -> p (a e)").unsqueeze(2)\
                    .broadcast_to([P, groups, width // groups])
                shape = dict(e=groups)
                dve.tensor_tensor(part.rearrange("p (e i) -> p e i", **shape), up.rearrange("p (e i) -> p e i", **shape),
                                  w, ALU.mult)
            else:
                dve.tensor_scalar(part, up, k.gates[:, 7:8], None, ALU.mult)
            dve.drain()
            dve.wait_ge(s["silu"], past["silu"] + i + 1)
            at_least(dve, s["pT"], i - 1, past["pT"])
            dve.tensor_tensor(k.hid3[n % 2][:, 0:width], part, k.silu3[n % 2][:, 0:width], ALU.mult)\
                .then_inc(s["hid"], 1)

        def add(t, tp):
            dve.wait_ge(s["out"], past["out"] + (t + 1) * self.CHUNKS)
            x = k.X[:, bass.ds(t, 1), :]
            dve.tensor_tensor(x, k.bank[6 + tp][:, 0:P].unsqueeze(1), x, ALU.add).then_inc(s["X"], 1)

        def take(t, tp):
            dve.tensor_scalar(k.hx[tp][:, :], k.HT[:, bass.ds(t * P, P)], 1.0, 0.0, ALU.mult, ALU.add)\
                .then_inc(s["x"], 1)

        def body(j, first):
            for u in range(2 * self.CHUNKS):
                t, n, tp = j * 2 + u // self.CHUNKS, u % self.CHUNKS, u // self.CHUNKS
                weigh(t, n)
                if n == 3:
                    take(t + 1, 1 - tp)
                if n == 2 and not (first and tp == 0):
                    add(t - 1, 1 - tp)

        dve.memset(k.HT[:, B * S:B * S + P], 0.0)
        dve.drain()
        take(0, 0)
        run_loop(dve, TILES // 2, body, lambda: add(TILES - 1, 1))

    def gpsimd(self, pool):
        pass

    def sync(self, sp):
        pass


def build(nc, ins, out):
    with ExitStack() as ctx:
        k = Kernel(nc, ins, out, ctx)
        block = ctx.enter_context(nc.Block())

        @block.sync
        def _(sp):
            k.load(sp)
            for n, part in enumerate(k.program):
                if n:
                    sp.wait_ge(k.s_part, 4 * n)
                part.sync(sp)
                k.load_late(sp, n)
            sp.wait_ge(k.s_part, 4 * len(k.program))
            sp.dma_start(out, k.X[:, :, :]).then_inc(k.s_out, 16)
            sp.wait_ge(k.s_out, 16)

        @block.tensor
        def _(pe):
            k.prepare_tensor(pe)
            for n, part in enumerate(k.program):
                k.enter(pe, n)
                part.tensor(pe)
                pe.drain().then_inc(k.s_part, 1)

        @block.scalar
        def _(act):
            k.prepare_scalar(act)
            for n, part in enumerate(k.program):
                k.enter(act, n)
                part.scalar(act)
                act.drain().then_inc(k.s_part, 1)

        @block.vector
        def _(dve):
            k.prepare_vector(dve)
            for n, part in enumerate(k.program):
                k.enter(dve, n)
                part.vector(dve)
                dve.drain().then_inc(k.s_part, 1)

        @block.gpsimd
        def _(pool):
            k.prepare_gpsimd(pool)
            for n, part in enumerate(k.program):
                k.enter(pool, n)
                part.gpsimd(pool)
                pool.drain().then_inc(k.s_part, 1)


def kernel_inputs(a):
    f = {n: np.asarray(v) for n, v in a.items()}
    x = f["x"].reshape(TILES, P, D).transpose(1, 0, 2)
    ctx = f["ctx_1024"].reshape(B * S, D)
    att = np.zeros((P, ATT_W.width), np.float32)

    def put(name, value):
        v = ATT_W(att, name)
        v[:] = np.asarray(value).reshape(v.shape)

    even_odd = np.arange(D).reshape(PAIRS, 2, DK).transpose(1, 0, 2).ravel()
    for n in ("wq", "wk", "wv", "wo"):
        cols = even_odd if n == "wv" else np.arange(D)
        put(f"{n}_x0", f["L0_xattn_" + n].T[:, cols])
        put(f"{n}_x1", f["L1_xattn_W" + n[1]][:, cols])
        put(f"{n}_x3", f["L3_xattn_W" + n[1]].T[:, cols])
    for n in ("bq", "bk", "bv"):
        for layer in (0, 1, 3):
            put(f"{n}_x{layer}", f[f"L{layer}_xattn_" + n])
    wqkv = f["L0_ffn_wqkv"]
    kv_rows = (np.arange(H)[:, None] // 4 * DK + np.arange(DK)[None]).ravel()
    swap = np.arange(D) // DK * DK + (np.arange(D) + DK // 2) % DK
    wq, wk, wv = wqkv[:H * DK], wqkv[H * DK:H * DK + 4 * DK][kv_rows], wqkv[H * DK + 4 * DK:][kv_rows]
    for n, w in (("wq_f0", wq), ("wqs_f0", wq[swap]), ("wk_f0", wk), ("wks_f0", wk[swap]), ("wv_f0", wv[even_odd]),
                 ("wo_f0", f["L0_ffn_wo"])):
        put(n, w.T)
    put("w1_x2", f["L2_xattn_W1"])
    put("w2t_x2", f["L2_xattn_W2"].T)
    put("b1_x2", f["L2_xattn_b1"])
    put("b2_x2", f["L2_xattn_b2"])
    put("ln1", f["L0_ffn_ln1_w"])
    put("ln2", f["L0_ffn_ln2_w"])
    put("mask", np.concatenate([f["fside_1xSxS2_0"][0]] * 2))
    put("gate0", f["L0_ffn_gate_w"].T)
    put("switch", f["L1_ffn_switch_w"])
    put("gate3", f["L3_ffn_gate_weight"].T)
    rows = np.zeros((1, ROWS.width), np.float32)
    for n, v in (("bo_x0", f["L0_xattn_bo"]), ("bo_x1", f["L1_xattn_bo"]), ("bo_x3", f["L3_xattn_bo"]),
                 ("b2_f2", f["L2_ffn_b2"]), ("g", np.concatenate([f["g_xattn"], f["g_ffn"]])),
                 ("decay", f["L0_xattn_time_decay"]), ("switch_b", f["L1_ffn_switch_b"]),
                 ("gate_bias", f["L3_ffn_gate_bias"])):
        ROWS(rows, n)[0] = v

    def down(w):
        return w.reshape(-1, P, D).transpose(1, 0, 2).reshape(P, -1)

    f0 = np.concatenate([f["L0_ffn_w13"].transpose(2, 0, 1).reshape(D, -1),
                         down(f["L0_ffn_w2"].transpose(0, 2, 1).reshape(-1, D))], 1)
    f1 = np.concatenate([f["L1_ffn_w1"].transpose(1, 0, 2).reshape(D, -1), down(f["L1_ffn_w2"].reshape(-1, D)),
                         f["L1_ffn_b1"].reshape(-1, P).T], 1)
    f2 = np.zeros((P, F2_W.width), np.float32)
    F2_W(f2, "m1")[:] = f["L2_ffn_m1"]
    F2_W(f2, "m2")[0:DL] = f["L2_ffn_m2"].reshape(DL, -1)
    F2_W(f2, "m2")[DL] = f["L2_ffn_mb"].ravel()
    F2_W(f2, "w1")[:] = f["L2_ffn_w1"].reshape(D, -1)
    F2_W(f2, "w2")[:] = down(f["L2_ffn_w2"].transpose(1, 0, 2).reshape(-1, D))
    shared_down = np.zeros((P, D), np.float32)
    shared_down[0:I3] = f["L3_ffn_shared_w_down"]

    def up3(which):
        return [f["L3_ffn_w_" + which].transpose(1, 0, 2).reshape(D, -1),
                f["L3_ffn_anchor_w_" + which].transpose(1, 0, 2).reshape(D, -1), f["L3_ffn_shared_w_" + which]]

    f3 = np.concatenate(up3("gate") + up3("up") + [down(f["L3_ffn_w_down"].reshape(-1, D)),
                                                   down(f["L3_ffn_anchor_w_down"].reshape(-1, D)), shared_down], 1)
    return {"x": x, "ctx_t": ctx.T, "ctx_n": ctx.reshape(B, S, D).transpose(1, 0, 2), "att_w": att, "rows": rows,
            "const": constants(), "f0_w": f0, "f1_w": f1, "f2_w": f2, "f3_w": f3, "b2e": f["L1_ffn_b2"]}


F2_W = Columns([("m1", DL), ("m2", D1 * D2), ("w1", D1 * D2), ("w2", D1 * D2)])
F0_COLS = E0 * 2 * F0 + E0 * F0 // P * D
F1_COLS = E1 * F1 + E1 * F1 // P * D + E1 * F1 // P
UP3 = E3 * I3 + L3 * A3 + I3
F3_COLS = 2 * UP3 + 21 * D
ATT_BUF = Columns([("probs0", H * S), ("probs1", H * S), ("PT0", H * S), ("PT1", H * S), ("Kblk0", 4 * H * S),
                   ("Kblk1", 4 * H * S), ("QT0", GT), ("QT1", GT), ("KT", GT), ("ctxT0", GT), ("ctxT1", GT),
                   ("attn0", GT), ("attn1", GT), ("aT", GT), ("soft0", TPG * S), ("soft1", TPG * S)])
X2_BUF = Columns([("skip", 4 * H * S), ("ctxN0", GB * D), ("ctxN1", GB * D)])
FFN_BUF = Columns([("HT", B * S + P), ("route", TILES * E3), ("anchor", TILES * L3), ("hid0", 4 * GT), ("hid1", 4 * GT),
                   ("silu", 2 * GT), ("lrT0", GT), ("lrT1", GT), ("hidc0", GT), ("hidc1", GT), ("eq0", GT), ("eq1", GT),
                   ("hidcT", GT), ("silu30", GT), ("silu31", GT), ("up30", GT), ("up31", GT), ("hid30", GT), ("hid31", GT),
                   ("hid3T0", GT), ("hid3T1", GT), ("hx0", P), ("hx1", P)])


class Kernel:

    def __init__(self, nc, ins, out, ctx):
        self.nc, self.ins, self.ctx = nc, ins, ctx
        self.named, self.given = {n: self.sem(n) for n in ("X", "aTp")}, {"X": 2, "aTp": 2}

        def sb(name, shape):
            return ctx.enter_context(nc.sbuf_tensor(name, shape, F32))

        self.X = sb("X", [P, TILES, D])
        self.att_w = sb("att_w", [P, ATT_W.width])
        self.rows = sb("rows", [P, ROWS.width])
        self.const = sb("const", [P, CONST.width])
        self.arena_a = sb("arena_a", [P, max(F0_COLS, F3_COLS)])
        self.arena_b = sb("arena_b", [P, F1_COLS])
        self.f2_w = sb("f2_w", [P, F2_W.width])
        self.b2e = sb("b2e", [E1, D])
        self.XH = self.arena_b[:, 0:TILES * D].rearrange("p (t n) -> p t n", t=TILES)
        vcols = GB * PAIRS * 2 * VW + S - 2 * VW
        self.Vblk = [sb(f"Vblk{i}", [P, vcols]) for i in range(2)]
        self.xn = sb("xn", [P, TPG, D])
        self.hT = [sb(f"hT{i}", [P, GT]) for i in range(2)]
        self.tmp = sb("tmp", [P, GT])
        work = sb("work", [P, max(ATT_BUF.width, FFN_BUF.width)])

        def att(name):
            return ATT_BUF(work, name)

        def ffn(name):
            return FFN_BUF(work, name)

        self.probs = [att("probs0"), att("probs1")]
        self.PT = [att("PT0"), att("PT1")]
        self.Kblk = [att(f"Kblk{i}").rearrange("p (b h n) -> p b h n", b=4, h=H) for i in range(2)]
        self.QT, self.KT = [att("QT0"), att("QT1")], att("KT")
        self.ctxT = [att("ctxT0"), att("ctxT1")]
        self.attn = [att(f"attn{i}").rearrange("p (c n) -> p c n", c=TPG) for i in range(2)]
        self.aT = att("aT")
        self.soft = [att(f"soft{i}").rearrange("p (c n) -> p c n", c=TPG) for i in range(2)]
        self.ctxN = [X2_BUF(work, f"ctxN{i}")[0:S].rearrange("p (b n) -> p b n", b=GB) for i in range(2)]
        self.HT = ffn("HT")
        self.route = ffn("route").rearrange("p (t e) -> p t e", t=TILES)
        self.anchor = ffn("anchor").rearrange("p (t e) -> p t e", t=TILES)
        self.hid = [ffn(f"hid{i}").rearrange("p (f n) -> p f n", f=4) for i in range(2)]
        self.silu = ffn("silu").rearrange("p (f n) -> p f n", f=2)
        self.lrT = [ffn("lrT0")[0:DL + 1], ffn("lrT1")[0:DL + 1]]
        self.hidc, self.eq, self.hidcT = [ffn("hidc0"), ffn("hidc1")], [ffn("eq0"), ffn("eq1")], ffn("hidcT")
        self.silu3, self.up3 = [ffn("silu30"), ffn("silu31")], [ffn("up30"), ffn("up31")]
        self.hid3, self.hid3T = [ffn("hid30"), ffn("hid31")], [ffn("hid3T0"), ffn("hid3T1")]
        self.hx = [ffn("hx0"), ffn("hx1")]

        self.bn, self.mv = sb("bn", [P, TPG, 6]), sb("mv", [P, TPG, 2])
        self.veps, self.rstd, self.rms = (sb(n, [P, TPG]) for n in ("veps", "rstd", "rms"))
        self.minus_half, self.eps = sb("minus_half", [P, TPG]), sb("eps", [P, TPG])
        self.zero, self.gate, self.alpha = sb("zero", [P, 1]), sb("gate", [P, 2]), sb("alpha", [P, 1])
        self.onesrow = sb("onesrow", [P, GT])
        self.top, self.rsum = sb("top", [P, 2 * H]), sb("rsum", [P, H])
        self.gates, self.decay, self.b2c = sb("gates", [P, 8]), sb("decay", [P, S]), sb("b2c", [P, D])[:, :]
        self.bqs = {n: sb(f"bqs_{n}", [P, 1])[:, :] for n in ("x0", "x1", "x3")}
        self.wo = {n: sb(f"wo_{n}s", [P, D])[:, :] for n in ("x0", "x1", "x3")}
        self.bo = {n: sb(f"bo_{n}s", [P, D])[:, :] for n in ("x0", "x1", "x3")}
        self.wo["f0"] = ATT_W(self.att_w, "wo_f0")
        self.decay = self.decay[:, :]
        self.wc, self.bc = sb("wc", [P, D])[:, :], sb("bc", [P, 2])
        self.lg, self.taken = sb("lg", [P, TPG, 16]), sb("taken", [P, TPG, E3 + 8])
        self.cand, self.ex = sb("cand", [P, TPG, E3 + 8]), sb("ex", [P, TPG, E3])
        self.sg, self.sc = sb("sg", [P, TPG, E3]), sb("sc", [P, TPG, E3])
        self.t8, self.m8 = sb("t8", [P, TPG, 8]), sb("m8", [P, TPG, 8])
        self.g8, self.gm = sb("g8", [P, TPG, G3, 8]), sb("gm", [P, TPG, 2, G3])
        self.pk, self.wt = sb("pk", [P, 2, TPG, 8]), sb("wt", [P, TPG, E1])
        self.wtT, self.sm = sb("wtT", [E1, GT]), sb("sm", [P, 16])

        psum = ctx.enter_context(nc.psum_tensor("psum", [P, 8, GT], F32))
        self.bank = [psum[:, i, :] for i in range(8)]
        self.scores = [psum[:, 2 * i:2 * i + 2, :].rearrange("p a (h n) -> p (a h) n", n=S) for i in range(2)]

        a, b = self.arena_a, self.arena_b
        n0, n1 = E0 * 2 * F0, E1 * F1
        self.experts = {
            "f0": (a[:, 0:n0].rearrange("p (e f) -> p e f", e=E0),
                   a[:, n0:F0_COLS].rearrange("p (e f n) -> p e f n", e=E0, n=D)),
            "f1": (b[:, 0:n1].rearrange("p (e f) -> p e f", e=E1),
                   b[:, n1:2 * n1].rearrange("p (e f n) -> p e f n", e=E1, n=D))}
        self.b1e = b[:, 2 * n1:F1_COLS]
        self.w3g, self.w3u = a[:, 0:UP3], a[:, UP3:2 * UP3]
        self.w3d = a[:, 2 * UP3:F3_COLS].rearrange("p (c n) -> p c n", n=D)
        self.m1, self.m2, self.w1c = (F2_W(self.f2_w, n) for n in ("m1", "m2", "w1"))
        self.m2 = self.m2[0:DL + 1]
        self.w2c = F2_W(self.f2_w, "w2").rearrange("p (c n) -> p c n", n=D)

        self.ctxT_dram, self.ctxN_dram = ins["ctx_t"], ins["ctx_n"]
        self.loaded = {n: self.sem(f"loaded_{n}") for n in ("small", "x", "f0", "f1", "f2", "f3")}
        self.parts = {"f0": 2, "f1": 2, "f2": 1, "f3": 2}
        self.s_part, self.s_out = self.sem("part_done"), self.sem("out_stored")
        self.s_gates, self.s_fold, self.s_consts = self.sem("gates"), self.sem("fold"), self.sem("constants")
        self.s_prepared = self.sem("prepared")
        self.program = [Attention(self, "x0"), Attention(self, "f0"), Route(self, "f0"), Experts(self, "f0"),
                        Attention(self, "x1"), Route(self, "f1"), Experts(self, "f1"), WholeAttention(self),
                        Choices(self), Attention(self, "x3"), Route(self, "f3"), Mixture(self)]

    def signals(self, times):
        past = {}
        for name, n in times.items():
            if name not in self.named:
                self.named[name] = self.sem(name)
            past[name] = self.given.get(name, 0)
            self.given[name] = past[name] + n
        return {name: self.named[name] for name in times}, past

    def sem(self, name):
        return self.ctx.enter_context(self.nc.semaphore("s_" + name))

    def load(self, sp):
        i, small = self.ins, self.loaded["small"]
        sp.dma_start(self.rows[:, :], i["rows"].rearrange("a n -> (a n)").partition_broadcast(P)).then_inc(small, 16)
        sp.dma_start(self.att_w[:, :], i["att_w"]).then_inc(small, 16)
        sp.dma_start(self.const[:, :], i["const"]).then_inc(small, 16)
        sp.dma_start(self.X[:, :, :], i["x"]).then_inc(self.loaded["x"], 16)
        sp.dma_start(self.b2e[:, :], i["b2e"]).then_inc(small, 16)

    def load_expert(self, sp, name, tile, cols):
        src = self.ins[name + "_w"]
        half = cols // 2
        for a, b in ((0, half), (half, cols)):
            sp.dma_start(tile[:, a:b], src[:, a:b]).then_inc(self.loaded[name], 16)

    def load_late(self, sp, n):
        if n == 0:
            self.load_expert(sp, "f0", self.arena_a, F0_COLS)
            sp.dma_start(self.f2_w[:, :], self.ins["f2_w"]).then_inc(self.loaded["f2"], 16)
        if n == 4:
            self.load_expert(sp, "f1", self.arena_b, F1_COLS)
            self.load_expert(sp, "f3", self.arena_a, F3_COLS)

    def enter(self, eng, n):
        if n:
            eng.wait_ge(self.s_part, 4 * n)
        else:
            eng.wait_ge(self.loaded["small"], 64)
            eng.wait_ge(self.loaded["x"], 16)
            eng.wait_ge(self.s_prepared, 2)

    def prepare_gpsimd(self, pool):
        pool.memset(self.minus_half[:, :], -0.5)
        pool.memset(self.eps[:, :], EPS)
        pool.memset(self.zero[:, :], 0.0)
        pool.memset(self.gate[:, :], 1.0)
        pool.memset(self.onesrow[:, :], 1.0)
        for v in self.Vblk:
            pool.memset(v[:, :], 0.0)
        pool.drain()
        for v in self.Vblk:
            w = v[:, 0:GB * PAIRS * 2 * VW].rearrange("p (r x) -> p r x", r=GB * PAIRS)
            pool.memset(w[0:S, :, DK:DK + 1], 1.0)
            pool.memset(w[S:P, :, 2 * VW - 1:2 * VW], 1.0)
        pool.drain().then_inc(self.s_prepared, 1)

    def prepare_scalar(self, act):
        act.wait_ge(self.loaded["small"], 64)
        act.activation(self.gates[:, :], ROWS(self.rows, "g"), ACT.Tanh).then_inc(self.s_gates, 1)

    def prepare_tensor(self, pe):
        pe.wait_ge(self.loaded["small"], 64)
        for i, n in enumerate(("x0", "x1", "x3")):
            pe.matmul(self.bank[i][:, 0:D], ATT_W(self.att_w, f"bv_{n}").broadcast_to([P, P]),
                      ATT_W(self.att_w, f"wo_{n}"), start=True, stop=True)
        w1, w2t = ATT_W(self.att_w, "w1_x2"), ATT_W(self.att_w, "w2t_x2")
        pe.matmul(self.bank[3][:, 0:D], w1, w2t, start=True, stop=True)
        for _ in range(2):
            pe.drain().then_inc(self.named["aTp"], 1)
        pe.matmul(self.bank[4][:, 0:1], w2t, ATT_W(self.att_w, "b1_x2"), start=True, stop=True).then_inc(self.s_fold, 1)

    def prepare_vector(self, dve):
        for _ in range(2):
            dve.drain().then_inc(self.named["X"], 1)
        dve.wait_ge(self.s_gates, 1)
        dve.wait_ge(self.s_fold, 1)
        dve.memset(self.alpha[:, :], 0.1)
        dve.tensor_scalar(self.decay, CONST(self.const, "dist"), ROWS(self.rows, "decay"), None, ALU.mult)
        dve.tensor_scalar(self.b2c, ROWS(self.rows, "b2_f2"), self.gates[:, 6:7], None, ALU.mult)
        dve.tensor_copy(self.wc, self.bank[3][:, 0:D])
        dve.tensor_tensor(self.bc[:, 0:1], self.bank[4][:, 0:1], ATT_W(self.att_w, "b2_x2"), ALU.add)
        for i, (n, g) in enumerate((("x0", 0), ("x1", 1), ("x3", 3))):
            dve.tensor_scalar(self.bqs[n], ATT_W(self.att_w, f"bq_{n}"), DK ** -0.5, None, ALU.mult)
            dve.tensor_scalar(self.wo[n], ATT_W(self.att_w, f"wo_{n}"), self.gates[:, g:g + 1], None, ALU.mult)
            dve.tensor_tensor(self.bo[n], self.bank[i][:, 0:D], ROWS(self.rows, f"bo_{n}"), ALU.add)
        dve.drain()
        for n, g in (("x0", 0), ("x1", 1), ("x3", 3)):
            dve.tensor_scalar(self.bo[n], self.bo[n], self.gates[:, g:g + 1], None, ALU.mult)
        dve.tensor_scalar(self.bc[:, 1:2], self.bc[:, 0:1], D ** -0.5, None, ALU.mult)
        dve.tensor_scalar(self.alpha[:, :], self.alpha[:, :], self.gates[:, 7:8], None, ALU.mult)
        dve.drain().then_inc(self.s_prepared, 1)


def kernel(**inputs):
    import concourse.bacc as bacc
    from concourse.bass_utils import run_bass_kernel_spmd

    arrays = {n: np.ascontiguousarray(v) for n, v in kernel_inputs(inputs).items()}
    nc = bacc.Bacc("TRN2", target_bir_lowering=False, num_devices=1)
    ins = {n: nc.dram_tensor(n + "_dram", v.shape, mybir.dt.from_np(v.dtype), kind="ExternalInput").ap()
           for n, v in arrays.items()}
    out = nc.dram_tensor("out_dram", (P, TILES, D), F32, kind="ExternalOutput").ap()
    build(nc, ins, out)
    r = run_bass_kernel_spmd(nc, [{n + "_dram": v for n, v in arrays.items()}], core_ids=[0])
    return r.results[0]["out_dram"].transpose(1, 0, 2).reshape(B, S, D)
```

```python
from contextlib import ExitStack

import numpy as np
import concourse.bass as bass
from concourse import mybir

F32 = mybir.dt.float32
ALU = mybir.AluOpType
ACT = mybir.ActivationFunctionType
AX_X = mybir.AxisListType.X

P = 128
D = 128
B, S = 64, 64
TILES = B * S // P
TPG = 4
GROUPS = TILES // TPG
GT = TPG * P
GB = GT // S
H, DK = 16, 8
PAIRS = H // 2
VW = DK + 1
EPS = 1e-5
E0, F0 = 8, 256
E1, F1 = 8, 512
D1, D2, DL = 8, 64, 64
E3, I3, G3, K3 = 32, 64, 4, 6
L3, A3 = 16, 32
SENT = -3.0e38
TAKEN = 3.0e38
LOW = -1.0e30


class Columns:

    def __init__(self, widths):
        self.at, self.width = {}, 0
        for name, n in widths:
            self.at[name] = (self.width, self.width + n)
            self.width += n

    def __call__(self, tile, name):
        a, b = self.at[name]
        return tile[:, a:b]


ATT = ("x0", "f0", "x1", "x3")
ATT_W = Columns([(f"{w}_{k}", D) for k in ATT for w in ("wq", "wk", "wv", "wo")]
                + [("wqs_f0", D), ("wks_f0", D), ("w1_x2", D), ("w2t_x2", D)]
                + [(f"{w}_{k}", 1) for k in ("x0", "x1", "x3") for w in ("bq", "bk", "bv")]
                + [("b1_x2", 1), ("b2_x2", 1), ("ln1", 1), ("ln2", 1), ("mask", S)]
                + [("gate0", E0), ("switch", E1), ("gate3", E3)])
ROWS = Columns([("bo_x0", D), ("bo_x1", D), ("bo_x3", D), ("b2_f2", D), ("g", 8), ("decay", 1),
                ("switch_b", E1), ("gate_bias", E3)])
CONST = Columns([("ident", P), ("head", H), ("dist", S), ("causal", S), ("qcos", S), ("qsin", S),
                 ("kcos", S), ("ksin", S), ("first", D2)])


def constants():
    c = np.zeros((P, CONST.width), np.float32)
    row = np.arange(P)
    CONST(c, "ident")[:] = np.eye(P)
    CONST(c, "head")[:] = row[:, None] // DK == np.arange(H)[None]
    q, k = row[:, None] % S, np.arange(S)[None]
    CONST(c, "dist")[:] = -np.abs(q - k)
    CONST(c, "causal")[:] = np.where(k <= q, 0.0, SENT)
    freq = (1.0 / 10000.0 ** (np.arange(0, DK, 2, dtype=np.float32) / DK)).astype(np.float32)
    angle = np.arange(S, dtype=np.float32)[None] * freq[row % (DK // 2)][:, None]
    sign = np.where(row % DK < DK // 2, -1.0, 1.0)[:, None]
    CONST(c, "kcos")[:] = np.cos(angle)
    CONST(c, "ksin")[:] = np.sin(angle) * sign
    CONST(c, "qcos")[:] = np.cos(angle) * DK ** -0.5
    CONST(c, "qsin")[:] = np.sin(angle) * sign * DK ** -0.5
    CONST(c, "first")[:] = D2 - np.arange(D2)[None]
    return c


def over_heads(table):
    return table.unsqueeze(1).broadcast_to([P, H, S])


def run_groups(eng, prologue, body, tail):
    prologue()
    body(0, 0, True, False)
    with eng.Fori(0, (GROUPS - 2) // 2) as j:
        body(j * 2 + 1, 1, False, False)
        body(j * 2 + 2, 0, False, False)
    body(GROUPS - 1, (GROUPS - 1) % 2, False, True)
    tail()


class Attention:


    def __init__(self, k, kind):
        self.k, self.kind = k, kind
        self.rope = kind == "f0"
        self.table = {"x0": k.decay, "f0": CONST(k.const, "causal")}.get(kind)
        nq = 2 if self.rope else 1
        self.s, self.past = k.signals(
            {n: GROUPS + 1 for n in ("stats", "rstd", "xn")}
            | {n: GROUPS for n in ("lnT", "hT", "aTp", "aT", "wo", "X")}
            | {n: nq * GROUPS for n in ("q", "QT", "k", "KT")} | {n: GROUPS for n in ("v", "V")}
            | {n: 2 * GROUPS for n in ("kblk0", "kblk1")}
            | {n: TILES for n in ("scores", "shifted", "exp", "pv", "attn")} | {n: 2 * TILES for n in ("pT", "PT")}
            | {n: 0 if self.rope else 8 * GROUPS for n in ("ctx0", "ctx1")})
        self.nq = 2 if self.rope else 1
        if self.rope:
            self.misc = {(0, "A"): "lnT", (0, "B"): "k", (0, "C"): "ks", (1, "A"): "q", (1, "B"): "qs",
                         (1, "C"): "v", (2, "B"): "aT", (3, "A"): "wo"}
        else:
            self.misc = {(0, "B"): "k", (0, "C"): "lnT", (1, "A"): "q", (1, "B"): "v", (2, "B"): "aT",
                         (3, "A"): "wo"}

    def w(self, name):
        return ATT_W(self.k.att_w, f"{name}_{self.kind}")

    def tensor(self, pe):
        k, s, past = self.k, self.s, self.past
        ident = CONST(k.const, "ident")
        misc = k.bank[7]

        def scores(t, c, gp, g):
            pe.wait_ge(s["QT"], past["QT"] + (g + 1) * self.nq)
            pe.wait_ge(s["kblk0"] if c < 2 else s["kblk1"], (past["kblk0"] if c < 2 else past["kblk1"]) + 2 * g + 2)
            if not (isinstance(t, int) and t < 2):
                pe.wait_ge(s["exp"], past["exp"] + t - 1)
            for n in range(2):
                for b in range(2):
                    at = c * P + b * S
                    last = pe.matmul(k.bank[2 * (c % 2) + n][b * S:(b + 1) * S, :],
                                     k.QT[gp][:, at:at + S],
                                     k.Kblk[c // 2][:, 2 * (c % 2) + b, n * 8:(n + 1) * 8, :],
                                     start=True, stop=True)
            last.then_inc(s["scores"], 1)

        def turn(t, c):
            pe.wait_ge(s["exp"], past["exp"] + t + 1)
            for half in range(2):
                if not (isinstance(t, int) and t < 1):
                    pe.wait_ge(s["PT"], past["PT"] + 2 * t - 1 + half)
                for p in range(4):
                    at = (half * 4 + p) * P
                    last = pe.transpose(k.bank[4 + half][:, p * P:(p + 1) * P],
                                        k.probs[c % 2][:, at:at + P], ident)
                last.then_inc(s["pT"], 1)

        def values(t, c, gp, g):
            pe.wait_ge(s["PT"], past["PT"] + 2 * t + 2)
            pe.wait_ge(s["V"], past["V"] + g + 1)
            if not (isinstance(t, int) and t < 1):
                pe.wait_ge(s["attn"], past["attn"] + t)
            for p in range(PAIRS):
                for b in range(2):
                    at = (2 * c + b) * PAIRS * 2 * VW + p * 2 * VW
                    last = pe.matmul(k.bank[6][b * S:(b + 1) * S, p * S:(p + 1) * S],
                                     k.PT[c % 2][:, p * P + b * S:p * P + (b + 1) * S],
                                     k.Vblk[gp][:, at:at + S], start=True, stop=True)
            last.then_inc(s["pv"], 1)

        def project(what, n, np_, first):
            if what == ("lnT" if self.rope else "k"):
                if first != "prologue":
                    pe.wait_ge(s["V"], past["V"] + n)
                if first is False:
                    pe.wait_ge(s["X"], past["X"] + n - 2)
            if what == "lnT":
                pe.wait_ge(s["xn"], past["xn"] + n + 1)
                if not self.rope:
                    pe.wait_ge(s["KT"], past["KT"] + n + 1)
                for c in range(TPG):
                    last = pe.transpose(misc[:, c * P:(c + 1) * P], k.xn[:, c, :], ident)
                last.then_inc(s["lnT"], 1)
            elif what in ("q", "qs"):
                if what == "qs":
                    pe.wait_ge(s["QT"], past["QT"] + 2 * n + 1)
                elif self.rope:
                    pe.wait_ge(s["KT"], past["KT"] + 2 * n + 2)
                else:
                    pe.wait_ge(s["hT"], past["hT"] + n + 1)
                w = self.w("wq") if what == "q" else self.w("wqs")
                pe.matmul(misc[:, :], w, k.hT[np_][:, :], start=True, stop=True).then_inc(s["q"], 1)
            elif what in ("k", "ks"):
                if not self.rope:
                    pe.wait_ge(s[f"ctx{np_}"], past[f"ctx{np_}"] + 8 * n + 16 - 8 * np_)
                elif what == "k":
                    pe.wait_ge(s["hT"], past["hT"] + n + 1)
                else:
                    pe.wait_ge(s["KT"], past["KT"] + 2 * n + 1)
                w = self.w("wk") if what == "k" else self.w("wks")
                src = k.hT[np_] if self.rope else k.ctxT[np_]
                pe.matmul(misc[:, :], w, src[:, :], start=True, stop=True).then_inc(s["k"], 1)
            elif what == "v":
                pe.wait_ge(s["QT"], past["QT"] + (n + 1) * self.nq)
                src = k.hT[np_] if self.rope else k.ctxT[np_]
                for b in range(GB):
                    for up in range(2):
                        last = pe.matmul(misc[up * S:(up + 1) * S, b * S:(b + 1) * S], src[:, b * S:(b + 1) * S],
                                         self.w("wv")[:, up * S:(up + 1) * S], start=True, stop=True)
                last.then_inc(s["v"], 1)

        def output(what, p, pp, before):
            if what == "aT":
                pe.wait_ge(s["attn"], past["attn"] + TPG * (p + 1))
                pe.wait_ge(*before)
                for c in range(TPG):
                    last = pe.transpose(misc[:, c * P:(c + 1) * P], k.attn[pp][:, c, :], ident)
                last.then_inc(s["aTp"], 1)
            else:
                pe.wait_ge(s["aT"], past["aT"] + p + 1)
                for c in range(TPG):
                    last = pe.matmul(misc[:, c * P:(c + 1) * P], k.aT[:, c * P:(c + 1) * P],
                                     k.wo[self.kind], start=True, stop=True)
                last.then_inc(s["wo"], 1)

        def place(c, where, g, gp, first, last):
            what = self.misc.get((c, where))
            if what in ("aT", "wo"):
                if not first:
                    before = (s["X"], past["X"] + g - 1) if last else (s["V"], past["V"] + g + 2)
                    output(what, g - 1, 1 - gp, before)
            elif what and not last:
                project(what, g + 1, 1 - gp, first)

        def prologue():
            for what in ("lnT", "k", "ks", "q", "qs", "v") if self.rope else ("k", "lnT", "q", "v"):
                project(what, 0, 0, "prologue")
            scores(0, 0, 0, 0)
            scores(1, 1, 0, 0)

        def body(g, gp, first, last):
            for c in range(TPG):
                t = g * TPG + c
                if c < 2:
                    scores(t + 2, c + 2, gp, g)
                elif not last:
                    scores(t + 2, c - 2, 1 - gp, g + 1)
                place(c, "A", g, gp, first, last)
                turn(t, c)
                place(c, "B", g, gp, first, last)
                if c > 0:
                    values(t - 1, c - 1, gp, g)
                elif not first:
                    values(t - 1, 3, 1 - gp, g - 1)
                place(c, "C", g, gp, first, last)

        def tail():
            values(TILES - 1, 3, (GROUPS - 1) % 2, GROUPS - 1)
            output("aT", GROUPS - 1, (GROUPS - 1) % 2, (s["X"], past["X"] + GROUPS - 1))
            output("wo", GROUPS - 1, (GROUPS - 1) % 2, None)

        run_groups(pe, prologue, body, tail)

    def scalar(self, act):
        k, s, past = self.k, self.s, self.past
        misc = k.bank[7]

        def evacuate(what, n, np_):
            if what == "lnT":
                act.wait_ge(s["lnT"], past["lnT"] + n + 1)
                act.activation(k.hT[np_][:, :], misc[:, :], ACT.Copy if not self.rope else ACT.Identity,
                               scale=1.0 if not self.rope else ATT_W(k.att_w, "ln1")).then_inc(s["hT"], 1)
            elif what == "q" and not self.rope:
                act.wait_ge(s["q"], past["q"] + n + 1)
                act.activation(k.QT[np_][:, :], misc[:, :], ACT.Identity, bias=k.bqs[self.kind],
                               scale=DK ** -0.5).then_inc(s["QT"], 1)
            elif what == "k" and not self.rope:
                act.wait_ge(s["k"], past["k"] + n + 1)
                if not (isinstance(n, int) and n < 1):
                    act.wait_ge(s["kblk0"], past["kblk0"] + 2 * n)
                    act.wait_ge(s["kblk1"], past["kblk1"] + 2 * n)
                act.activation(k.KT[:, :], misc[:, :], ACT.Identity, bias=self.w("bk")).then_inc(s["KT"], 1)
            elif what == "v":
                act.wait_ge(s["v"], past["v"] + n + 1)
                dst = k.Vblk[np_][:, 0:GB * PAIRS * 2 * VW].rearrange("p (b r x) -> p b r x", b=GB, r=PAIRS)
                src = misc[:, :].rearrange("p (b r x) -> p b r x", b=GB, r=PAIRS)
                for up in range(2):
                    last = act.activation(dst[up * S:(up + 1) * S, :, :, up * VW:up * VW + DK],
                                          src[up * S:(up + 1) * S], ACT.Copy)
                last.then_inc(s["V"], 1)

        def turned(t, c):
            for half in range(2):
                act.wait_ge(s["pT"], past["pT"] + 2 * t + 1 + half)
                if not (isinstance(t, int) and t < 2):
                    act.wait_ge(s["pv"], past["pv"] + t - 1)
                act.activation(k.PT[c % 2][:, half * GT:(half + 1) * GT], k.bank[4 + half][:, :],
                               ACT.Copy).then_inc(s["PT"], 1)

        def exp(t, c):
            act.wait_ge(s["shifted"], past["shifted"] + t + 1)
            if not (isinstance(t, int) and t < 2):
                act.wait_ge(s["pT"], past["pT"] + 2 * (t - 1))
            act.activation(k.probs[c % 2][:, :].rearrange("p (h n) -> p h n", h=H), k.scores[c % 2], ACT.Exp).then_inc(s["exp"], 1)

        def block_keys(g, heads):
            act.wait_ge(s["KT"], past["KT"] + (g + 1) * self.nq)
            if not (isinstance(g, int) and g < 1):
                act.wait_ge(s["scores"], past["scores"] + TPG * g)
            src = k.KT[:, GT // 2:GT].rearrange("p (b n) -> p b n", b=4)
            for h in heads:
                last = act.activation(k.Kblk[1][:, :, h, :], src, ACT.Copy,
                                      scale=CONST(k.const, "head")[:, h:h + 1])
            if heads[-1] == H - 1:
                last.then_inc(s["kblk1"], 1)

        def output(p, before=None):
            act.wait_ge(s["aTp"], past["aTp"] + p + 1)
            if not (isinstance(p, int) and p < 1):
                act.wait_ge(s["wo"], past["wo"] + p)
            act.activation(k.aT[:, :], misc[:, :], ACT.Copy).then_inc(s["aT"], 1)

        def place(c, where, g, gp, first, last):
            what = self.misc.get((c, where))
            if what == "aT":
                if not first:
                    output(g - 1)
            elif what not in (None, "wo") and not last:
                evacuate(what, g + 1, 1 - gp)

        def prologue():
            for what in ("lnT", "v") if self.rope else ("k", "lnT", "q", "v"):
                evacuate(what, 0, 0)
            exp(0, 0)
            block_keys(0, range(8, H))
            exp(1, 1)

        def body(g, gp, first, last):
            for c in range(TPG):
                t = g * TPG + c
                place(c, "A", g, gp, first, last)
                turned(t, c)
                if c in (1, 2) and not last:
                    block_keys(g + 1, range(4 + 4 * c, 8 + 4 * c))
                place(c, "B", g, gp, first, last)
                if c < 2 or not last:
                    exp(t + 2, c % 2)
                place(c, "C", g, gp, first, last)

        def tail():
            output(GROUPS - 1)

        run_groups(act, prologue, body, tail)

    def vector(self, dve):
        k, s, past = self.k, self.s, self.past
        misc = k.bank[7]

        def stats(n):
            layer_stats(dve, k, n, s["stats"])

        def normalise(n):
            dve.wait_ge(s["rstd"], past["rstd"] + n + 1)
            if not (isinstance(n, int) and n < 1):
                dve.wait_ge(s["lnT"], past["lnT"] + n)
            for c in range(TPG):
                x = k.X[:, bass.ds(n * TPG + c, 1), :]
                if self.rope:
                    h0 = k.XH[:, bass.ds(n * TPG + c, 1), :]
                    dve.tensor_scalar(h0, x, k.mv[:, c, 0:1], k.rstd[:, c:c + 1], ALU.subtract, ALU.mult)
                    dve.drain()
                    last = dve.tensor_scalar(k.xn[:, c, :], h0, k.rms[:, c:c + 1], 0.0, ALU.mult, ALU.add)
                else:
                    last = dve.tensor_scalar(k.xn[:, c, :], x, k.mv[:, c, 0:1], k.rstd[:, c:c + 1],
                                             ALU.subtract, ALU.mult)
            last.then_inc(s["xn"], 1)

        def shift(t, c):
            dve.wait_ge(s["scores"], past["scores"] + t + 1)
            sc = k.scores[c % 2]
            if self.table is not None:
                dve.tensor_tensor(sc, sc, over_heads(self.table), ALU.add)
                dve.drain()
            top = k.top[:, c % 2 * H:(c % 2 + 1) * H]
            dve.tensor_reduce(top, sc, AX_X, ALU.max)
            dve.drain()
            dve.tensor_tensor(sc, sc, top.unsqueeze(2).broadcast_to([P, H, S]),
                              ALU.subtract).then_inc(s["shifted"], 1)

        def divide(t, c, gp, g):
            dve.wait_ge(s["pv"], past["pv"] + t + 1)
            if not (isinstance(g, int) and g < 2):
                dve.wait_ge(s["aTp"], past["aTp"] + g - 1)
            pv = k.bank[6][:, :].rearrange("p (r x) -> p r x", r=PAIRS)[:, :, 0:2 * VW]\
                .rearrange("p r (u x) -> p r u x", u=2)
            dve.reciprocal(k.rsum[:, :], pv[:, :, :, DK])
            dve.drain()
            dve.tensor_tensor(k.attn[gp][:, c, :].rearrange("p (h x) -> p h x", h=H).rearrange("p (r u) x -> p r u x", u=2),
                              pv[:, :, :, 0:DK],
                              k.rsum[:, :].rearrange("p (r u) -> p r u", u=2).unsqueeze(3)
                              .broadcast_to([P, PAIRS, 2, DK]), ALU.mult).then_inc(s["attn"], 1)

        def rotate(what, n, np_):
            which = what[0]
            done, ready = which, which.upper() + "T"
            dst = (k.QT[np_] if which == "q" else k.KT)[:, :].rearrange("p (b n) -> p b n", b=GB)
            src = misc[:, :].rearrange("p (b n) -> p b n", b=GB)
            second = len(what) == 2
            dve.wait_ge(s[done], past[done] + 2 * n + 1 + second)
            if which == "k" and not second and not (isinstance(n, int) and n < 1):
                dve.wait_ge(s["kblk0"], past["kblk0"] + 2 * n)
                dve.wait_ge(s["kblk1"], past["kblk1"] + 2 * n)
            trig = CONST(k.const, which + ("sin" if second else "cos")).unsqueeze(1).broadcast_to([P, GB, S])
            if not second:
                dve.tensor_tensor(dst, src, trig, ALU.mult).then_inc(s[ready], 1)
            else:
                part = k.tmp[:, :].rearrange("p (b n) -> p b n", b=GB)
                dve.tensor_tensor(part, src, trig, ALU.mult)
                dve.drain()
                dve.tensor_tensor(dst, dst, part, ALU.add).then_inc(s[ready], 1)

        def block_keys(n, heads):
            dve.wait_ge(s["KT"], past["KT"] + (n + 1) * self.nq)
            if not (isinstance(n, int) and n < 1):
                dve.wait_ge(s["scores"], past["scores"] + TPG * n - 2)
            if self.rope:
                dve.tensor_copy(k.gate[:, 1:2], k.gate[:, 2:3])
                dve.drain()
            src = k.KT[:, 0:GT // 2].rearrange("p (b n) -> p b n", b=4)
            for h in heads:
                last = dve.tensor_scalar(k.Kblk[0][:, :, h, :], src, CONST(k.const, "head")[:, h:h + 1], 0.0,
                                         ALU.mult, ALU.add)
            if heads[-1] == H - 1:
                last.then_inc(s["kblk0"], 1)

        def residual(p):
            dve.wait_ge(s["wo"], past["wo"] + p + 1)
            prod = misc[:, :].rearrange("p (c n) -> p c n", c=TPG)
            if self.rope:
                xh = k.XH[:, bass.ds(p * TPG, TPG), :]
                dve.tensor_tensor(xh, prod, xh, ALU.add).then_inc(s["X"], 1)
            else:
                x = k.X[:, bass.ds(p * TPG, TPG), :]
                tmp = k.tmp[:, :].rearrange("p (c n) -> p c n", c=TPG)
                dve.tensor_tensor(tmp, prod, k.bo[self.kind].unsqueeze(1).broadcast_to([P, TPG, D]), ALU.add)
                dve.drain()
                dve.tensor_tensor(x, x, tmp, ALU.add).then_inc(s["X"], 1)

        def place(c, where, g, gp, last):
            what = self.misc.get((c, where))
            if self.rope and what in ("q", "qs", "k", "ks") and not last:
                rotate(what, g + 1, 1 - gp)

        def prologue():
            stats(0)
            normalise(0)
            if self.rope:
                for what in ("k", "ks", "q", "qs"):
                    rotate(what, 0, 0)
            block_keys(0, range(8, H))
            shift(0, 0)
            stats(1)
            normalise(1)
            shift(1, 1)

        def body(g, gp, first, last):
            for c in range(TPG):
                t = g * TPG + c
                place(c, "A", g, gp, last)
                if c < 2 or not last:
                    shift(t + 2, c % 2)
                if c == 1 and not last:
                    block_keys(g + 1, range(12, H))
                place(c, "B", g, gp, last)
                if c > 0:
                    divide(t - 1, c - 1, gp, g)
                elif not first:
                    divide(t - 1, 3, 1 - gp, g - 1)
                place(c, "C", g, gp, last)
                if c == 0 and not last:
                    block_keys(g + 1, range(8, 12))
                if c == 3 and not first:
                    residual(g - 1)
                if c == 2 and not last:
                    stats(g + 2)
                if c == 3 and not last:
                    normalise(g + 2)

        def tail():
            divide(TILES - 1, 3, (GROUPS - 1) % 2, GROUPS - 1)
            residual(GROUPS - 1)

        run_groups(dve, prologue, body, tail)

    def gpsimd(self, pool):
        k, s, past = self.k, self.s, self.past

        def block_keys(g):
            pool.wait_ge(s["KT"], past["KT"] + (g + 1) * self.nq)
            for half, done in enumerate((s["kblk0"], s["kblk1"])):
                if not (isinstance(g, int) and g < 1):
                    pool.wait_ge(s["scores"], past["scores"] + TPG * g - 2 + 2 * half)
                spot = 0 if half == 0 else 3
                pool.tensor_tensor(k.gate[:, spot:spot + 1], k.gate[:, 2:3], k.gate[:, 2:3], ALU.mult)
                src = k.KT[:, half * GT // 2:(half + 1) * GT // 2].rearrange("p (b n) -> p b n", b=4)
                for h in range(8):
                    last = pool.tensor_scalar(k.Kblk[half][:, :, h, :], src, CONST(k.const, "head")[:, h:h + 1],
                                              k.zero[:, 0:1], ALU.mult, ALU.add)
                last.then_inc(done, 1)

        def prologue():
            layer_rstd(pool, k, 0, s, past, self.rope)
            block_keys(0)
            layer_rstd(pool, k, 1, s, past, self.rope)

        def body(g, gp, first, last):
            if not last:
                block_keys(g + 1)
                layer_rstd(pool, k, g + 2, s, past, self.rope)

        run_groups(pool, prologue, body, lambda: None)

    def sync(self, sp):
        k, s, past = self.k, self.s, self.past
        if self.rope:
            return

        def load(g, gp):
            if g >= 2:
                sp.wait_ge(s["v"], past["v"] + g - 1)
            sp.dma_start(k.ctxT[gp][:, :], k.ctxT_dram[:, bass.ds(g * GT, GT)]).then_inc(s[f"ctx{gp}"], 16)

        for g in range(GROUPS):
            load(g, g % 2)


def layer_stats(dve, k, n, done):
    for c in range(TPG):
        dve.bn_stats(k.bn[:, c, :], k.X[:, bass.ds(n * TPG + c, 1), :].rearrange("p a n -> p (a n)"))
    dve.drain()
    for c in range(TPG):
        dve.bn_aggr(k.mv[:, c, :], k.bn[:, c, :])
    dve.drain()
    dve.tensor_scalar(k.veps[:, :], k.mv[:, :, 1], EPS, None, ALU.add).then_inc(done, 1)


def layer_rstd(pool, k, n, s, past, rms=False):
    pool.wait_ge(s["stats"], past["stats"] + n + 1)
    last = pool.tensor_tensor(k.rstd[:, :], k.veps[:, :], k.minus_half[:, 0:TPG], ALU.pow)
    if rms:
        pool.drain()
        pool.tensor_tensor(k.rms[:, :], k.mv[:, :, 1], k.rstd[:, :], ALU.mult)
        pool.drain()
        pool.tensor_tensor(k.rms[:, :], k.rms[:, :], k.rstd[:, :], ALU.mult)
        pool.drain()
        pool.tensor_tensor(k.rms[:, :], k.rms[:, :], k.eps[:, 0:TPG], ALU.add)
        pool.drain()
        last = pool.tensor_tensor(k.rms[:, :], k.rms[:, :], k.minus_half[:, 0:TPG], ALU.pow)
    last.then_inc(s["rstd"], 1)


def run_loop(eng, count, body, tail):
    body(0, True)
    with eng.Fori(1, count) as j:
        body(j, False)
    tail()


def pe_gate(pe, k):
    pe.matmul(k.bank[7][0:1, GT - 1:GT], CONST(k.const, "ident")[:, 0:1], CONST(k.const, "ident")[:, 0:1],
              start=True, stop=True)


def at_least(eng, sem, value, base):
    if not (isinstance(value, int) and value < 1):
        eng.wait_ge(sem, base + value)


class WholeAttention:


    def __init__(self, k):
        self.k = k
        self.s, self.past = k.signals(
            {n: GROUPS for n in ("stats", "rstd", "xn", "lnT", "hT", "q", "QT", "k", "KT", "scores", "shifted", "exp",
                                 "pT", "PT", "out", "X")} | {n: 16 * GROUPS for n in ("ctx0", "ctx1")})

    def tensor(self, pe):
        k, s, past = self.k, self.s, self.past
        ident = CONST(k.const, "ident")

        def front(n, np_):
            pe.wait_ge(s["xn"], past["xn"] + n + 1)
            at_least(pe, s["hT"], n, past["hT"])
            for c in range(TPG):
                last = pe.transpose(k.bank[0][:, c * P:(c + 1) * P], k.xn[:, c, :], ident)
            last.then_inc(s["lnT"], 1)
            pe.wait_ge(s[f"ctx{np_}"], past[f"ctx{np_}"] + 16 * n + 32 - 16 * np_)
            at_least(pe, s["KT"], n, past["KT"])
            pe.matmul(k.bank[2][:, :], k.wc, k.ctxT[np_][:, :], start=True, stop=True).then_inc(s["k"], 1)
            pe.wait_ge(s["hT"], past["hT"] + n + 1)
            at_least(pe, s["QT"], n, past["QT"])
            pe.matmul(k.bank[1][:, :], k.wc, k.hT[0][:, :], start=True, stop=True).then_inc(s["q"], 1)

        def scores(n):
            pe.wait_ge(s["KT"], past["KT"] + n + 1)
            pe.wait_ge(s["QT"], past["QT"] + n + 1)
            at_least(pe, s["shifted"], n, past["shifted"])
            for c in range(TPG):
                for b in range(2):
                    at = c * P + b * S
                    last = pe.matmul(k.bank[3][b * S:(b + 1) * S, c * S:(c + 1) * S], k.QT[0][:, at:at + S],
                                     k.KT[:, at:at + S], start=True, stop=True)
            last.then_inc(s["scores"], 1)

        def back(g, gp):
            pe.wait_ge(s["exp"], past["exp"] + g + 1)
            at_least(pe, s["PT"], g, past["PT"])
            pe_gate(pe, k)
            for c in range(TPG):
                last = pe.transpose(k.bank[4][0:S, c * P:(c + 1) * P], k.soft[gp][:, c, :], ident)
            last.then_inc(s["pT"], 1)

        def multiply(g, gp):
            pe.wait_ge(s["PT"], past["PT"] + g + 1)
            at_least(pe, s["X"], g, past["X"])
            pe_gate(pe, k)
            for c in range(TPG):
                for b in range(2):
                    at = c * P + b * S
                    last = pe.matmul(k.bank[5][b * S:(b + 1) * S, c * P:(c + 1) * P], k.PT[0][0:S, at:at + S],
                                     k.ctxN[gp][:, 2 * c + b, :], start=True, stop=True)
            last.then_inc(s["out"], 1)

        def prologue():
            front(0, 0)
            scores(0)

        def body(g, gp, first, last):
            if not last:
                front(g + 1, 1 - gp)
            back(g, gp)
            if not last:
                scores(g + 1)
            multiply(g, gp)

        run_groups(pe, prologue, body, lambda: None)

    def scalar(self, act):
        k, s, past = self.k, self.s, self.past

        def front(n):
            act.wait_ge(s["lnT"], past["lnT"] + n + 1)
            at_least(act, s["q"], n, past["q"])
            act.activation(k.hT[0][:, :], k.bank[0][:, :], ACT.Copy).then_inc(s["hT"], 1)
            act.wait_ge(s["k"], past["k"] + n + 1)
            at_least(act, s["scores"], n, past["scores"])
            act.activation(k.KT[:, :], k.bank[2][:, :], ACT.Identity, bias=k.bc[:, 0:1]).then_inc(s["KT"], 1)
            act.wait_ge(s["q"], past["q"] + n + 1)
            act.activation(k.QT[0][:, :], k.bank[1][:, :], ACT.Identity, bias=k.bc[:, 1:2],
                           scale=D ** -0.5).then_inc(s["QT"], 1)

        def exp(n, np_):
            act.wait_ge(s["shifted"], past["shifted"] + n + 1)
            act.activation(k.soft[np_][:, :, :], k.soft[np_][:, :, :], ACT.Exp).then_inc(s["exp"], 1)

        def prologue():
            front(0)
            exp(0, 0)

        def body(g, gp, first, last):
            if not last:
                front(g + 1)
            act.wait_ge(s["pT"], past["pT"] + g + 1)
            at_least(act, s["out"], g, past["out"])
            act.activation(k.PT[0][0:S, 0:GT], k.bank[4][0:S, :], ACT.Copy).then_inc(s["PT"], 1)
            if not last:
                exp(g + 1, 1 - gp)

        run_groups(act, prologue, body, lambda: None)

    def vector(self, dve):
        k, s, past = self.k, self.s, self.past

        def normalise(n):
            layer_stats(dve, k, n, s["stats"])
            dve.wait_ge(s["rstd"], past["rstd"] + n + 1)
            at_least(dve, s["lnT"], n, past["lnT"])
            for c in range(TPG):
                last = dve.tensor_scalar(k.xn[:, c, :], k.X[:, bass.ds(n * TPG + c, 1), :], k.mv[:, c, 0:1],
                                         k.rstd[:, c:c + 1], ALU.subtract, ALU.mult)
            last.then_inc(s["xn"], 1)

        def shift(n, np_):
            dve.wait_ge(s["scores"], past["scores"] + n + 1)
            soft = k.soft[np_][:, :, :]
            sc = k.bank[3][:, 0:TPG * S].rearrange("p (c n) -> p c n", c=TPG)
            mask = ATT_W(k.att_w, "mask").unsqueeze(1).broadcast_to([P, TPG, S])
            dve.tensor_tensor(soft, sc, mask, ALU.add)
            dve.drain()
            dve.tensor_reduce(k.top[:, 0:TPG], soft, AX_X, ALU.max)
            dve.drain()
            dve.tensor_tensor(soft, soft, k.top[:, 0:TPG].unsqueeze(2).broadcast_to([P, TPG, S]),
                              ALU.subtract).then_inc(s["shifted"], 1)

        def add(g, gp):
            dve.wait_ge(s["exp"], past["exp"] + g + 1)
            dve.tensor_reduce(k.rsum[:, 0:TPG], k.soft[gp][:, :, :], AX_X, ALU.add)
            dve.drain()
            dve.reciprocal(k.rsum[:, 4:8], k.rsum[:, 0:TPG])
            dve.drain()
            dve.tensor_scalar(k.rsum[:, 8:12], k.rsum[:, 4:8], k.gates[:, 2:3], None, ALU.mult)
            dve.drain()
            dve.wait_ge(s["out"], past["out"] + g + 1)
            for c in range(TPG):
                x = k.X[:, bass.ds(g * TPG + c, 1), :]
                last = dve.scalar_tensor_tensor(out=x, in0=k.bank[5][:, c * P:(c + 1) * P].unsqueeze(1),
                                                scalar=k.rsum[:, 8 + c:9 + c], in1=x, op0=ALU.mult, op1=ALU.add)
            last.then_inc(s["X"], 1)

        def prologue():
            normalise(0)
            shift(0, 0)

        def body(g, gp, first, last):
            if not last:
                normalise(g + 1)
                shift(g + 1, 1 - gp)
            add(g, gp)

        run_groups(dve, prologue, body, lambda: None)

    def gpsimd(self, pool):
        k, s, past = self.k, self.s, self.past
        layer_rstd(pool, k, 0, s, past)
        with pool.Fori(1, GROUPS) as g:
            layer_rstd(pool, k, g, s, past)

    def sync(self, sp):
        k, s, past = self.k, self.s, self.past

        def load(g, gp):
            at_least(sp, s["k"], g - 1, past["k"])
            at_least(sp, s["out"], g - 1, past["out"])
            sp.dma_start(k.ctxT[gp][:, :], k.ctxT_dram[:, bass.ds(g * GT, GT)]).then_inc(s[f"ctx{gp}"], 16)
            sp.dma_start(k.ctxN[gp][:, :, :], k.ctxN_dram[:, bass.ds(g * GB, GB), :]).then_inc(s[f"ctx{gp}"], 16)

        for g in range(GROUPS):
            load(g, g % 2)


class Route:


    def __init__(self, k, kind):
        self.k, self.kind = k, kind
        own = ("w", "wTp", "wT", "bias", "biased") if kind == "f1" else ()
        self.s, self.past = k.signals(
            {n: GROUPS for n in ("stats", "rstd", "xn", "lnT", "hT", "logits", "lg", "e", "exp") + own})
        self.E = {"f0": E0, "f1": E1, "f3": E3}[kind]
        self.gate = ATT_W(k.att_w, {"f0": "gate0", "f1": "switch", "f3": "gate3"}[kind])
        self.turned = k.bank[7] if kind == "f3" else k.bank[6]
        self.logits_at = k.bank[7][:, 0:TPG * self.E]

    def turn(self, pe, n):
        k, s, past = self.k, self.s, self.past
        pe.wait_ge(s["xn"], past["xn"] + n + 1)
        at_least(pe, s["hT"], n, past["hT"])
        if self.kind == "f3":
            at_least(pe, s["lg"], n, past["lg"])
        for c in range(TPG):
            last = pe.transpose(self.turned[:, c * P:(c + 1) * P], k.xn[:, c, :], CONST(k.const, "ident"))
        last.then_inc(s["lnT"], 1)

    def logits(self, pe, n):
        k, s, past = self.k, self.s, self.past
        pe.wait_ge(s["hT"], past["hT"] + n + 1)
        at_least(pe, s["lg"], n, past["lg"])
        if self.kind == "f1":
            at_least(pe, s["biased"], n, past["biased"])
        for c in range(TPG):
            last = pe.matmul(self.logits_at[:, c * self.E:(c + 1) * self.E], k.hT[0][:, c * P:(c + 1) * P],
                             self.gate, start=True, stop=True)
        last.then_inc(s["logits"], 1)

    def turn_weights(self, pe, n):
        k, s, past = self.k, self.s, self.past
        pe.wait_ge(s["w"], past["w"] + n + 1)
        for c in range(TPG):
            last = pe.transpose(k.bank[6][0:E1, c * P:(c + 1) * P], k.wt[:, c, :], CONST(k.const, "ident"))
        last.then_inc(s["wTp"], 1)

    def biases(self, pe, n):
        k, s, past = self.k, self.s, self.past
        pe.wait_ge(s["wT"], past["wT"] + n + 1)
        for c in range(TPG):
            last = pe.matmul(k.bank[7][:, c * P:(c + 1) * P], k.wtT[0:E1, c * P:(c + 1) * P], k.b2e[0:E1, :],
                             start=True, stop=True)
        last.then_inc(s["bias"], 1)

    def keep(self, act, n):
        k, s, past = self.k, self.s, self.past
        act.wait_ge(s["lnT"], past["lnT"] + n + 1)
        at_least(act, s["logits"], n, past["logits"])
        scale = ATT_W(k.att_w, "ln2") if self.kind == "f0" else 1.0
        fn = ACT.Identity if self.kind == "f0" else ACT.Copy
        act.activation(k.HT[:, bass.ds(n * GT, GT)], self.turned[:, :], fn, scale=scale)
        act.activation(k.hT[0][:, :], self.turned[:, :], fn, scale=scale).then_inc(s["hT"], 1)

    def exps(self, act, n):
        k, s, past = self.k, self.s, self.past
        act.wait_ge(s["e"], past["e"] + n + 1)
        width = {"f0": 2, "f1": E1, "f3": E3}[self.kind]
        act.activation(k.ex[:, :, 0:width], k.ex[:, :, 0:width], ACT.Exp).then_inc(s["exp"], 1)

    def keep_weights(self, act, n):
        k, s, past = self.k, self.s, self.past
        act.wait_ge(s["wTp"], past["wTp"] + n + 1)
        at_least(act, s["bias"], n, past["bias"])
        act.activation(k.wtT[0:E1, :], k.bank[6][0:E1, :], ACT.Copy).then_inc(s["wT"], 1)

    def statistics(self, dve, n):
        k, s = self.k, self.s
        dve.drain()
        if self.kind != "f0":
            layer_stats(dve, k, n, s["stats"])
            return
        for c in range(TPG):
            dve.bn_stats(k.bn[:, c, :], k.XH[:, bass.ds(n * TPG + c, 1), :].rearrange("p a n -> p (a n)"))
        dve.drain()
        for c in range(TPG):
            dve.bn_aggr(k.mv[:, c, :], k.bn[:, c, :])
        dve.drain()
        dve.tensor_tensor(k.veps[:, :], k.mv[:, :, 0], k.mv[:, :, 0], ALU.mult)
        dve.drain()
        dve.tensor_tensor(k.veps[:, :], k.veps[:, :], k.mv[:, :, 1], ALU.add)
        dve.drain()
        dve.tensor_scalar(k.veps[:, :], k.veps[:, :], EPS, None, ALU.add).then_inc(s["stats"], 1)

    def normalise(self, dve, n):
        k, s, past = self.k, self.s, self.past
        dve.wait_ge(s["rstd"], past["rstd"] + n + 1)
        at_least(dve, s["lnT"], n, past["lnT"])
        for c in range(TPG):
            if self.kind == "f0":
                last = dve.tensor_scalar(k.xn[:, c, :], k.XH[:, bass.ds(n * TPG + c, 1), :],
                                         k.rstd[:, c:c + 1], 0.0, ALU.mult, ALU.add)
            else:
                last = dve.tensor_scalar(k.xn[:, c, :], k.X[:, bass.ds(n * TPG + c, 1), :], k.mv[:, c, 0:1],
                                         k.rstd[:, c:c + 1], ALU.subtract, ALU.mult)
        last.then_inc(s["xn"], 1)

    def fill(self, dve):
        dve.memset(self.k.lg[:, :, :], SENT)
        dve.memset(self.k.cand[:, :, :], SENT)
        dve.drain()

    def mark(self, dve, rows, width, top, n):
        taken = self.k.taken
        dve.memset(top[:, :, n:8], SENT)
        dve.drain()
        for c in range(TPG):
            dve.match_replace(taken[:, c, 0:width], top[:, c, :], rows[:, c, 0:width], TAKEN)
        dve.drain()

    def sums(self, dve, values, weight):
        k = self.k
        dve.tensor_reduce(k.sm[:, 0:TPG], values, AX_X, ALU.add)
        dve.drain()
        if self.kind == "f3":
            dve.tensor_scalar(k.sm[:, 0:TPG], k.sm[:, 0:TPG], 1e-20, None, ALU.add)
            dve.drain()
        dve.reciprocal(k.sm[:, 4:8], k.sm[:, 0:TPG])
        dve.drain()
        if self.kind == "f3":
            dve.tensor_scalar(k.sm[:, 8:12], k.sm[:, 4:8], 0.2, weight, ALU.mult, ALU.mult)
        else:
            dve.tensor_scalar(k.sm[:, 8:12], k.sm[:, 4:8], weight, None, ALU.mult)
        dve.drain()

    def choose0(self, dve, n, step):
        k, s, past, E = self.k, self.s, self.past, self.E
        if step == 0:
            dve.drain()
            dve.wait_ge(s["logits"], past["logits"] + n + 1)
            dve.tensor_copy(k.lg[:, :, 0:E], self.logits_at.rearrange("p (c e) -> p c e", c=TPG))\
                .then_inc(s["lg"], 1)
            dve.drain()
            for c in range(TPG):
                dve.max(k.t8[:, c, :], k.lg[:, c, 0:16])
            dve.drain()
            best = k.t8[:, :, 0:1].broadcast_to([P, TPG, 2])
            dve.tensor_tensor(k.ex[:, :, 0:2], k.t8[:, :, 0:2], best, ALU.subtract).then_inc(s["e"], 1)
        elif step in (1, 2):
            dve.tensor_copy(k.m8[:, :, :], k.t8[:, :, :])
            dve.drain()
            self.mark(dve, k.lg, 16, k.m8, step)
            dve.tensor_scalar(k.pk[:, step - 1, :, 0:E], k.taken[:, :, 0:E], TAKEN, None, ALU.is_equal)
            dve.drain()
        elif step == 3:
            dve.tensor_tensor(k.pk[:, 1, :, 0:E], k.pk[:, 1, :, 0:E], k.pk[:, 0, :, 0:E], ALU.subtract)
            dve.drain()
            dve.wait_ge(s["exp"], past["exp"] + n + 1)
            self.sums(dve, k.ex[:, :, 0:2], k.gates[:, 4:5])
        elif step == 4:
            dve.tensor_tensor(k.ex[:, :, 0:2], k.ex[:, :, 0:2],
                              k.sm[:, 8:12].unsqueeze(2).broadcast_to([P, TPG, 2]), ALU.mult)
            dve.drain()
            for i in range(2):
                dve.tensor_tensor(k.pk[:, i, :, 0:E], k.pk[:, i, :, 0:E],
                                  k.ex[:, :, i:i + 1].broadcast_to([P, TPG, E]), ALU.mult)
            dve.drain()
            dve.tensor_tensor(k.route[:, bass.ds(n * TPG, TPG), 0:E], k.pk[:, 0, :, 0:E], k.pk[:, 1, :, 0:E], ALU.add)
        else:
            x, xh = (v[:, bass.ds(n * TPG, TPG), :] for v in (k.X, k.XH))
            dve.scalar_tensor_tensor(out=x, in0=xh, scalar=k.gates[:, 4:5], in1=x, op0=ALU.mult, op1=ALU.add)

    def choose1(self, dve, n, step):
        k, s, past, E = self.k, self.s, self.past, self.E
        if step == 0:
            dve.drain()
            dve.wait_ge(s["logits"], past["logits"] + n + 1)
            sb = ROWS(k.rows, "switch_b").unsqueeze(1).broadcast_to([P, TPG, E])
            dve.tensor_tensor(k.lg[:, :, 0:E], self.logits_at.rearrange("p (c e) -> p c e", c=TPG), sb,
                              ALU.add).then_inc(s["lg"], 1)
            dve.drain()
            for c in range(TPG):
                dve.max(k.t8[:, c, :], k.lg[:, c, 0:16])
            dve.drain()
            dve.tensor_tensor(k.ex[:, :, 0:E], k.lg[:, :, 0:E], k.t8[:, :, 0:1].broadcast_to([P, TPG, E]),
                              ALU.subtract).then_inc(s["e"], 1)
        elif step == 1:
            self.mark(dve, k.lg, 16, k.t8, 1)
            dve.tensor_scalar(k.pk[:, 0, :, 0:E], k.taken[:, :, 0:E], TAKEN, None, ALU.is_equal)
            dve.drain()
        elif step == 2:
            dve.wait_ge(s["exp"], past["exp"] + n + 1)
            self.sums(dve, k.ex[:, :, 0:E], k.gates[:, 5:6])
            at_least(dve, s["wTp"], n, past["wTp"])
            dve.tensor_tensor(k.wt[:, :, :], k.pk[:, 0, :, 0:E],
                              k.sm[:, 8:12].unsqueeze(2).broadcast_to([P, TPG, E]), ALU.mult).then_inc(s["w"], 1)
            dve.drain()
            dve.tensor_copy(k.route[:, bass.ds(n * TPG, TPG), 0:E], k.wt[:, :, :])
        else:
            dve.wait_ge(s["bias"], past["bias"] + n + 1)
            x = k.X[:, bass.ds(n * TPG, TPG), :]
            dve.tensor_tensor(x, k.bank[7][:, :].rearrange("p (c n) -> p c n", c=TPG), x, ALU.add)\
                .then_inc(s["biased"], 1)

    def choose3(self, dve, n, step):
        k, s, past, E = self.k, self.s, self.past, self.E
        if step == 0:
            dve.drain()
            dve.wait_ge(s["logits"], past["logits"] + n + 1)
            dve.tensor_scalar(k.ex[:, :, 0:E], self.logits_at.rearrange("p (c e) -> p c e", c=TPG), -1.0,
                              None, ALU.mult).then_inc(s["lg"], 1)
            dve.drain().then_inc(s["e"], 1)
        elif step == 1:
            dve.wait_ge(s["exp"], past["exp"] + n + 1)
            dve.tensor_scalar(k.ex[:, :, 0:E], k.ex[:, :, 0:E], 1.0, None, ALU.add)
            dve.drain()
            dve.reciprocal(k.sg[:, :, :], k.ex[:, :, 0:E])
            dve.drain()
            gb = ROWS(k.rows, "gate_bias").unsqueeze(1).broadcast_to([P, TPG, E])
            dve.tensor_tensor(k.sc[:, :, :], k.sg[:, :, :], gb, ALU.add)
            dve.drain()
        elif step in (2, 3):
            for c in range((step - 2) * 2, (step - 1) * 2):
                for q in range(G3):
                    dve.max(k.g8[:, c, q, :], k.sc[:, c, q * 8:(q + 1) * 8])
        elif step == 4:
            dve.drain()
            dve.tensor_tensor(k.lg[:, :, 0:G3], k.g8[:, :, :, 0], k.g8[:, :, :, 1], ALU.add)
            dve.drain()
            for c in range(TPG):
                dve.max(k.t8[:, c, :], k.lg[:, c, 0:16])
            dve.drain()
        elif step == 5:
            self.mark(dve, k.lg, 16, k.t8, 2)
            dve.tensor_scalar(k.gm[:, :, 0, :], k.taken[:, :, 0:G3], TAKEN, None, ALU.is_equal)
            dve.drain()
            dve.tensor_scalar(k.gm[:, :, 1, :], k.gm[:, :, 0, :], 1.0, -LOW, ALU.subtract, ALU.mult)
            dve.drain()
        elif step in (6, 7):
            for c in range(TPG):
                cand = k.cand[:, c, 0:E].rearrange("p (q e) -> p q e", q=G3)
                src = k.sc[:, c, :].rearrange("p (q e) -> p q e", q=G3) if step == 6 else cand
                dve.tensor_tensor(cand, src, k.gm[:, c, step - 6, :].unsqueeze(2).broadcast_to([P, G3, 8]),
                                  ALU.mult if step == 6 else ALU.add)
            dve.drain()
        elif step == 8:
            for c in range(TPG):
                dve.max(k.t8[:, c, :], k.cand[:, c, 0:E + 8])
            dve.drain()
        elif step == 9:
            self.mark(dve, k.cand, E + 8, k.t8, K3)
            dve.tensor_scalar(k.ex[:, :, 0:E], k.taken[:, :, 0:E], TAKEN, None, ALU.is_equal)
            dve.drain()
        elif step == 10:
            dve.tensor_tensor(k.ex[:, :, 0:E], k.ex[:, :, 0:E], k.sg[:, :, :], ALU.mult)
            dve.drain()
            self.sums(dve, k.ex[:, :, 0:E], k.gates[:, 7:8])
        elif step == 11:
            dve.tensor_tensor(k.route[:, bass.ds(n * TPG, TPG), 0:E], k.ex[:, :, 0:E],
                              k.sm[:, 8:12].unsqueeze(2).broadcast_to([P, TPG, E]), ALU.mult)
        elif step == 12:
            self.mark(dve, k.cand, E + 8, k.t8, 1)
        else:
            dve.tensor_scalar(k.ex[:, :, 0:E], k.taken[:, :, 0:E], TAKEN, k.alpha[:, 0:1], ALU.is_equal, ALU.mult)
            dve.drain()
            two = k.ex[:, :, 0:E].rearrange("p c (l u) -> p c l u", u=2)
            dve.tensor_tensor(k.anchor[:, bass.ds(n * TPG, TPG), :], two[:, :, :, 0], two[:, :, :, 1], ALU.add)
            dve.drain()

    def choose(self, dve, n, step):
        {"f0": self.choose0, "f1": self.choose1, "f3": self.choose3}[self.kind](dve, n, step)

    def first_tensor(self, pe):
        self.turn(pe, 0)
        self.logits(pe, 0)
        if self.kind == "f1":
            self.turn_weights(pe, 0)
            self.biases(pe, 0)

    def first_scalar(self, act):
        self.keep(act, 0)
        self.exps(act, 0)
        if self.kind == "f1":
            self.keep_weights(act, 0)

    def first_vector(self, dve):
        self.fill(dve)
        self.statistics(dve, 0)
        self.normalise(dve, 0)
        for step in range({"f0": 6, "f1": 4, "f3": 14}[self.kind]):
            self.choose(dve, 0, step)

    def gpsimd(self, pool):
        k, s, past = self.k, self.s, self.past
        layer_rstd(pool, k, 0, s, past)
        with pool.Fori(1, GROUPS) as g:
            layer_rstd(pool, k, g, s, past)


def run_routed(eng, body, tail):
    body(0, True, False)
    with eng.Fori(1, GROUPS - 1) as g:
        body(g, False, False)
    body(GROUPS - 1, False, True)
    tail()


class Experts:


    def __init__(self, k, kind):
        self.k, self.kind = k, kind
        self.gated = kind == "f0"
        self.NF = (F0 if self.gated else F1) // P
        self.E = E0 if self.gated else E1
        self.up_w, self.down_w = k.experts[kind]
        n = GROUPS * self.E
        self.s, self.past = k.signals({"up": n * self.NF, "act": n * self.NF, "hid": n * self.NF * self.gated,
                                       "y": n, "X": n})
        self.route = Route(k, kind)

    def tensor(self, pe):
        k, s, past, NF, E = self.k, self.s, self.past, self.NF, self.E
        r = self.route

        def up(g, e):
            i = g * E + e
            x = k.HT[:, bass.ds(g * GT, GT)]
            for f in range(NF):
                at_least(pe, s["hid"] if self.gated else s["act"], (i - 1) * NF + f + 1, (past["hid"] if self.gated else past["act"]))
                last = pe.matmul(k.bank[f][:, :], self.up_w[:, e, f * P:(f + 1) * P], x, start=True, stop=True)
                if self.gated:
                    last = pe.matmul(k.bank[2 + f][:, :], self.up_w[:, e, F0 + f * P:F0 + (f + 1) * P], x,
                                     start=True, stop=True)
                last.then_inc(s["up"], 1)

        def down(g, e):
            i = g * E + e
            pe.wait_ge(s["hid"] if self.gated else s["act"], (past["hid"] if self.gated else past["act"]) + (i + 1) * NF)
            at_least(pe, s["X"], i - 1, past["X"])
            for c in range(TPG):
                for f in range(NF):
                    last = pe.matmul(k.bank[4 + e % 2][:, c * P:(c + 1) * P], k.hid[e % 2][:, f, c * P:(c + 1) * P],
                                     self.down_w[:, e, f, :], start=(f == 0), stop=(f == NF - 1))
            last.then_inc(s["y"], 1)

        def body(g, first, last):
            for e in range(E):
                up(g, e)
                if e > 0:
                    down(g, e - 1)
                elif not first:
                    down(g - 1, E - 1)
                if not last:
                    if e == 2:
                        r.turn(pe, g + 1)
                    elif e == 3:
                        r.logits(pe, g + 1)
                    elif e == 5 and not self.gated:
                        r.turn_weights(pe, g + 1)
                    elif e == 6 and not self.gated:
                        r.biases(pe, g + 1)

        r.first_tensor(pe)
        pe.wait_ge(k.loaded[self.kind], 16 * k.parts[self.kind])
        run_routed(pe, body, lambda: down(GROUPS - 1, E - 1))

    def scalar(self, act):
        k, s, past, NF, E = self.k, self.s, self.past, self.NF, self.E
        r = self.route

        def body(g, first, last):
            for e in range(E):
                i = g * E + e
                for f in range(NF):
                    act.wait_ge(s["up"], past["up"] + i * NF + f + 1)
                    if self.gated:
                        at_least(act, s["hid"], (i - 1) * NF + f + 1, past["hid"])
                        act.activation(k.silu[:, f, :], k.bank[f][:, :], ACT.Silu).then_inc(s["act"], 1)
                    else:
                        at_least(act, s["y"], i - 1, past["y"])
                        act.activation(k.hid[e % 2][:, f, :], k.bank[f][:, :], ACT.Gelu_apprx_tanh,
                                       bias=k.b1e[:, e * NF + f:e * NF + f + 1]).then_inc(s["act"], 1)
                if not last:
                    if e == 2:
                        r.keep(act, g + 1)
                    elif e == 4:
                        r.exps(act, g + 1)
                    elif e == 5 and not self.gated:
                        r.keep_weights(act, g + 1)

        r.first_scalar(act)
        act.wait_ge(k.loaded[self.kind], 16 * k.parts[self.kind])
        run_routed(act, body, lambda: None)

    def vector(self, dve):
        k, s, past, NF, E = self.k, self.s, self.past, self.NF, self.E
        r = self.route

        def add(g, e):
            i = g * E + e
            dve.drain()
            dve.wait_ge(s["y"], past["y"] + i + 1)
            for c in range(TPG):
                x = k.X[:, bass.ds(g * TPG + c, 1), :]
                w = k.route[:, bass.ds(g * TPG + c, 1), e:e + 1].rearrange("p a e -> p (a e)")
                last = dve.scalar_tensor_tensor(out=x, in0=k.bank[4 + e % 2][:, c * P:(c + 1) * P].unsqueeze(1),
                                                scalar=w, in1=x, op0=ALU.mult, op1=ALU.add)
            last.then_inc(s["X"], 1)

        def body(g, first, last):
            for e in range(E):
                i = g * E + e
                if self.gated:
                    for f in range(NF):
                        dve.wait_ge(s["act"], past["act"] + i * NF + f + 1)
                        at_least(dve, s["y"], i - 1, past["y"])
                        dve.tensor_tensor(k.hid[e % 2][:, f, :], k.bank[2 + f][:, :], k.silu[:, f, :],
                                          ALU.mult).then_inc(s["hid"], 1)
                if e > 0:
                    add(g, e - 1)
                elif not first:
                    add(g - 1, E - 1)
                if not last:
                    if e == 0:
                        r.statistics(dve, g + 1)
                    elif e == 1:
                        r.normalise(dve, g + 1)
                    elif self.gated and e >= 4:
                        for step in ((0,), (1, 2), (3, 4), (5,))[e - 4]:
                            r.choose(dve, g + 1, step)
                    elif e >= 4:
                        for step in ((0, 1), (2,), (), (3,))[e - 4]:
                            r.choose(dve, g + 1, step)

        r.first_vector(dve)
        run_routed(dve, body, lambda: add(GROUPS - 1, E - 1))

    def gpsimd(self, pool):
        self.route.gpsimd(pool)

    def sync(self, sp):
        pass


class Choices:


    def __init__(self, k):
        self.k = k
        self.s, self.past = k.signals(
            {n: GROUPS for n in ("stats", "rstd", "xn", "lnT", "hT", "lr", "lrT")}
            | {n: TILES for n in ("logits", "mid", "eq", "ranked", "hid", "pT", "hidT", "out", "X")})

    def tensor(self, pe):
        k, s, past = self.k, self.s, self.past
        ident = CONST(k.const, "ident")

        def front(n, np_):
            pe.wait_ge(s["xn"], past["xn"] + n + 1)
            at_least(pe, s["hT"], n, past["hT"])
            for c in range(TPG):
                last = pe.transpose(k.bank[0][:, c * P:(c + 1) * P], k.xn[:, c, :], ident)
            last.then_inc(s["lnT"], 1)
            pe.wait_ge(s["hT"], past["hT"] + n + 1)
            at_least(pe, s["lrT"], n, past["lrT"])
            pe.matmul(k.bank[1][0:DL, :], k.m1, k.hT[np_][:, :], start=True, stop=True).then_inc(s["lr"], 1)

        def units(t, c, gp, g):
            pe.wait_ge(s["lrT"], past["lrT"] + g + 1)
            at_least(pe, s["hid"], t - 1 if not isinstance(t, int) else max(t - 1, 0), past["hid"])
            pe.matmul(k.bank[2 + c % 2][:, :], k.lrT[gp][:, c * P:(c + 1) * P], k.m2, start=True, stop=True)\
                .then_inc(s["logits"], 1)
            pe.matmul(k.bank[4 + c % 2][:, :], k.hT[gp][:, c * P:(c + 1) * P], k.w1c, start=True, stop=True)\
                .then_inc(s["mid"], 1)

        def turn(t, c):
            pe.wait_ge(s["hid"], past["hid"] + t + 1)
            at_least(pe, s["hidT"], t, past["hidT"])
            for f in range(4):
                last = pe.transpose(k.bank[6][:, f * P:(f + 1) * P], k.hidc[c % 2][:, f * P:(f + 1) * P], ident)
            last.then_inc(s["pT"], 1)

        def multiply(t, c):
            pe.wait_ge(s["hidT"], past["hidT"] + t + 1)
            at_least(pe, s["X"], t, past["X"])
            for f in range(4):
                last = pe.matmul(k.bank[7][:, 0:P], k.hidcT[:, f * P:(f + 1) * P], k.w2c[:, f, :], start=(f == 0),
                                 stop=(f == 3))
            last.then_inc(s["out"], 1)

        def prologue():
            front(0, 0)
            units(0, 0, 0, 0)

        def body(g, gp, first, last):
            for c in range(TPG):
                t = g * TPG + c
                if c < 3:
                    units(t + 1, c + 1, gp, g)
                elif not last:
                    units(t + 1, 0, 1 - gp, g + 1)
                turn(t, c)
                if c == 1 and not last:
                    front(g + 1, 1 - gp)
                multiply(t, c)

        pe.wait_ge(k.loaded["f2"], 16 * k.parts["f2"])
        run_groups(pe, prologue, body, lambda: None)

    def scalar(self, act):
        k, s, past = self.k, self.s, self.past

        def front(n, np_):
            act.wait_ge(s["lnT"], past["lnT"] + n + 1)
            act.activation(k.hT[np_][:, :], k.bank[0][:, :], ACT.Copy).then_inc(s["hT"], 1)
            act.wait_ge(s["lr"], past["lr"] + n + 1)
            act.activation(k.lrT[np_][0:DL, :], k.bank[1][0:DL, :], ACT.Copy).then_inc(s["lrT"], 1)

        def body(g, gp, first, last):
            for c in range(TPG):
                t = g * TPG + c
                act.wait_ge(s["pT"], past["pT"] + t + 1)
                at_least(act, s["out"], t, past["out"])
                act.activation(k.hidcT[:, :], k.bank[6][:, :], ACT.Copy).then_inc(s["hidT"], 1)
                if c == 1 and not last:
                    front(g + 1, 1 - gp)

        for lr in k.lrT:
            act.activation(lr[DL:DL + 1, :], k.onesrow[DL:DL + 1, :], ACT.Copy)
        act.drain()
        run_groups(act, lambda: front(0, 0), body, lambda: None)

    def vector(self, dve):
        k, s, past = self.k, self.s, self.past

        def normalise(n):
            layer_stats(dve, k, n, s["stats"])
            dve.wait_ge(s["rstd"], past["rstd"] + n + 1)
            at_least(dve, s["lnT"], n, past["lnT"])
            for c in range(TPG):
                last = dve.tensor_scalar(k.xn[:, c, :], k.X[:, bass.ds(n * TPG + c, 1), :], k.mv[:, c, 0:1],
                                         k.rstd[:, c:c + 1], ALU.subtract, ALU.mult)
            last.then_inc(s["xn"], 1)

        def blocks(ap):
            return ap.rearrange("p (j y) -> p j y", j=D1)

        def largest(t, c):
            dve.wait_ge(s["logits"], past["logits"] + t + 1)
            dve.tensor_reduce(k.top[:, 0:D1], blocks(k.bank[2 + c % 2][:, :]), AX_X, ALU.max)
            dve.drain()
            dve.tensor_tensor(blocks(k.eq[c % 2][:, :]), blocks(k.bank[2 + c % 2][:, :]),
                              k.top[:, 0:D1].unsqueeze(2).broadcast_to([P, D1, D2]), ALU.is_equal)
            dve.drain().then_inc(s["eq"], 1)

        def choose(t, c):
            dve.wait_ge(s["ranked"], past["ranked"] + t + 1)
            dve.tensor_reduce(k.top[:, 8:16], blocks(k.eq[c % 2][:, :]), AX_X, ALU.max)
            dve.drain()
            dve.tensor_tensor(blocks(k.eq[c % 2][:, :]), blocks(k.eq[c % 2][:, :]),
                              k.top[:, 8:16].unsqueeze(2).broadcast_to([P, D1, D2]), ALU.is_equal)
            dve.drain()
            dve.wait_ge(s["mid"], past["mid"] + t + 1)
            at_least(dve, s["pT"], t - 1 if not isinstance(t, int) else max(t - 1, 0), past["pT"])
            dve.scalar_tensor_tensor(out=k.hidc[c % 2][:, :], in0=k.bank[4 + c % 2][:, :], scalar=0.0,
                                     in1=k.eq[c % 2][:, :], op0=ALU.max, op1=ALU.mult).then_inc(s["hid"], 1)

        def add(t):
            dve.drain()
            dve.wait_ge(s["out"], past["out"] + t + 1)
            x = k.X[:, bass.ds(t, 1), :]
            dve.scalar_tensor_tensor(out=k.tmp[:, 0:P], in0=k.bank[7][:, 0:P], scalar=k.gates[:, 6:7], in1=k.b2c,
                                     op0=ALU.mult, op1=ALU.add)
            dve.drain().then_inc(s["X"], 1)
            dve.tensor_tensor(x, x, k.tmp[:, 0:P].unsqueeze(1), ALU.add)

        def prologue():
            normalise(0)
            largest(0, 0)
            choose(0, 0)

        def body(g, gp, first, last):
            for c in range(TPG):
                t = g * TPG + c
                if c < 3 or not last:
                    largest(t + 1, (c + 1) % 2)
                if c == 0 and not last:
                    normalise(g + 1)
                if c > 0 or not first:
                    add(t - 1)
                if c < 3 or not last:
                    choose(t + 1, (c + 1) % 2)

        run_groups(dve, prologue, body, lambda: add(TILES - 1))

    def gpsimd(self, pool):
        k, s, past = self.k, self.s, self.past

        def rank(t, c):
            pool.wait_ge(s["eq"], past["eq"] + t + 1)
            eq = k.eq[c % 2][:, :].rearrange("p (j y) -> p j y", j=D1)
            pool.tensor_tensor(eq, eq, CONST(k.const, "first").unsqueeze(1).broadcast_to([P, D1, D2]), ALU.mult)\
                .then_inc(s["ranked"], 1)

        def prologue():
            layer_rstd(pool, k, 0, s, past)
            rank(0, 0)

        def body(g, gp, first, last):
            for c in range(TPG):
                if c < 3 or not last:
                    rank(g * TPG + c + 1, (c + 1) % 2)
                if c == 0 and not last:
                    layer_rstd(pool, k, g + 1, s, past)

        run_groups(pool, prologue, body, lambda: None)

    def sync(self, sp):
        pass


class Mixture:

    CHUNKS = 6

    def __init__(self, k):
        self.k = k
        self.s, self.past = k.signals(
            {n: TILES * self.CHUNKS for n in ("up", "silu", "hid", "pT", "hidT", "out")} | {"x": TILES, "X": TILES})
        self.route = Route(k, "f3")
        self.chunks = [(k.w3g[:, n * 512:(n + 1) * 512], k.w3u[:, n * 512:(n + 1) * 512],
                        k.w3d[:, 4 * n:4 * n + 4, :], 512) for n in range(5)]
        self.chunks.append((k.w3g[:, 2560:2624], k.w3u[:, 2560:2624], k.w3d[:, 20:21, :], I3))

    def tensor(self, pe):
        k, s, past = self.k, self.s, self.past
        r = self.route
        ident = CONST(k.const, "ident")

        def up(t, tp, n):
            i = t * self.CHUNKS + n
            gate, upw, _, width = self.chunks[n]
            if n == 0:
                pe.wait_ge(s["x"], past["x"] + t + 1)
            at_least(pe, s["hid"], i - 1, past["hid"])
            b = 2 * (n % 2)
            pe.matmul(k.bank[b][:, 0:width], k.hx[tp][:, :], gate, start=True, stop=True)
            pe.matmul(k.bank[b + 1][:, 0:width], k.hx[tp][:, :], upw, start=True, stop=True).then_inc(s["up"], 1)

        def turn(t, n):
            i = t * self.CHUNKS + n
            width = self.chunks[n][3]
            pe.wait_ge(s["hid"], past["hid"] + i + 1)
            at_least(pe, s["hidT"], i - 1, past["hidT"])
            for f in range(max(width // P, 1)):
                last = pe.transpose(k.bank[4 + n % 2][:, f * P:(f + 1) * P], k.hid3[n % 2][:, f * P:(f + 1) * P],
                                    ident)
            last.then_inc(s["pT"], 1)

        def down(t, n):
            i = t * self.CHUNKS + n
            width = self.chunks[n][3]
            pe.wait_ge(s["hidT"], past["hidT"] + i + 1)
            if n == 0:
                at_least(pe, s["X"], t, past["X"])
            for f in range(max(width // P, 1)):
                w = min(width, P)
                last = pe.matmul(k.bank[6][:, 0:P], k.hid3T[n % 2][0:w, f * P:(f + 1) * P],
                                 self.chunks[n][2][0:w, f, :], start=(n == 0 and f == 0),
                                 stop=(n == self.CHUNKS - 1))
            last.then_inc(s["out"], 1)

        def body(g, first, last):
            for u in range(TPG * self.CHUNKS):
                t, n = g * TPG + u // self.CHUNKS, u % self.CHUNKS
                up(t, u // self.CHUNKS % 2, n)
                if u >= 1:
                    turn(g * TPG + (u - 1) // self.CHUNKS, (u - 1) % self.CHUNKS)
                elif not first:
                    turn(g * TPG - 1, self.CHUNKS - 1)
                if u >= 2:
                    down(g * TPG + (u - 2) // self.CHUNKS, (u - 2) % self.CHUNKS)
                elif not first:
                    down(g * TPG - 1, self.CHUNKS - 2 + u)
                if u == 4 and not last:
                    r.turn(pe, g + 1)
                elif u == 6 and not last:
                    r.logits(pe, g + 1)

        def tail():
            turn(TILES - 1, self.CHUNKS - 1)
            down(TILES - 1, self.CHUNKS - 2)
            down(TILES - 1, self.CHUNKS - 1)

        r.first_tensor(pe)
        pe.wait_ge(k.loaded["f3"], 16 * k.parts["f3"])
        run_routed(pe, body, tail)

    def scalar(self, act):
        k, s, past = self.k, self.s, self.past
        r = self.route

        def silu(t, n):
            i = t * self.CHUNKS + n
            width = self.chunks[n][3]
            act.wait_ge(s["up"], past["up"] + i + 1)
            at_least(act, s["hid"], i - 1, past["hid"])
            act.activation(k.silu3[n % 2][:, 0:width], k.bank[2 * (n % 2)][:, 0:width], ACT.Silu)\
                .then_inc(s["silu"], 1)

        def turned(t, n):
            i = t * self.CHUNKS + n
            w = min(self.chunks[n][3], P)
            act.wait_ge(s["pT"], past["pT"] + i + 1)
            at_least(act, s["out"], i - 1, past["out"])
            cols = GT if w == P else P
            act.activation(k.hid3T[n % 2][0:w, 0:cols], k.bank[4 + n % 2][0:w, 0:cols], ACT.Copy)\
                .then_inc(s["hidT"], 1)

        def body(g, first, last):
            for u in range(TPG * self.CHUNKS):
                silu(g * TPG + u // self.CHUNKS, u % self.CHUNKS)
                if u >= 1:
                    turned(g * TPG + (u - 1) // self.CHUNKS, (u - 1) % self.CHUNKS)
                elif not first:
                    turned(g * TPG - 1, self.CHUNKS - 1)
                if u == 4 and not last:
                    r.keep(act, g + 1)
                elif u == 8 and not last:
                    r.exps(act, g + 1)

        r.first_scalar(act)
        run_routed(act, body, lambda: turned(TILES - 1, self.CHUNKS - 1))

    def vector(self, dve):
        k, s, past = self.k, self.s, self.past
        r = self.route

        def weigh(t, n):
            i = t * self.CHUNKS + n
            width = self.chunks[n][3]
            dve.wait_ge(s["up"], past["up"] + i + 1)
            up = k.bank[2 * (n % 2) + 1][:, 0:width]
            part = k.up3[n % 2][:, 0:width]
            if n < 5:
                groups, src, lo = (8, k.route, 8 * n) if n < 4 else (L3, k.anchor, 0)
                w = src[:, bass.ds(t, 1), lo:lo + groups].rearrange("p a e -> p (a e)").unsqueeze(2)\
                    .broadcast_to([P, groups, width // groups])
                shape = dict(e=groups)
                dve.tensor_tensor(part.rearrange("p (e i) -> p e i", **shape), up.rearrange("p (e i) -> p e i", **shape),
                                  w, ALU.mult)
            else:
                dve.tensor_scalar(part, up, k.gates[:, 7:8], None, ALU.mult)
            dve.drain()
            dve.wait_ge(s["silu"], past["silu"] + i + 1)
            at_least(dve, s["pT"], i - 1, past["pT"])
            dve.tensor_tensor(k.hid3[n % 2][:, 0:width], part, k.silu3[n % 2][:, 0:width], ALU.mult)\
                .then_inc(s["hid"], 1)

        def add(t):
            dve.wait_ge(s["out"], past["out"] + (t + 1) * self.CHUNKS)
            x = k.X[:, bass.ds(t, 1), :]
            dve.tensor_tensor(x, k.bank[6][:, 0:P].unsqueeze(1), x, ALU.add).then_inc(s["X"], 1)

        def take(t, tp):
            dve.tensor_scalar(k.hx[tp][:, :], k.HT[:, bass.ds(t * P, P)], 1.0, 0.0, ALU.mult, ALU.add)\
                .then_inc(s["x"], 1)

        def body(g, first, last):
            for u in range(TPG * self.CHUNKS):
                c, n = u // self.CHUNKS, u % self.CHUNKS
                t, tp = g * TPG + c, c % 2
                weigh(t, n)
                if n == 3 and not (last and c == TPG - 1):
                    if c == TPG - 1:
                        dve.wait_ge(r.s["hT"], r.past["hT"] + g + 2)
                    take(t + 1, 1 - tp)
                if n == 1 and not (first and c == 0):
                    add(t - 1)
                if not last:
                    if u == 0:
                        r.statistics(dve, g + 1)
                    elif u == 2:
                        r.normalise(dve, g + 1)
                    elif u == 7:
                        r.choose(dve, g + 1, 0)
                    elif 10 <= u < 23:
                        r.choose(dve, g + 1, u - 9)

        r.first_vector(dve)
        dve.wait_ge(r.s["hT"], r.past["hT"] + 1)
        take(0, 0)
        run_routed(dve, body, lambda: add(TILES - 1))

    def gpsimd(self, pool):
        self.route.gpsimd(pool)

    def sync(self, sp):
        pass


def build(nc, ins, out):
    with ExitStack() as ctx:
        k = Kernel(nc, ins, out, ctx)
        block = ctx.enter_context(nc.Block())

        @block.sync
        def _(sp):
            k.load(sp)
            for n, part in enumerate(k.program):
                if n:
                    sp.wait_ge(k.s_part, 4 * n)
                part.sync(sp)
                k.load_late(sp, n)
            sp.wait_ge(k.s_part, 4 * len(k.program))
            sp.dma_start(out, k.X[:, 0:TILES, :]).then_inc(k.s_out, 16)
            sp.wait_ge(k.s_out, 16)

        @block.tensor
        def _(pe):
            k.prepare_tensor(pe)
            for n, part in enumerate(k.program):
                k.enter(pe, n)
                part.tensor(pe)
                pe.drain().then_inc(k.s_part, 1)

        @block.scalar
        def _(act):
            k.prepare_scalar(act)
            for n, part in enumerate(k.program):
                k.enter(act, n)
                part.scalar(act)
                act.drain().then_inc(k.s_part, 1)

        @block.vector
        def _(dve):
            k.prepare_vector(dve)
            for n, part in enumerate(k.program):
                k.enter(dve, n)
                part.vector(dve)
                dve.drain().then_inc(k.s_part, 1)

        @block.gpsimd
        def _(pool):
            k.prepare_gpsimd(pool)
            for n, part in enumerate(k.program):
                k.enter(pool, n)
                part.gpsimd(pool)
                pool.drain().then_inc(k.s_part, 1)


def kernel_inputs(a):
    f = {n: np.asarray(v) for n, v in a.items()}
    x = f["x"].reshape(TILES, P, D).transpose(1, 0, 2)
    ctx = f["ctx_1024"].reshape(B * S, D)
    att = np.zeros((P, ATT_W.width), np.float32)

    def put(name, value):
        v = ATT_W(att, name)
        v[:] = np.asarray(value).reshape(v.shape)

    even_odd = np.arange(D).reshape(PAIRS, 2, DK).transpose(1, 0, 2).ravel()
    for n in ("wq", "wk", "wv", "wo"):
        cols = even_odd if n == "wv" else np.arange(D)
        put(f"{n}_x0", f["L0_xattn_" + n].T[:, cols])
        put(f"{n}_x1", f["L1_xattn_W" + n[1]][:, cols])
        put(f"{n}_x3", f["L3_xattn_W" + n[1]].T[:, cols])
    for n in ("bq", "bk", "bv"):
        for layer in (0, 1, 3):
            put(f"{n}_x{layer}", f[f"L{layer}_xattn_" + n])
    wqkv = f["L0_ffn_wqkv"]
    kv_rows = (np.arange(H)[:, None] // 4 * DK + np.arange(DK)[None]).ravel()
    swap = np.arange(D) // DK * DK + (np.arange(D) + DK // 2) % DK
    wq, wk, wv = wqkv[:H * DK], wqkv[H * DK:H * DK + 4 * DK][kv_rows], wqkv[H * DK + 4 * DK:][kv_rows]
    for n, w in (("wq_f0", wq), ("wqs_f0", wq[swap]), ("wk_f0", wk), ("wks_f0", wk[swap]), ("wv_f0", wv[even_odd]),
                 ("wo_f0", f["L0_ffn_wo"])):
        put(n, w.T)
    put("w1_x2", f["L2_xattn_W1"])
    put("w2t_x2", f["L2_xattn_W2"].T)
    put("b1_x2", f["L2_xattn_b1"])
    put("b2_x2", f["L2_xattn_b2"])
    put("ln1", f["L0_ffn_ln1_w"])
    put("ln2", f["L0_ffn_ln2_w"])
    put("mask", np.concatenate([f["fside_1xSxS2_0"][0]] * 2))
    put("gate0", f["L0_ffn_gate_w"].T)
    put("switch", f["L1_ffn_switch_w"])
    put("gate3", f["L3_ffn_gate_weight"].T)
    rows = np.zeros((1, ROWS.width), np.float32)
    for n, v in (("bo_x0", f["L0_xattn_bo"]), ("bo_x1", f["L1_xattn_bo"]), ("bo_x3", f["L3_xattn_bo"]),
                 ("b2_f2", f["L2_ffn_b2"]), ("g", np.concatenate([f["g_xattn"], f["g_ffn"]])),
                 ("decay", f["L0_xattn_time_decay"]), ("switch_b", f["L1_ffn_switch_b"]),
                 ("gate_bias", f["L3_ffn_gate_bias"])):
        ROWS(rows, n)[0] = v

    def down(w):
        return w.reshape(-1, P, D).transpose(1, 0, 2).reshape(P, -1)

    f0 = np.concatenate([f["L0_ffn_w13"].transpose(2, 0, 1).reshape(D, -1),
                         down(f["L0_ffn_w2"].transpose(0, 2, 1).reshape(-1, D))], 1)
    f1 = np.concatenate([f["L1_ffn_w1"].transpose(1, 0, 2).reshape(D, -1), down(f["L1_ffn_w2"].reshape(-1, D)),
                         f["L1_ffn_b1"].reshape(-1, P).T], 1)
    f2 = np.zeros((P, F2_W.width), np.float32)
    F2_W(f2, "m1")[:] = f["L2_ffn_m1"]
    F2_W(f2, "m2")[0:DL] = f["L2_ffn_m2"].reshape(DL, -1)
    F2_W(f2, "m2")[DL] = f["L2_ffn_mb"].ravel()
    F2_W(f2, "w1")[:] = f["L2_ffn_w1"].reshape(D, -1)
    F2_W(f2, "w2")[:] = down(f["L2_ffn_w2"].transpose(1, 0, 2).reshape(-1, D))
    shared_down = np.zeros((P, D), np.float32)
    shared_down[0:I3] = f["L3_ffn_shared_w_down"]

    def up3(which):
        return [f["L3_ffn_w_" + which].transpose(1, 0, 2).reshape(D, -1),
                f["L3_ffn_anchor_w_" + which].transpose(1, 0, 2).reshape(D, -1), f["L3_ffn_shared_w_" + which]]

    f3 = np.concatenate(up3("gate") + up3("up") + [down(f["L3_ffn_w_down"].reshape(-1, D)),
                                                   down(f["L3_ffn_anchor_w_down"].reshape(-1, D)), shared_down], 1)
    return {"x": x, "ctx_t": ctx.T, "ctx_n": ctx.reshape(B, S, D).transpose(1, 0, 2), "att_w": att, "rows": rows,
            "const": constants(), "f0_w": f0, "f1_w": f1, "f2_w": f2, "f3_w": f3, "b2e": f["L1_ffn_b2"]}


F2_W = Columns([("m1", DL), ("m2", D1 * D2), ("w1", D1 * D2), ("w2", D1 * D2)])
F0_COLS = E0 * 2 * F0 + E0 * F0 // P * D
F1_COLS = E1 * F1 + E1 * F1 // P * D + E1 * F1 // P
UP3 = E3 * I3 + L3 * A3 + I3
F3_COLS = 2 * UP3 + 21 * D
ATT_BUF = Columns([("probs0", H * S), ("probs1", H * S), ("PT0", H * S), ("PT1", H * S), ("Kblk0", 4 * H * S),
                   ("Kblk1", 4 * H * S), ("QT0", GT), ("QT1", GT), ("KT", GT), ("ctxT0", GT), ("ctxT1", GT),
                   ("attn0", GT), ("attn1", GT), ("aT", GT), ("soft0", TPG * S), ("soft1", TPG * S)])
X2_BUF = Columns([("skip", 4 * H * S), ("ctxN0", GB * D), ("ctxN1", GB * D)])
FFN_BUF = Columns([("HT", B * S), ("route", TILES * E3), ("anchor", TILES * L3), ("hid0", 4 * GT), ("hid1", 4 * GT),
                   ("silu", 2 * GT), ("lrT0", GT), ("lrT1", GT), ("hidc0", GT), ("hidc1", GT), ("eq0", GT), ("eq1", GT),
                   ("hidcT", GT), ("silu30", GT), ("silu31", GT), ("up30", GT), ("up31", GT), ("hid30", GT), ("hid31", GT),
                   ("hid3T0", GT), ("hid3T1", GT), ("hx0", P), ("hx1", P)])


class Kernel:

    def __init__(self, nc, ins, out, ctx):
        self.nc, self.ins, self.ctx = nc, ins, ctx
        self.named, self.given = {n: self.sem(n) for n in ("X", "aTp")}, {"X": 2, "aTp": 2}

        def sb(name, shape):
            return ctx.enter_context(nc.sbuf_tensor(name, shape, F32))

        self.X = sb("X", [P, TILES + TPG, D])
        self.att_w = sb("att_w", [P, ATT_W.width])
        self.rows = sb("rows", [P, ROWS.width])
        self.const = sb("const", [P, CONST.width])
        self.arena_a = sb("arena_a", [P, max(F0_COLS, F3_COLS)])
        self.arena_b = sb("arena_b", [P, F1_COLS])
        self.f2_w = sb("f2_w", [P, F2_W.width])
        self.b2e = sb("b2e", [E1, D])
        self.XH = self.arena_b[:, 0:(TILES + TPG) * D].rearrange("p (t n) -> p t n", t=TILES + TPG)
        vcols = GB * PAIRS * 2 * VW + S - 2 * VW
        self.Vblk = [sb(f"Vblk{i}", [P, vcols]) for i in range(2)]
        self.xn = sb("xn", [P, TPG, D])
        self.hT = [sb(f"hT{i}", [P, GT]) for i in range(2)]
        self.tmp = sb("tmp", [P, GT])
        work = sb("work", [P, max(ATT_BUF.width, FFN_BUF.width)])

        def att(name):
            return ATT_BUF(work, name)

        def ffn(name):
            return FFN_BUF(work, name)

        self.probs = [att("probs0"), att("probs1")]
        self.PT = [att("PT0"), att("PT1")]
        self.Kblk = [att(f"Kblk{i}").rearrange("p (b h n) -> p b h n", b=4, h=H) for i in range(2)]
        self.QT, self.KT = [att("QT0"), att("QT1")], att("KT")
        self.ctxT = [att("ctxT0"), att("ctxT1")]
        self.attn = [att(f"attn{i}").rearrange("p (c n) -> p c n", c=TPG) for i in range(2)]
        self.aT = att("aT")
        self.soft = [att(f"soft{i}").rearrange("p (c n) -> p c n", c=TPG) for i in range(2)]
        self.ctxN = [X2_BUF(work, f"ctxN{i}")[0:S].rearrange("p (b n) -> p b n", b=GB) for i in range(2)]
        self.HT = ffn("HT")
        self.route = ffn("route").rearrange("p (t e) -> p t e", t=TILES)
        self.anchor = ffn("anchor").rearrange("p (t e) -> p t e", t=TILES)
        self.hid = [ffn(f"hid{i}").rearrange("p (f n) -> p f n", f=4) for i in range(2)]
        self.silu = ffn("silu").rearrange("p (f n) -> p f n", f=2)
        self.lrT = [ffn("lrT0")[0:DL + 1], ffn("lrT1")[0:DL + 1]]
        self.hidc, self.eq, self.hidcT = [ffn("hidc0"), ffn("hidc1")], [ffn("eq0"), ffn("eq1")], ffn("hidcT")
        self.silu3, self.up3 = [ffn("silu30"), ffn("silu31")], [ffn("up30"), ffn("up31")]
        self.hid3, self.hid3T = [ffn("hid30"), ffn("hid31")], [ffn("hid3T0"), ffn("hid3T1")]
        self.hx = [ffn("hx0"), ffn("hx1")]

        self.bn, self.mv = sb("bn", [P, TPG, 6]), sb("mv", [P, TPG, 2])
        self.veps, self.rstd, self.rms = (sb(n, [P, TPG]) for n in ("veps", "rstd", "rms"))
        self.minus_half, self.eps = sb("minus_half", [P, TPG]), sb("eps", [P, TPG])
        self.zero, self.gate, self.alpha = sb("zero", [P, 1]), sb("gate", [P, 4]), sb("alpha", [P, 1])
        self.onesrow = sb("onesrow", [P, GT])
        self.top, self.rsum = sb("top", [P, 2 * H]), sb("rsum", [P, H])
        self.gates, self.decay, self.b2c = sb("gates", [P, 8]), sb("decay", [P, S]), sb("b2c", [P, D])[:, :]
        self.bqs = {n: sb(f"bqs_{n}", [P, 1])[:, :] for n in ("x0", "x1", "x3")}
        self.wo = {n: sb(f"wo_{n}s", [P, D])[:, :] for n in ("x0", "x1", "x3")}
        self.bo = {n: sb(f"bo_{n}s", [P, D])[:, :] for n in ("x0", "x1", "x3")}
        self.wo["f0"] = ATT_W(self.att_w, "wo_f0")
        self.decay = self.decay[:, :]
        self.wc, self.bc = sb("wc", [P, D])[:, :], sb("bc", [P, 2])
        self.lg, self.taken = sb("lg", [P, TPG, 16]), sb("taken", [P, TPG, E3 + 8])
        self.cand, self.ex = sb("cand", [P, TPG, E3 + 8]), sb("ex", [P, TPG, E3])
        self.sg, self.sc = sb("sg", [P, TPG, E3]), sb("sc", [P, TPG, E3])
        self.t8, self.m8 = sb("t8", [P, TPG, 8]), sb("m8", [P, TPG, 8])
        self.g8, self.gm = sb("g8", [P, TPG, G3, 8]), sb("gm", [P, TPG, 2, G3])
        self.pk, self.wt = sb("pk", [P, 2, TPG, 8]), sb("wt", [P, TPG, E1])
        self.wtT, self.sm = sb("wtT", [E1, GT]), sb("sm", [P, 16])

        psum = ctx.enter_context(nc.psum_tensor("psum", [P, 8, GT], F32))
        self.bank = [psum[:, i, :] for i in range(8)]
        self.scores = [psum[:, 2 * i:2 * i + 2, :].rearrange("p a (h n) -> p (a h) n", n=S) for i in range(2)]

        a, b = self.arena_a, self.arena_b
        n0, n1 = E0 * 2 * F0, E1 * F1
        self.experts = {
            "f0": (a[:, 0:n0].rearrange("p (e f) -> p e f", e=E0),
                   a[:, n0:F0_COLS].rearrange("p (e f n) -> p e f n", e=E0, n=D)),
            "f1": (b[:, 0:n1].rearrange("p (e f) -> p e f", e=E1),
                   b[:, n1:2 * n1].rearrange("p (e f n) -> p e f n", e=E1, n=D))}
        self.b1e = b[:, 2 * n1:F1_COLS]
        self.w3g, self.w3u = a[:, 0:UP3], a[:, UP3:2 * UP3]
        self.w3d = a[:, 2 * UP3:F3_COLS].rearrange("p (c n) -> p c n", n=D)
        self.m1, self.m2, self.w1c = (F2_W(self.f2_w, n) for n in ("m1", "m2", "w1"))
        self.m2 = self.m2[0:DL + 1]
        self.w2c = F2_W(self.f2_w, "w2").rearrange("p (c n) -> p c n", n=D)

        self.ctxT_dram, self.ctxN_dram = ins["ctx_t"], ins["ctx_n"]
        self.loaded = {n: self.sem(f"loaded_{n}") for n in ("small", "x", "f0", "f1", "f2", "f3")}
        self.parts = {"f0": 2, "f1": 2, "f2": 1, "f3": 2}
        self.s_part, self.s_out = self.sem("part_done"), self.sem("out_stored")
        self.s_gates, self.s_fold, self.s_consts = self.sem("gates"), self.sem("fold"), self.sem("constants")
        self.s_prepared = self.sem("prepared")
        self.program = [Attention(self, "x0"), Attention(self, "f0"), Experts(self, "f0"), Attention(self, "x1"),
                        Experts(self, "f1"), WholeAttention(self), Choices(self), Attention(self, "x3"), Mixture(self)]

    def signals(self, times):
        past = {}
        for name, n in times.items():
            if name not in self.named:
                self.named[name] = self.sem(name)
            past[name] = self.given.get(name, 0)
            self.given[name] = past[name] + n
        return {name: self.named[name] for name in times}, past

    def sem(self, name):
        return self.ctx.enter_context(self.nc.semaphore("s_" + name))

    def load(self, sp):
        i, small = self.ins, self.loaded["small"]
        sp.dma_start(self.rows[:, :], i["rows"].rearrange("a n -> (a n)").partition_broadcast(P)).then_inc(small, 16)
        sp.dma_start(self.att_w[:, :], i["att_w"]).then_inc(small, 16)
        sp.dma_start(self.const[:, :], i["const"]).then_inc(small, 16)
        sp.dma_start(self.X[:, 0:TILES, :], i["x"]).then_inc(self.loaded["x"], 16)
        sp.dma_start(self.b2e[:, :], i["b2e"]).then_inc(small, 16)

    def load_expert(self, sp, name, tile, cols):
        src = self.ins[name + "_w"]
        half = cols // 2
        for a, b in ((0, half), (half, cols)):
            sp.dma_start(tile[:, a:b], src[:, a:b]).then_inc(self.loaded[name], 16)

    def load_late(self, sp, n):
        if n == 0:
            self.load_expert(sp, "f0", self.arena_a, F0_COLS)
            sp.dma_start(self.f2_w[:, :], self.ins["f2_w"]).then_inc(self.loaded["f2"], 16)
        if n == 3:
            self.load_expert(sp, "f1", self.arena_b, F1_COLS)
            self.load_expert(sp, "f3", self.arena_a, F3_COLS)

    def enter(self, eng, n):
        if n:
            eng.wait_ge(self.s_part, 4 * n)
        else:
            eng.wait_ge(self.loaded["small"], 64)
            eng.wait_ge(self.loaded["x"], 16)
            eng.wait_ge(self.s_prepared, 2)

    def prepare_gpsimd(self, pool):
        pool.memset(self.minus_half[:, :], -0.5)
        pool.memset(self.eps[:, :], EPS)
        pool.memset(self.zero[:, :], 0.0)
        pool.memset(self.gate[:, :], 1.0)
        pool.memset(self.X[:, TILES:TILES + TPG, :], 0.0)
        pool.memset(self.onesrow[:, :], 1.0)
        for v in self.Vblk:
            pool.memset(v[:, :], 0.0)
        pool.drain()
        for v in self.Vblk:
            w = v[:, 0:GB * PAIRS * 2 * VW].rearrange("p (r x) -> p r x", r=GB * PAIRS)
            pool.memset(w[0:S, :, DK:DK + 1], 1.0)
            pool.memset(w[S:P, :, 2 * VW - 1:2 * VW], 1.0)
        pool.drain().then_inc(self.s_prepared, 1)

    def prepare_scalar(self, act):
        act.wait_ge(self.loaded["small"], 64)
        act.activation(self.gates[:, :], ROWS(self.rows, "g"), ACT.Tanh).then_inc(self.s_gates, 1)

    def prepare_tensor(self, pe):
        pe.wait_ge(self.loaded["small"], 64)
        for i, n in enumerate(("x0", "x1", "x3")):
            pe.matmul(self.bank[i][:, 0:D], ATT_W(self.att_w, f"bv_{n}").broadcast_to([P, P]),
                      ATT_W(self.att_w, f"wo_{n}"), start=True, stop=True)
        w1, w2t = ATT_W(self.att_w, "w1_x2"), ATT_W(self.att_w, "w2t_x2")
        pe.matmul(self.bank[3][:, 0:D], w1, w2t, start=True, stop=True)
        for _ in range(2):
            pe.drain().then_inc(self.named["aTp"], 1)
        pe.matmul(self.bank[4][:, 0:1], w2t, ATT_W(self.att_w, "b1_x2"), start=True, stop=True).then_inc(self.s_fold, 1)

    def prepare_vector(self, dve):
        for _ in range(2):
            dve.drain().then_inc(self.named["X"], 1)
        dve.wait_ge(self.s_gates, 1)
        dve.wait_ge(self.s_fold, 1)
        dve.memset(self.alpha[:, :], 0.1)
        dve.tensor_scalar(self.decay, CONST(self.const, "dist"), ROWS(self.rows, "decay"), None, ALU.mult)
        dve.tensor_scalar(self.b2c, ROWS(self.rows, "b2_f2"), self.gates[:, 6:7], None, ALU.mult)
        dve.tensor_copy(self.wc, self.bank[3][:, 0:D])
        dve.tensor_tensor(self.bc[:, 0:1], self.bank[4][:, 0:1], ATT_W(self.att_w, "b2_x2"), ALU.add)
        for i, (n, g) in enumerate((("x0", 0), ("x1", 1), ("x3", 3))):
            dve.tensor_scalar(self.bqs[n], ATT_W(self.att_w, f"bq_{n}"), DK ** -0.5, None, ALU.mult)
            dve.tensor_scalar(self.wo[n], ATT_W(self.att_w, f"wo_{n}"), self.gates[:, g:g + 1], None, ALU.mult)
            dve.tensor_tensor(self.bo[n], self.bank[i][:, 0:D], ROWS(self.rows, f"bo_{n}"), ALU.add)
        dve.drain()
        for n, g in (("x0", 0), ("x1", 1), ("x3", 3)):
            dve.tensor_scalar(self.bo[n], self.bo[n], self.gates[:, g:g + 1], None, ALU.mult)
        dve.tensor_scalar(self.bc[:, 1:2], self.bc[:, 0:1], D ** -0.5, None, ALU.mult)
        dve.tensor_scalar(self.alpha[:, :], self.alpha[:, :], self.gates[:, 7:8], None, ALU.mult)
        dve.drain().then_inc(self.s_prepared, 1)


def kernel(**inputs):
    import concourse.bacc as bacc
    from concourse.bass_utils import run_bass_kernel_spmd

    arrays = {n: np.ascontiguousarray(v) for n, v in kernel_inputs(inputs).items()}
    nc = bacc.Bacc("TRN2", target_bir_lowering=False, num_devices=1)
    ins = {n: nc.dram_tensor(n + "_dram", v.shape, mybir.dt.from_np(v.dtype), kind="ExternalInput").ap()
           for n, v in arrays.items()}
    out = nc.dram_tensor("out_dram", (P, TILES, D), F32, kind="ExternalOutput").ap()
    build(nc, ins, out)
    r = run_bass_kernel_spmd(nc, [{n + "_dram": v for n, v in arrays.items()}], core_ids=[0])
    return r.results[0]["out_dram"].transpose(1, 0, 2).reshape(B, S, D)
```

```python
from contextlib import ExitStack

import numpy as np
import concourse.bass as bass
from concourse import mybir

F32 = mybir.dt.float32
F32R = mybir.dt.float32r
I32 = mybir.dt.int32
ALU = mybir.AluOpType
ACT = mybir.ActivationFunctionType
AX_X = mybir.AxisListType.X

P = 128
D = 128
B, S = 64, 64
TILES = B * S // P
TPG = 4
GROUPS = TILES // TPG
GT = TPG * P
GB = GT // S
H, DK = 16, 8
PAIRS = H // 2
VW = DK + 1
EPS = 1e-5
E0, F0 = 8, 256
E1, F1 = 8, 512
D1, D2, DL = 8, 64, 64
E3, I3, G3, K3 = 32, 64, 4, 6
L3, A3 = 16, 32
CHUNKS3 = (("anchor", 0, L3, A3), ("route", 0, 7, I3), ("route", 7, 6, I3), ("route", 13, 7, I3),
           ("route", 20, 6, I3), ("route", 26, 7, I3))
SENT = -3.0e38
TAKEN = 3.0e38
HIGH = -4096
LOW = -1.0e30


class Columns:

    def __init__(self, widths):
        self.at, self.width = {}, 0
        for name, n in widths:
            self.at[name] = (self.width, self.width + n)
            self.width += n

    def __call__(self, tile, name):
        a, b = self.at[name]
        return tile[:, a:b]


ATT = ("x0", "f0", "x1", "x3")
ATT_W = Columns([(f"{w}_{k}", D) for k in ATT for w in ("wq", "wk", "wv", "wo")]
                + [("wqs_f0", D), ("wks_f0", D), ("w1_x2", D), ("w2t_x2", D)]
                + [(f"{w}_{k}", 1) for k in ("x0", "x1", "x3") for w in ("bq", "bk", "bv")]
                + [("b1_x2", 1), ("b2_x2", 1), ("ln1", 1), ("ln2", 1), ("mask", S)]
                + [("gate0", E0), ("switch", E1), ("gate3", E3)])
ROWS = Columns([("bo_x0", D), ("bo_x1", D), ("bo_x3", D), ("b2_f2", D), ("g", 8), ("decay", 1),
                ("switch_b", E1), ("gate_bias", E3)])
CONST = Columns([("ident", P), ("head", H), ("dist", S), ("causal", S), ("qcos", S), ("qsin", S),
                 ("kcos", S), ("ksin", S), ("first", D2)])


def constants():
    c = np.zeros((P, CONST.width), np.float32)
    row = np.arange(P)
    CONST(c, "ident")[:] = np.eye(P)
    CONST(c, "head")[:] = row[:, None] // DK == np.arange(H)[None]
    q, k = row[:, None] % S, np.arange(S)[None]
    CONST(c, "dist")[:] = -np.abs(q - k)
    CONST(c, "causal")[:] = np.where(k <= q, 0.0, SENT)
    freq = (1.0 / 10000.0 ** (np.arange(0, DK, 2, dtype=np.float32) / DK)).astype(np.float32)
    angle = np.arange(S, dtype=np.float32)[None] * freq[row % (DK // 2)][:, None]
    sign = np.where(row % DK < DK // 2, -1.0, 1.0)[:, None]
    CONST(c, "kcos")[:] = np.cos(angle)
    CONST(c, "ksin")[:] = np.sin(angle) * sign
    CONST(c, "qcos")[:] = np.cos(angle) * DK ** -0.5
    CONST(c, "qsin")[:] = np.sin(angle) * sign * DK ** -0.5
    CONST(c, "first")[:] = D2 - np.arange(D2)[None]
    return c


def over_heads(table):
    return table.unsqueeze(1).broadcast_to([P, H, S])


def split(dve, value, u, high, low):
    dve.tensor_scalar(u.bitcast(I32), value.bitcast(I32), HIGH, None, ALU.bitwise_and)
    dve.drain()
    dve.tensor_tensor(low, value, u, ALU.subtract)
    dve.drain()
    dve.tensor_copy(high, u)
    return dve.drain()


def product(pe, out, weights, x):
    pe.matmul(out, weights[0], x[0], start=True, stop=False)
    pe.matmul(out, weights[0], x[1], start=False, stop=False)
    return pe.matmul(out, weights[1], x[0], start=False, stop=True)


def run_groups(eng, prologue, body, tail):
    prologue()
    body(0, 0, True, False)
    with eng.Fori(0, (GROUPS - 2) // 2) as j:
        body(j * 2 + 1, 1, False, False)
        body(j * 2 + 2, 0, False, False)
    body(GROUPS - 1, (GROUPS - 1) % 2, False, True)
    tail()


class Attention:


    def __init__(self, k, kind):
        self.k, self.kind = k, kind
        self.rope = kind == "f0"
        self.table = {"x0": k.decay, "f0": CONST(k.const, "causal")}.get(kind)
        self.nq = nq = 2 if self.rope else 1
        self.s, self.past = k.signals(
            {n: GROUPS + 1 for n in ("stats", "rstd", "xn")}
            | {n: GROUPS for n in ("lnT", "hT", "aTp", "aT", "wo", "X")}
            | {n: nq * GROUPS for n in ("q", "QT", "k", "KT")} | {n: GROUPS for n in ("v", "V")}
            | {n: 2 * GROUPS for n in ("kblk0", "kblk1")}
            | {n: TILES for n in ("scores", "shifted", "exp", "pv", "attn")} | {n: 2 * TILES for n in ("pT", "PT")}
            | {n: 0 if self.rope else 8 * GROUPS for n in ("ctx0", "ctx1")})
        if self.rope:
            self.misc = {(0, "A"): "lnT", (0, "B"): "k", (0, "C"): "ks", (1, "A"): "q", (1, "B"): "qs",
                         (2, "A"): "v", (2, "B"): "aT", (3, "A"): "wo"}
        else:
            self.misc = {(0, "B"): "k", (0, "C"): "lnT", (1, "A"): "q", (1, "B"): "v", (2, "B"): "aT",
                         (3, "A"): "wo"}

    def w(self, name):
        return ATT_W(self.k.att_w, f"{name}_{self.kind}")

    def tensor(self, pe):
        k, s, past = self.k, self.s, self.past
        ident = CONST(k.const, "ident")
        misc = k.bank[7]

        def scores(t, c, gp, g):
            pe.wait_ge(s["QT"], past["QT"] + (g + 1) * self.nq)
            pe.wait_ge(s["kblk0"] if c < 2 else s["kblk1"], (past["kblk0"] if c < 2 else past["kblk1"]) + 2 * g + 2)
            if not (isinstance(t, int) and t < 2):
                pe.wait_ge(s["exp"], past["exp"] + t - 1)
            for n in range(2):
                for b in range(2):
                    at = c * P + b * S
                    last = pe.matmul(k.bank[2 * (c % 2) + n][b * S:(b + 1) * S, :],
                                     k.QT[gp][:, at:at + S],
                                     k.Kblk[c // 2][:, 2 * (c % 2) + b, n * 8:(n + 1) * 8, :],
                                     start=True, stop=True)
            last.then_inc(s["scores"], 1)

        def turn(t, c):
            pe.wait_ge(s["exp"], past["exp"] + t + 1)
            for half in range(2):
                if not (isinstance(t, int) and t < 1):
                    pe.wait_ge(s["PT"], past["PT"] + 2 * t - 1 + half)
                for p in range(4):
                    at = (half * 4 + p) * P
                    last = pe.transpose(k.bank[4 + half][:, p * P:(p + 1) * P],
                                        k.probs[c % 2][:, at:at + P], ident)
                last.then_inc(s["pT"], 1)

        def values(t, c, gp, g):
            pe.wait_ge(s["PT"], past["PT"] + 2 * t + 2)
            pe.wait_ge(s["V"], past["V"] + g + 1)
            if not (isinstance(t, int) and t < 1):
                pe.wait_ge(s["attn"], past["attn"] + t)
            for p in range(PAIRS):
                for b in range(2):
                    at = (2 * c + b) * PAIRS * 2 * VW + p * 2 * VW
                    last = pe.matmul(k.bank[6][b * S:(b + 1) * S, p * S:(p + 1) * S],
                                     k.PT[c % 2][:, p * P + b * S:p * P + (b + 1) * S],
                                     k.Vblk[gp][:, at:at + S], start=True, stop=True)
            last.then_inc(s["pv"], 1)

        def project(what, n, np_, first):
            if what == ("lnT" if self.rope else "k"):
                if first != "prologue":
                    pe.wait_ge(s["V"], past["V"] + n)
                if first is False:
                    pe.wait_ge(s["X"], past["X"] + n - 2)
            if what == "lnT":
                pe.wait_ge(s["xn"], past["xn"] + n + 1)
                if not self.rope:
                    pe.wait_ge(s["KT"], past["KT"] + n + 1)
                for c in range(TPG):
                    last = pe.transpose(misc[:, c * P:(c + 1) * P], k.xn[:, c, :], ident)
                last.then_inc(s["lnT"], 1)
            elif what in ("q", "qs"):
                if what == "qs":
                    pe.wait_ge(s["QT"], past["QT"] + 2 * n + 1)
                elif self.rope:
                    pe.wait_ge(s["KT"], past["KT"] + 2 * n + 2)
                else:
                    pe.wait_ge(s["hT"], past["hT"] + n + 1)
                w = self.w("wq") if what == "q" else self.w("wqs")
                pe.matmul(misc[:, :], w, k.hT[np_][:, :], start=True, stop=True).then_inc(s["q"], 1)
            elif what in ("k", "ks"):
                if not self.rope:
                    pe.wait_ge(s[f"ctx{np_}"], past[f"ctx{np_}"] + 8 * n + 16 - 8 * np_)
                elif what == "k":
                    pe.wait_ge(s["hT"], past["hT"] + n + 1)
                else:
                    pe.wait_ge(s["KT"], past["KT"] + 2 * n + 1)
                w = self.w("wk") if what == "k" else self.w("wks")
                src = k.hT[np_] if self.rope else k.ctxT[np_]
                pe.matmul(misc[:, :], w, src[:, :], start=True, stop=True).then_inc(s["k"], 1)
            elif what == "v":
                pe.wait_ge(s["QT"], past["QT"] + (n + 1) * self.nq)
                src = k.hT[np_] if self.rope else k.ctxT[np_]
                for b in range(GB):
                    for up in range(2):
                        last = pe.matmul(misc[up * S:(up + 1) * S, b * S:(b + 1) * S], src[:, b * S:(b + 1) * S],
                                         self.w("wv")[:, up * S:(up + 1) * S], start=True, stop=True)
                last.then_inc(s["v"], 1)

        def output(what, p, pp, before):
            if what == "aT":
                pe.wait_ge(s["attn"], past["attn"] + TPG * (p + 1))
                pe.wait_ge(*before)
                for c in range(TPG):
                    last = pe.transpose(misc[:, c * P:(c + 1) * P], k.attn[pp][:, c, :], ident)
                last.then_inc(s["aTp"], 1)
            else:
                pe.wait_ge(s["aT"], past["aT"] + p + 1)
                for c in range(TPG):
                    last = pe.matmul(misc[:, c * P:(c + 1) * P], k.aT[:, c * P:(c + 1) * P],
                                     k.wo[self.kind], start=True, stop=True)
                last.then_inc(s["wo"], 1)

        def place(c, where, g, gp, first, last):
            what = self.misc.get((c, where))
            if what in ("aT", "wo"):
                if not first:
                    before = (s["X"], past["X"] + g - 1) if last else (s["V"], past["V"] + g + 2)
                    output(what, g - 1, 1 - gp, before)
            elif what and not last:
                project(what, g + 1, 1 - gp, first)

        def prologue():
            for what in ("lnT", "k", "ks", "q", "qs") if self.rope else ("k", "lnT", "q"):
                project(what, 0, 0, "prologue")
            scores(0, 0, 0, 0)
            scores(1, 1, 0, 0)
            project("v", 0, 0, "prologue")

        def body(g, gp, first, last):
            for c in range(TPG):
                t = g * TPG + c
                if c < 2:
                    scores(t + 2, c + 2, gp, g)
                elif not last:
                    scores(t + 2, c - 2, 1 - gp, g + 1)
                place(c, "A", g, gp, first, last)
                turn(t, c)
                place(c, "B", g, gp, first, last)
                if c > 0:
                    values(t - 1, c - 1, gp, g)
                elif not first:
                    values(t - 1, 3, 1 - gp, g - 1)
                place(c, "C", g, gp, first, last)

        def tail():
            values(TILES - 1, 3, (GROUPS - 1) % 2, GROUPS - 1)
            output("aT", GROUPS - 1, (GROUPS - 1) % 2, (s["X"], past["X"] + GROUPS - 1))
            output("wo", GROUPS - 1, (GROUPS - 1) % 2, None)

        run_groups(pe, prologue, body, tail)

    def scalar(self, act):
        k, s, past = self.k, self.s, self.past
        misc = k.bank[7]

        def evacuate(what, n, np_):
            if what == "lnT":
                act.wait_ge(s["lnT"], past["lnT"] + n + 1)
                act.activation(k.hT[np_][:, :], misc[:, :], ACT.Copy if not self.rope else ACT.Identity,
                               scale=1.0 if not self.rope else ATT_W(k.att_w, "ln1")).then_inc(s["hT"], 1)
            elif what == "q" and not self.rope:
                act.wait_ge(s["q"], past["q"] + n + 1)
                act.activation(k.QT[np_][:, :], misc[:, :], ACT.Identity, bias=k.bqs[self.kind],
                               scale=DK ** -0.5).then_inc(s["QT"], 1)
            elif what == "k" and not self.rope:
                act.wait_ge(s["k"], past["k"] + n + 1)
                if not (isinstance(n, int) and n < 1):
                    act.wait_ge(s["kblk0"], past["kblk0"] + 2 * n)
                    act.wait_ge(s["kblk1"], past["kblk1"] + 2 * n)
                act.activation(k.KT[:, :], misc[:, :], ACT.Identity, bias=self.w("bk")).then_inc(s["KT"], 1)
            elif what == "v":
                act.wait_ge(s["v"], past["v"] + n + 1)
                dst = k.Vblk[np_][:, 0:GB * PAIRS * 2 * VW].rearrange("p (b r x) -> p b r x", b=GB, r=PAIRS)
                src = misc[:, :].rearrange("p (b r x) -> p b r x", b=GB, r=PAIRS)
                for up in range(2):
                    last = act.activation(dst[up * S:(up + 1) * S, :, :, up * VW:up * VW + DK],
                                          src[up * S:(up + 1) * S], ACT.Copy)
                last.then_inc(s["V"], 1)

        def turned(t, c):
            for half in range(2):
                act.wait_ge(s["pT"], past["pT"] + 2 * t + 1 + half)
                if not (isinstance(t, int) and t < 2):
                    act.wait_ge(s["pv"], past["pv"] + t - 1)
                act.activation(k.PT[c % 2][:, half * GT:(half + 1) * GT], k.bank[4 + half][:, :],
                               ACT.Copy).then_inc(s["PT"], 1)

        def exp(t, c):
            act.wait_ge(s["shifted"], past["shifted"] + t + 1)
            if not (isinstance(t, int) and t < 2):
                act.wait_ge(s["pT"], past["pT"] + 2 * (t - 1))
            act.activation(k.probs[c % 2][:, :].rearrange("p (h n) -> p h n", h=H), k.scores[c % 2],
                           ACT.Exp).then_inc(s["exp"], 1)

        def block_keys(g, half, heads):
            act.wait_ge(s["KT"], past["KT"] + (g + 1) * self.nq)
            if not (isinstance(g, int) and g < 1):
                act.wait_ge(s["scores"], past["scores"] + TPG * g - 2 + 2 * half)
            src = k.KT[:, half * GT // 2:(half + 1) * GT // 2].rearrange("p (b n) -> p b n", b=4)
            for h in heads:
                last = act.activation(k.Kblk[half][:, :, h, :], src, ACT.Copy,
                                      scale=CONST(k.const, "head")[:, h:h + 1])
            if heads[-1] == H - 1:
                last.then_inc(s["kblk1"] if half else s["kblk0"], 1)

        def output(p, before=None):
            act.wait_ge(s["aTp"], past["aTp"] + p + 1)
            if not (isinstance(p, int) and p < 1):
                act.wait_ge(s["wo"], past["wo"] + p)
            act.activation(k.aT[:, :], misc[:, :], ACT.Copy).then_inc(s["aT"], 1)

        def place(c, where, g, gp, first, last):
            what = self.misc.get((c, where))
            if what == "aT":
                if not first:
                    output(g - 1)
            elif what not in (None, "wo") and not last:
                evacuate(what, g + 1, 1 - gp)

        def prologue():
            for what in ("lnT",) if self.rope else ("k", "lnT", "q"):
                evacuate(what, 0, 0)
            block_keys(0, 1, range(8, H))
            exp(0, 0)
            evacuate("v", 0, 0)
            exp(1, 1)

        def body(g, gp, first, last):
            for c in range(TPG):
                t = g * TPG + c
                place(c, "A", g, gp, first, last)
                turned(t, c)
                if c == 1 and self.rope and not last:
                    block_keys(g + 1, 0, range(12, H))
                    block_keys(g + 1, 1, range(8, H))
                elif c in (1, 2) and not self.rope and not last:
                    block_keys(g + 1, 1, range(4 + 4 * c, 8 + 4 * c))
                place(c, "B", g, gp, first, last)
                if c < 2 or not last:
                    exp(t + 2, c % 2)
                place(c, "C", g, gp, first, last)
                if c == 0 and self.rope and not last:
                    block_keys(g + 1, 0, range(8, 12))

        def tail():
            output(GROUPS - 1)

        run_groups(act, prologue, body, tail)

    def vector(self, dve):
        k, s, past = self.k, self.s, self.past
        misc = k.bank[7]

        def stats(n):
            layer_stats(dve, k, n, s["stats"])

        def normalise(n):
            dve.wait_ge(s["rstd"], past["rstd"] + n + 1)
            if not (isinstance(n, int) and n < 1):
                dve.wait_ge(s["lnT"], past["lnT"] + n)
            for c in range(TPG):
                x = k.X[:, bass.ds(n * TPG + c, 1), :]
                dst = k.XH[:, bass.ds(n * TPG + c, 1), :] if self.rope else k.xn[:, c, :]
                last = dve.tensor_scalar(dst, x, k.mv[:, c, 0:1], k.rstd[:, c:c + 1], ALU.subtract, ALU.mult)
            if self.rope:
                dve.drain()
                for c in range(TPG):
                    last = dve.tensor_scalar(k.xn[:, c, :], k.XH[:, bass.ds(n * TPG + c, 1), :],
                                             k.rms[:, c:c + 1], 0.0, ALU.mult, ALU.add)
            last.then_inc(s["xn"], 1)

        def shift(t, c):
            dve.wait_ge(s["scores"], past["scores"] + t + 1)
            sc = k.scores[c % 2]
            if self.table is not None:
                dve.tensor_tensor(sc, sc, over_heads(self.table), ALU.add)
                dve.drain()
            top = k.top[:, c % 2 * H:(c % 2 + 1) * H]
            dve.tensor_reduce(top, sc, AX_X, ALU.max)
            dve.drain()
            dve.tensor_tensor(sc, sc, top.unsqueeze(2).broadcast_to([P, H, S]),
                              ALU.subtract).then_inc(s["shifted"], 1)

        def divide(t, c, gp, g):
            dve.wait_ge(s["pv"], past["pv"] + t + 1)
            if not (isinstance(g, int) and g < 2):
                dve.wait_ge(s["aTp"], past["aTp"] + g - 1)
            pv = k.bank[6][:, :].rearrange("p (r x) -> p r x", r=PAIRS)[:, :, 0:2 * VW]\
                .rearrange("p r (u x) -> p r u x", u=2)
            dve.reciprocal(k.rsum[:, :], pv[:, :, :, DK])
            dve.drain()
            dve.tensor_tensor(k.attn[gp][:, c, :].rearrange("p (h x) -> p h x", h=H).rearrange("p (r u) x -> p r u x", u=2),
                              pv[:, :, :, 0:DK],
                              k.rsum[:, :].rearrange("p (r u) -> p r u", u=2).unsqueeze(3)
                              .broadcast_to([P, PAIRS, 2, DK]), ALU.mult).then_inc(s["attn"], 1)

        def rotate(what, n, np_):
            which = what[0]
            done, ready = which, which.upper() + "T"
            dst = (k.QT[np_] if which == "q" else k.KT)[:, :].rearrange("p (b n) -> p b n", b=GB)
            src = misc[:, :].rearrange("p (b n) -> p b n", b=GB)
            second = len(what) == 2
            dve.wait_ge(s[done], past[done] + 2 * n + 1 + second)
            if which == "k" and not second and not (isinstance(n, int) and n < 1):
                dve.wait_ge(s["kblk0"], past["kblk0"] + 2 * n)
                dve.wait_ge(s["kblk1"], past["kblk1"] + 2 * n)
            trig = CONST(k.const, which + ("sin" if second else "cos")).unsqueeze(1).broadcast_to([P, GB, S])
            if not second:
                dve.tensor_tensor(dst, src, trig, ALU.mult).then_inc(s[ready], 1)
            else:
                part = k.tmp[:, :].rearrange("p (b n) -> p b n", b=GB)
                dve.tensor_tensor(part, src, trig, ALU.mult)
                dve.drain()
                dve.tensor_tensor(dst, dst, part, ALU.add).then_inc(s[ready], 1)

        def block_keys(n, heads):
            dve.wait_ge(s["KT"], past["KT"] + (n + 1) * self.nq)
            if not (isinstance(n, int) and n < 1):
                dve.wait_ge(s["scores"], past["scores"] + TPG * n - 2)
            if self.rope:
                dve.drain()
            src = k.KT[:, 0:GT // 2].rearrange("p (b n) -> p b n", b=4)
            for h in heads:
                last = dve.tensor_scalar(k.Kblk[0][:, :, h, :], src, CONST(k.const, "head")[:, h:h + 1], 0.0,
                                         ALU.mult, ALU.add)
            if heads[-1] == H - 1:
                last.then_inc(s["kblk0"], 2 if len(heads) == H else 1)

        def residual(p):
            dve.wait_ge(s["wo"], past["wo"] + p + 1)
            prod = misc[:, :].rearrange("p (c n) -> p c n", c=TPG)
            if self.rope:
                xh = k.XH[:, bass.ds(p * TPG, TPG), :]
                dve.tensor_tensor(xh, prod, xh, ALU.add).then_inc(s["X"], 1)
            else:
                x = k.X[:, bass.ds(p * TPG, TPG), :]
                tmp = k.tmp[:, :].rearrange("p (c n) -> p c n", c=TPG)
                dve.tensor_tensor(tmp, prod, k.bo[self.kind].unsqueeze(1).broadcast_to([P, TPG, D]), ALU.add)
                dve.drain()
                dve.tensor_tensor(x, x, tmp, ALU.add).then_inc(s["X"], 1)

        def place(c, where, g, gp, last):
            what = self.misc.get((c, where))
            if self.rope and what in ("q", "qs", "k", "ks") and not last:
                rotate(what, g + 1, 1 - gp)

        def prologue():
            stats(0)
            normalise(0)
            if self.rope:
                for what in ("k", "ks", "q", "qs"):
                    rotate(what, 0, 0)
            block_keys(0, range(8, H) if self.rope else range(H))
            shift(0, 0)
            if not self.rope:
                shift(1, 1)
            stats(1)
            normalise(1)
            if self.rope:
                shift(1, 1)

        def body(g, gp, first, last):
            for c in range(TPG):
                t = g * TPG + c
                place(c, "A", g, gp, last)
                if self.rope and c == 1:
                    place(c, "B", g, gp, last)
                    shift(t + 2, c % 2)
                else:
                    if c < 2 or not last:
                        shift(t + 2, c % 2)
                    if c == 1 and not last:
                        block_keys(g + 1, range(12, H))
                    place(c, "B", g, gp, last)
                if c > 0:
                    divide(t - 1, c - 1, gp, g)
                elif not first:
                    divide(t - 1, 3, 1 - gp, g - 1)
                place(c, "C", g, gp, last)
                if c == 0 and not last and not self.rope:
                    block_keys(g + 1, range(8, 12))
                if c == 3 and not first:
                    residual(g - 1)
                if c == 1 and not last:
                    stats(g + 2)
                if c == 2 and not last:
                    normalise(g + 2)

        def tail():
            divide(TILES - 1, 3, (GROUPS - 1) % 2, GROUPS - 1)
            residual(GROUPS - 1)

        run_groups(dve, prologue, body, tail)

    def gpsimd(self, pool):
        k, s, past = self.k, self.s, self.past

        def block_keys(g):
            pool.wait_ge(s["KT"], past["KT"] + (g + 1) * self.nq)
            for half, done in enumerate((s["kblk0"], s["kblk1"])):
                if half == 0 and isinstance(g, int) and g == 0 and not self.rope:
                    continue
                if not (isinstance(g, int) and g < 1):
                    pool.wait_ge(s["scores"], past["scores"] + TPG * g - 2 + 2 * half)
                spot = 0 if half == 0 else 3
                pool.tensor_tensor(k.gate[:, spot:spot + 1], k.gate[:, 2:3], k.gate[:, 2:3], ALU.mult)
                src = k.KT[:, half * GT // 2:(half + 1) * GT // 2].rearrange("p (b n) -> p b n", b=4)
                for h in range(8):
                    last = pool.tensor_scalar(k.Kblk[half][:, :, h, :], src, CONST(k.const, "head")[:, h:h + 1],
                                              k.zero[:, 0:1], ALU.mult, ALU.add)
                last.then_inc(done, 1)

        def prologue():
            layer_rstd(pool, k, 0, s, past, self.rope)
            block_keys(0)
            layer_rstd(pool, k, 1, s, past, self.rope)

        def body(g, gp, first, last):
            if not last:
                block_keys(g + 1)
                layer_rstd(pool, k, g + 2, s, past, self.rope)

        run_groups(pool, prologue, body, lambda: None)

    def sync(self, sp):
        k, s, past = self.k, self.s, self.past
        if self.rope:
            return

        def load(g, gp):
            if g >= 2:
                sp.wait_ge(s["v"], past["v"] + g - 1)
            sp.dma_start(k.ctxT[gp][:, :], k.ctxT_dram[:, bass.ds(g * GT, GT)]).then_inc(s[f"ctx{gp}"], 16)

        for g in range(GROUPS):
            load(g, g % 2)


def layer_stats(dve, k, n, done):
    for c in range(TPG):
        dve.bn_stats(k.bn[:, c, :], k.X[:, bass.ds(n * TPG + c, 1), :].rearrange("p a n -> p (a n)"))
    dve.drain()
    for c in range(TPG):
        dve.bn_aggr(k.mv[:, c, :], k.bn[:, c, :])
    dve.drain()
    dve.tensor_scalar(k.veps[:, :], k.mv[:, :, 1], EPS, None, ALU.add).then_inc(done, 1)


def layer_rstd(pool, k, n, s, past, rms=False):
    pool.wait_ge(s["stats"], past["stats"] + n + 1)
    last = pool.tensor_tensor(k.rstd[:, :], k.veps[:, :], k.minus_half[:, 0:TPG], ALU.pow)
    if rms:
        pool.drain()
        pool.tensor_tensor(k.rms[:, :], k.mv[:, :, 1], k.rstd[:, :], ALU.mult)
        pool.drain()
        pool.tensor_tensor(k.rms[:, :], k.rms[:, :], k.rstd[:, :], ALU.mult)
        pool.drain()
        pool.tensor_tensor(k.rms[:, :], k.rms[:, :], k.eps[:, 0:TPG], ALU.add)
        pool.drain()
        last = pool.tensor_tensor(k.rms[:, :], k.rms[:, :], k.minus_half[:, 0:TPG], ALU.pow)
    last.then_inc(s["rstd"], 1)


def run_loop(eng, count, body, tail):
    body(0, True)
    with eng.Fori(1, count) as j:
        body(j, False)
    tail()


def pe_gate(pe, k):
    pe.matmul(k.bank[7][0:1, GT - 1:GT], CONST(k.const, "ident")[:, 0:1], CONST(k.const, "ident")[:, 0:1],
              start=True, stop=True)


def at_least(eng, sem, value, base):
    if not (isinstance(value, int) and value < 1):
        eng.wait_ge(sem, base + value)


class WholeAttention:


    def __init__(self, k):
        self.k = k
        self.s, self.past = k.signals(
            {n: GROUPS + 1 for n in ("stats", "rstd", "xn")}
            | {n: GROUPS for n in ("lnT", "hT", "q", "QT", "k", "KT", "scores", "shifted", "exp",
                                 "pT", "PT", "out", "X")} | {n: 8 * GROUPS for n in ("ctx0", "ctx1", "values0",
                                                                                  "values1")})

    def tensor(self, pe):
        k, s, past = self.k, self.s, self.past
        ident = CONST(k.const, "ident")

        def front(n, np_):
            pe.wait_ge(s["xn"], past["xn"] + n + 1)
            at_least(pe, s["hT"], n, past["hT"])
            for c in range(TPG):
                last = pe.transpose(k.bank[0][:, c * P:(c + 1) * P], k.xn[:, c, :], ident)
            last.then_inc(s["lnT"], 1)
            pe.wait_ge(s[f"ctx{np_}"], past[f"ctx{np_}"] + 8 * n + 16 - 8 * np_)
            at_least(pe, s["KT"], n, past["KT"])
            pe.matmul(k.bank[2][:, :], k.wc, k.ctxT[np_][:, :], start=True, stop=True).then_inc(s["k"], 1)
            pe.wait_ge(s["hT"], past["hT"] + n + 1)
            at_least(pe, s["QT"], n, past["QT"])
            pe.matmul(k.bank[1][:, :], k.wc, k.hT[0][:, :], start=True, stop=True).then_inc(s["q"], 1)

        def scores(n):
            pe.wait_ge(s["KT"], past["KT"] + n + 1)
            pe.wait_ge(s["QT"], past["QT"] + n + 1)
            at_least(pe, s["shifted"], n, past["shifted"])
            for c in range(TPG):
                for b in range(2):
                    at = c * P + b * S
                    last = pe.matmul(k.bank[3][b * S:(b + 1) * S, c * S:(c + 1) * S], k.QT[0][:, at:at + S],
                                     k.KT[:, at:at + S], start=True, stop=True)
            last.then_inc(s["scores"], 1)

        def back(g, gp):
            pe.wait_ge(s["exp"], past["exp"] + g + 1)
            at_least(pe, s["PT"], g, past["PT"])
            pe_gate(pe, k)
            for c in range(TPG):
                last = pe.transpose(k.bank[4][0:S, c * P:(c + 1) * P], k.soft[gp][:, c, :], ident)
            last.then_inc(s["pT"], 1)

        def multiply(g, gp):
            pe.wait_ge(s["PT"], past["PT"] + g + 1)
            pe.wait_ge(s[f"values{gp}"], past[f"values{gp}"] + 8 * g + 16 - 8 * gp)
            at_least(pe, s["X"], g, past["X"])
            pe_gate(pe, k)
            for c in range(TPG):
                for b in range(2):
                    at = c * P + b * S
                    last = pe.matmul(k.bank[5][b * S:(b + 1) * S, c * P:(c + 1) * P], k.PT[0][0:S, at:at + S],
                                     k.ctxN[gp][:, 2 * c + b, :], start=True, stop=True)
            last.then_inc(s["out"], 1)

        def prologue():
            front(0, 0)
            scores(0)

        def body(g, gp, first, last):
            if not last:
                front(g + 1, 1 - gp)
            back(g, gp)
            if not last:
                scores(g + 1)
            multiply(g, gp)

        run_groups(pe, prologue, body, lambda: None)

    def scalar(self, act):
        k, s, past = self.k, self.s, self.past

        def front(n):
            act.wait_ge(s["lnT"], past["lnT"] + n + 1)
            at_least(act, s["q"], n, past["q"])
            act.activation(k.hT[0][:, :], k.bank[0][:, :], ACT.Copy).then_inc(s["hT"], 1)
            act.wait_ge(s["k"], past["k"] + n + 1)
            at_least(act, s["scores"], n, past["scores"])
            act.activation(k.KT[:, :], k.bank[2][:, :], ACT.Identity, bias=k.bc[:, 0:1]).then_inc(s["KT"], 1)
            act.wait_ge(s["q"], past["q"] + n + 1)
            act.activation(k.QT[0][:, :], k.bank[1][:, :], ACT.Identity, bias=k.bc[:, 1:2],
                           scale=D ** -0.5).then_inc(s["QT"], 1)

        def exp(n, np_):
            act.wait_ge(s["shifted"], past["shifted"] + n + 1)
            act.activation(k.soft[np_][:, :, :], k.soft[np_][:, :, :], ACT.Exp).then_inc(s["exp"], 1)

        def prologue():
            front(0)
            exp(0, 0)

        def body(g, gp, first, last):
            if not last:
                front(g + 1)
            act.wait_ge(s["pT"], past["pT"] + g + 1)
            at_least(act, s["out"], g, past["out"])
            act.activation(k.PT[0][0:S, 0:GT], k.bank[4][0:S, :], ACT.Copy).then_inc(s["PT"], 1)
            if not last:
                exp(g + 1, 1 - gp)

        run_groups(act, prologue, body, lambda: None)

    def vector(self, dve):
        k, s, past = self.k, self.s, self.past

        def normalise(n):
            layer_stats(dve, k, n, s["stats"])
            dve.wait_ge(s["rstd"], past["rstd"] + n + 1)
            at_least(dve, s["lnT"], n, past["lnT"])
            for c in range(TPG):
                last = dve.tensor_scalar(k.xn[:, c, :], k.X[:, bass.ds(n * TPG + c, 1), :], k.mv[:, c, 0:1],
                                         k.rstd[:, c:c + 1], ALU.subtract, ALU.mult)
            last.then_inc(s["xn"], 1)

        def shift(n, np_):
            dve.wait_ge(s["scores"], past["scores"] + n + 1)
            soft = k.soft[np_][:, :, :]
            sc = k.bank[3][:, 0:TPG * S].rearrange("p (c n) -> p c n", c=TPG)
            mask = ATT_W(k.att_w, "mask").unsqueeze(1).broadcast_to([P, TPG, S])
            dve.tensor_tensor(soft, sc, mask, ALU.add)
            dve.drain()
            dve.tensor_reduce(k.top[:, 0:TPG], soft, AX_X, ALU.max)
            dve.drain()
            dve.tensor_tensor(soft, soft, k.top[:, 0:TPG].unsqueeze(2).broadcast_to([P, TPG, S]),
                              ALU.subtract).then_inc(s["shifted"], 1)

        def add(g, gp):
            dve.wait_ge(s["exp"], past["exp"] + g + 1)
            dve.tensor_reduce(k.rsum[:, 0:TPG], k.soft[gp][:, :, :], AX_X, ALU.add)
            dve.drain()
            dve.reciprocal(k.rsum[:, 4:8], k.rsum[:, 0:TPG])
            dve.drain()
            dve.tensor_scalar(k.rsum[:, 8:12], k.rsum[:, 4:8], k.gates[:, 2:3], None, ALU.mult)
            dve.drain()
            dve.wait_ge(s["out"], past["out"] + g + 1)
            for c in range(TPG):
                x = k.X[:, bass.ds(g * TPG + c, 1), :]
                last = dve.scalar_tensor_tensor(out=x, in0=k.bank[5][:, c * P:(c + 1) * P].unsqueeze(1),
                                                scalar=k.rsum[:, 8 + c:9 + c], in1=x, op0=ALU.mult, op1=ALU.add)
            last.then_inc(s["X"], 1)

        def prologue():
            normalise(0)
            normalise(1)
            shift(0, 0)

        def body(g, gp, first, last):
            if not last:
                normalise(g + 2)
                shift(g + 1, 1 - gp)
            add(g, gp)

        run_groups(dve, prologue, body, lambda: None)

    def gpsimd(self, pool):
        k, s, past = self.k, self.s, self.past
        layer_rstd(pool, k, 0, s, past)
        with pool.Fori(1, GROUPS + 1) as g:
            layer_rstd(pool, k, g, s, past)

    def sync(self, sp):
        k, s, past = self.k, self.s, self.past

        def load(g, gp):
            at_least(sp, s["k"], g - 1, past["k"])
            sp.dma_start(k.ctxT[gp][:, :], k.ctxT_dram[:, bass.ds(g * GT, GT)]).then_inc(s[f"ctx{gp}"], 16)
            at_least(sp, s["out"], g - 1, past["out"])
            sp.dma_start(k.ctxN[gp][:, :, :], k.ctxN_dram[:, bass.ds(g * GB, GB), :]).then_inc(s[f"values{gp}"], 16)

        for g in range(GROUPS):
            load(g, g % 2)


class Route:


    def __init__(self, k, kind):
        self.k, self.kind = k, kind
        own = ("w", "wTp", "wT", "bias", "biased") if kind == "f1" else ()
        self.s, self.past = k.signals(
            {n: GROUPS for n in ("stats", "rstd", "xn", "lnT", "hT", "logits", "lg", "e", "exp") + own})
        self.E = {"f0": E0, "f1": E1, "f3": E3}[kind]
        self.weights = k.route if kind == "f3" else k.route8
        self.gate = ATT_W(k.att_w, {"f0": "gate0", "f1": "switch", "f3": "gate3"}[kind])
        self.turned = k.bank[7] if kind == "f3" else k.bank[6]
        self.logits_at = k.bank[7][:, 0:TPG * self.E]

    def turn(self, pe, n):
        k, s, past = self.k, self.s, self.past
        pe.wait_ge(s["xn"], past["xn"] + n + 1)
        at_least(pe, s["hT"], n, past["hT"])
        if self.kind == "f3":
            at_least(pe, s["lg"], n, past["lg"])
        for c in range(TPG):
            last = pe.transpose(self.turned[:, c * P:(c + 1) * P], k.xn[:, c, :], CONST(k.const, "ident"))
        last.then_inc(s["lnT"], 1)

    def logits(self, pe, n):
        k, s, past = self.k, self.s, self.past
        pe.wait_ge(s["hT"], past["hT"] + n + 1)
        at_least(pe, s["lg"], n, past["lg"])
        if self.kind == "f1":
            at_least(pe, s["biased"], n, past["biased"])
        for c in range(TPG):
            last = pe.matmul(self.logits_at[:, c * self.E:(c + 1) * self.E], k.hT[0][:, c * P:(c + 1) * P],
                             self.gate, start=True, stop=True)
        last.then_inc(s["logits"], 1)

    def turn_weights(self, pe, n):
        k, s, past = self.k, self.s, self.past
        pe.wait_ge(s["w"], past["w"] + n + 1)
        for c in range(TPG):
            last = pe.transpose(k.bank[6][0:E1, c * P:(c + 1) * P], k.wt[:, c, :], CONST(k.const, "ident"))
        last.then_inc(s["wTp"], 1)

    def biases(self, pe, n):
        k, s, past = self.k, self.s, self.past
        pe.wait_ge(s["wT"], past["wT"] + n + 1)
        for c in range(TPG):
            last = pe.matmul(k.bank[7][:, c * P:(c + 1) * P], k.wtT[0:E1, c * P:(c + 1) * P], k.b2e[0:E1, :],
                             start=True, stop=True)
        last.then_inc(s["bias"], 1)

    def keep(self, act, n):
        k, s, past = self.k, self.s, self.past
        act.wait_ge(s["lnT"], past["lnT"] + n + 1)
        at_least(act, s["logits"], n, past["logits"])
        scale = ATT_W(k.att_w, "ln2") if self.kind == "f0" else 1.0
        fn = ACT.Identity if self.kind == "f0" else ACT.Copy
        act.activation(k.hT[0][:, :], self.turned[:, :], fn, scale=scale).then_inc(s["hT"], 1)

    def exps(self, act, n):
        k, s, past = self.k, self.s, self.past
        act.wait_ge(s["e"], past["e"] + n + 1)
        width = {"f0": 2, "f1": E1, "f3": E3}[self.kind]
        act.activation(k.ex[:, :, 0:width], k.ex[:, :, 0:width], ACT.Exp).then_inc(s["exp"], 1)

    def keep_weights(self, act, n):
        k, s, past = self.k, self.s, self.past
        act.wait_ge(s["wTp"], past["wTp"] + n + 1)
        at_least(act, s["bias"], n, past["bias"])
        act.activation(k.wtT[0:E1, :], k.bank[6][0:E1, :], ACT.Copy).then_inc(s["wT"], 1)

    def statistics(self, dve, n):
        k, s = self.k, self.s
        dve.drain()
        if self.kind != "f0":
            layer_stats(dve, k, n, s["stats"])
            return
        for c in range(TPG):
            dve.bn_stats(k.bn[:, c, :], k.XH[:, bass.ds(n * TPG + c, 1), :].rearrange("p a n -> p (a n)"))
        dve.drain()
        for c in range(TPG):
            dve.bn_aggr(k.mv[:, c, :], k.bn[:, c, :])
        dve.drain()
        dve.tensor_tensor(k.veps[:, :], k.mv[:, :, 0], k.mv[:, :, 0], ALU.mult)
        dve.drain()
        dve.tensor_tensor(k.veps[:, :], k.veps[:, :], k.mv[:, :, 1], ALU.add)
        dve.drain()
        dve.tensor_scalar(k.veps[:, :], k.veps[:, :], EPS, None, ALU.add).then_inc(s["stats"], 1)

    def normalise(self, dve, n):
        k, s, past = self.k, self.s, self.past
        dve.wait_ge(s["rstd"], past["rstd"] + n + 1)
        at_least(dve, s["lnT"], n, past["lnT"])
        for c in range(TPG):
            if self.kind == "f0":
                last = dve.tensor_scalar(k.xn[:, c, :], k.XH[:, bass.ds(n * TPG + c, 1), :],
                                         k.rstd[:, c:c + 1], 0.0, ALU.mult, ALU.add)
            else:
                last = dve.tensor_scalar(k.xn[:, c, :], k.X[:, bass.ds(n * TPG + c, 1), :], k.mv[:, c, 0:1],
                                         k.rstd[:, c:c + 1], ALU.subtract, ALU.mult)
        last.then_inc(s["xn"], 1)

    def fill(self, dve):
        dve.memset(self.k.lg[:, :, :], SENT)
        dve.memset(self.k.cand[:, :, :], SENT)
        dve.drain()

    def mark(self, dve, rows, width, top, n):
        taken = self.k.taken
        dve.memset(top[:, :, n:8], SENT)
        dve.drain()
        for c in range(TPG):
            dve.match_replace(taken[:, c, 0:width], top[:, c, :], rows[:, c, 0:width], TAKEN)
        dve.drain()

    def sums(self, dve, values, weight):
        k = self.k
        dve.tensor_reduce(k.sm[:, 0:TPG], values, AX_X, ALU.add)
        dve.drain()
        if self.kind == "f3":
            dve.tensor_scalar(k.sm[:, 0:TPG], k.sm[:, 0:TPG], 1e-20, None, ALU.add)
            dve.drain()
        dve.reciprocal(k.sm[:, 4:8], k.sm[:, 0:TPG])
        dve.drain()
        if self.kind == "f3":
            dve.tensor_scalar(k.sm[:, 8:12], k.sm[:, 4:8], 0.2, weight, ALU.mult, ALU.mult)
        else:
            dve.tensor_scalar(k.sm[:, 8:12], k.sm[:, 4:8], weight, None, ALU.mult)
        dve.drain()

    def choose0(self, dve, n, step):
        k, s, past, E = self.k, self.s, self.past, self.E
        if step == 0:
            dve.drain()
            dve.wait_ge(s["logits"], past["logits"] + n + 1)
            dve.tensor_copy(k.lg[:, :, 0:E], self.logits_at.rearrange("p (c e) -> p c e", c=TPG))\
                .then_inc(s["lg"], 1)
            dve.drain()
            for c in range(TPG):
                dve.max(k.t8[:, c, :], k.lg[:, c, 0:16])
            dve.drain()
            best = k.t8[:, :, 0:1].broadcast_to([P, TPG, 2])
            dve.tensor_tensor(k.ex[:, :, 0:2], k.t8[:, :, 0:2], best, ALU.subtract).then_inc(s["e"], 1)
        elif step in (1, 2):
            dve.tensor_copy(k.m8[:, :, :], k.t8[:, :, :])
            dve.drain()
            self.mark(dve, k.lg, 16, k.m8, step)
            dve.tensor_scalar(k.pk[:, step - 1, :, 0:E], k.taken[:, :, 0:E], TAKEN, None, ALU.is_equal)
            dve.drain()
        elif step == 3:
            dve.tensor_tensor(k.pk[:, 1, :, 0:E], k.pk[:, 1, :, 0:E], k.pk[:, 0, :, 0:E], ALU.subtract)
            dve.drain()
            dve.wait_ge(s["exp"], past["exp"] + n + 1)
            self.sums(dve, k.ex[:, :, 0:2], k.gates[:, 4:5])
        elif step == 4:
            dve.tensor_tensor(k.ex[:, :, 0:2], k.ex[:, :, 0:2],
                              k.sm[:, 8:12].unsqueeze(2).broadcast_to([P, TPG, 2]), ALU.mult)
            dve.drain()
            for i in range(2):
                dve.tensor_tensor(k.pk[:, i, :, 0:E], k.pk[:, i, :, 0:E],
                                  k.ex[:, :, i:i + 1].broadcast_to([P, TPG, E]), ALU.mult)
            dve.drain()
            dve.tensor_tensor(self.weights[:, bass.ds(n * TPG, TPG), 0:E], k.pk[:, 0, :, 0:E], k.pk[:, 1, :, 0:E], ALU.add)
        else:
            x, xh = (v[:, bass.ds(n * TPG, TPG), :] for v in (k.X, k.XH))
            dve.scalar_tensor_tensor(out=x, in0=xh, scalar=k.gates[:, 4:5], in1=x, op0=ALU.mult, op1=ALU.add)

    def choose1(self, dve, n, step):
        k, s, past, E = self.k, self.s, self.past, self.E
        if step == 0:
            dve.drain()
            dve.wait_ge(s["logits"], past["logits"] + n + 1)
            sb = ROWS(k.rows, "switch_b").unsqueeze(1).broadcast_to([P, TPG, E])
            dve.tensor_tensor(k.lg[:, :, 0:E], self.logits_at.rearrange("p (c e) -> p c e", c=TPG), sb,
                              ALU.add).then_inc(s["lg"], 1)
            dve.drain()
            for c in range(TPG):
                dve.max(k.t8[:, c, :], k.lg[:, c, 0:16])
            dve.drain()
            dve.tensor_tensor(k.ex[:, :, 0:E], k.lg[:, :, 0:E], k.t8[:, :, 0:1].broadcast_to([P, TPG, E]),
                              ALU.subtract).then_inc(s["e"], 1)
        elif step == 1:
            self.mark(dve, k.lg, 16, k.t8, 1)
            dve.tensor_scalar(k.pk[:, 0, :, 0:E], k.taken[:, :, 0:E], TAKEN, None, ALU.is_equal)
            dve.drain()
        elif step == 2:
            dve.wait_ge(s["exp"], past["exp"] + n + 1)
            self.sums(dve, k.ex[:, :, 0:E], k.gates[:, 5:6])
            at_least(dve, s["wTp"], n, past["wTp"])
            dve.tensor_tensor(k.wt[:, :, :], k.pk[:, 0, :, 0:E],
                              k.sm[:, 8:12].unsqueeze(2).broadcast_to([P, TPG, E]), ALU.mult).then_inc(s["w"], 1)
            dve.drain()
            dve.tensor_copy(self.weights[:, bass.ds(n * TPG, TPG), 0:E], k.wt[:, :, :])
        else:
            dve.wait_ge(s["bias"], past["bias"] + n + 1)
            x = k.X[:, bass.ds(n * TPG, TPG), :]
            dve.tensor_tensor(x, k.bank[7][:, :].rearrange("p (c n) -> p c n", c=TPG), x, ALU.add)\
                .then_inc(s["biased"], 1)

    def choose3(self, dve, n, step):
        k, s, past, E = self.k, self.s, self.past, self.E
        if step == 0:
            dve.drain()
            dve.wait_ge(s["logits"], past["logits"] + n + 1)
            dve.tensor_scalar(k.ex[:, :, 0:E], self.logits_at.rearrange("p (c e) -> p c e", c=TPG), -1.0,
                              None, ALU.mult).then_inc(s["lg"], 1)
            dve.drain().then_inc(s["e"], 1)
        elif step == 1:
            dve.wait_ge(s["exp"], past["exp"] + n + 1)
            dve.tensor_scalar(k.ex[:, :, 0:E], k.ex[:, :, 0:E], 1.0, None, ALU.add)
            dve.drain()
            dve.reciprocal(k.sg[:, :, :], k.ex[:, :, 0:E])
            dve.drain()
            gb = ROWS(k.rows, "gate_bias").unsqueeze(1).broadcast_to([P, TPG, E])
            dve.tensor_tensor(k.sc[:, :, :], k.sg[:, :, :], gb, ALU.add)
            dve.drain()
        elif step in (2, 3):
            for c in range((step - 2) * 2, (step - 1) * 2):
                for q in range(G3):
                    dve.max(k.g8[:, c, q, :], k.sc[:, c, q * 8:(q + 1) * 8])
        elif step == 4:
            dve.drain()
            dve.tensor_tensor(k.lg[:, :, 0:G3], k.g8[:, :, :, 0], k.g8[:, :, :, 1], ALU.add)
            dve.drain()
            for c in range(TPG):
                dve.max(k.t8[:, c, :], k.lg[:, c, 0:16])
            dve.drain()
        elif step == 5:
            self.mark(dve, k.lg, 16, k.t8, 2)
            dve.tensor_scalar(k.gm[:, :, 0, :], k.taken[:, :, 0:G3], TAKEN, None, ALU.is_equal)
            dve.drain()
            dve.tensor_scalar(k.gm[:, :, 1, :], k.gm[:, :, 0, :], 1.0, -LOW, ALU.subtract, ALU.mult)
            dve.drain()
        elif step in (6, 7):
            cand = k.cand[:, :, 0:E].rearrange("p c (q e) -> p c q e", q=G3)
            src = k.sc[:, :, :].rearrange("p c (q e) -> p c q e", q=G3) if step == 6 else cand
            dve.tensor_tensor(cand, src, k.gm[:, :, step - 6, :].unsqueeze(3).broadcast_to([P, TPG, G3, 8]),
                              ALU.mult if step == 6 else ALU.add)
            dve.drain()
        elif step == 8:
            for c in range(TPG):
                dve.max(k.t8[:, c, :], k.cand[:, c, 0:E + 8])
            dve.drain()
        elif step == 9:
            self.mark(dve, k.cand, E + 8, k.t8, K3)
            dve.tensor_scalar(k.ex[:, :, 0:E], k.taken[:, :, 0:E], TAKEN, None, ALU.is_equal)
            dve.drain()
        elif step == 10:
            dve.tensor_tensor(k.ex[:, :, 0:E], k.ex[:, :, 0:E], k.sg[:, :, :], ALU.mult)
            dve.drain()
        elif step == 11:
            self.sums(dve, k.ex[:, :, 0:E], k.gates[:, 7:8])
        elif step == 12:
            dve.tensor_tensor(self.weights[:, bass.ds(n * TPG, TPG), 0:E], k.ex[:, :, 0:E],
                              k.sm[:, 8:12].unsqueeze(2).broadcast_to([P, TPG, E]), ALU.mult)
        elif step == 13:
            self.mark(dve, k.cand, E + 8, k.t8, 1)
        else:
            dve.tensor_scalar(k.ex[:, :, 0:E], k.taken[:, :, 0:E], TAKEN, k.alpha[:, 0:1], ALU.is_equal, ALU.mult)
            dve.drain()
            two = k.ex[:, :, 0:E].rearrange("p c (l u) -> p c l u", u=2)
            dve.tensor_tensor(k.anchor[:, bass.ds(n * TPG, TPG), :], two[:, :, :, 0], two[:, :, :, 1], ALU.add)
            dve.drain()

    def choose(self, dve, n, step):
        {"f0": self.choose0, "f1": self.choose1, "f3": self.choose3}[self.kind](dve, n, step)

    def first_tensor(self, pe):
        self.turn(pe, 0)
        self.logits(pe, 0)

    def first_scalar(self, act):
        self.keep(act, 0)
        self.exps(act, 0)

    def first_choice(self, dve):
        for step in range({"f0": 6, "f1": 4, "f3": 15}[self.kind]):
            self.choose(dve, 0, step)

    def gpsimd(self, pool):
        k, s, past = self.k, self.s, self.past
        layer_rstd(pool, k, 0, s, past)
        with pool.Fori(1, GROUPS) as g:
            layer_rstd(pool, k, g, s, past)


def run_routed(eng, body, tail):
    body(0, True, False)
    with eng.Fori(1, GROUPS - 1) as g:
        body(g, False, False)
    body(GROUPS - 1, False, True)
    tail()


class Experts:


    def __init__(self, k, kind):
        self.k, self.kind = k, kind
        self.gated = kind == "f0"
        self.NF = (F0 if self.gated else F1) // P
        self.E = E0 if self.gated else E1
        self.up_w, self.down_w = k.experts[kind]
        self.parts = [v.rearrange("p (e f) -> p e f", e=self.E) for v in (k.w_high[kind], k.w_low)]
        n = GROUPS * self.E
        self.s, self.past = k.signals({"up": n * self.NF, "act": n * self.NF, "hid": n * self.NF * self.gated,
                                       "y": n, "X": n, "wsplit": self.E, "xsplit": GROUPS})
        self.route = Route(k, kind)

    def tensor(self, pe):
        k, s, past, NF, E = self.k, self.s, self.past, self.NF, self.E
        r = self.route

        def up(g, e, first):
            i = g * E + e
            x = [v[:, bass.ds(g * GT, GT)] for v in (k.HThigh, k.HTlow)]
            if e == 0:
                pe.wait_ge(s["xsplit"], past["xsplit"] + g + 1)
            if first:
                pe.wait_ge(s["wsplit"], past["wsplit"] + e + 1)
            for f in range(NF):
                at_least(pe, s["hid"] if self.gated else s["act"], (i - 1) * NF + f + 1, (past["hid"] if self.gated else past["act"]))
                for which, at in enumerate((f * P, F0 + f * P) if self.gated else (f * P,)):
                    last = product(pe, k.bank[2 * which + f][:, :], [w[:, e, at:at + P] for w in self.parts], x)
                last.then_inc(s["up"], 1)

        def down(g, e):
            i = g * E + e
            pe.wait_ge(s["hid"] if self.gated else s["act"], (past["hid"] if self.gated else past["act"]) + (i + 1) * NF)
            at_least(pe, s["X"], i - 1, past["X"])
            for c in range(TPG):
                for f in range(NF):
                    last = pe.matmul(k.bank[4 + e % 2][:, c * P:(c + 1) * P], k.hid[e % 2][:, f, c * P:(c + 1) * P],
                                     self.down_w[:, e, f, :], start=(f == 0), stop=(f == NF - 1))
            last.then_inc(s["y"], 1)

        def body(g, first, last):
            for e in range(E):
                up(g, e, first)
                if e > 0:
                    down(g, e - 1)
                elif not first:
                    down(g - 1, E - 1)
                elif not self.gated:
                    r.turn_weights(pe, 0)
                    r.biases(pe, 0)
                if not last:
                    if e == 2:
                        r.turn(pe, g + 1)
                    elif e == 3:
                        r.logits(pe, g + 1)
                    elif e == 6 and not self.gated:
                        r.turn_weights(pe, g + 1)
                    elif e == 7 and not self.gated:
                        r.biases(pe, g + 1)

        r.first_tensor(pe)
        pe.wait_ge(k.loaded[self.kind], 16 * k.loads[self.kind])
        run_routed(pe, body, lambda: down(GROUPS - 1, E - 1))

    def scalar(self, act):
        k, s, past, NF, E = self.k, self.s, self.past, self.NF, self.E
        r = self.route

        def body(g, first, last):
            for e in range(E):
                i = g * E + e
                for f in range(NF):
                    act.wait_ge(s["up"], past["up"] + i * NF + f + 1)
                    if self.gated:
                        at_least(act, s["hid"], (i - 1) * NF + f + 1, past["hid"])
                        act.activation(k.silu[:, f, :], k.bank[f][:, :], ACT.Silu).then_inc(s["act"], 1)
                    else:
                        at_least(act, s["y"], i - 1, past["y"])
                        act.activation(k.hid[e % 2][:, f, :], k.bank[f][:, :], ACT.Gelu_apprx_tanh,
                                       bias=k.b1e[:, e * NF + f:e * NF + f + 1]).then_inc(s["act"], 1)
                if first and e == 0 and not self.gated:
                    r.keep_weights(act, 0)
                if not last:
                    if e == 2:
                        r.keep(act, g + 1)
                    elif e == 4:
                        r.exps(act, g + 1)
                    elif e == 6 and not self.gated:
                        r.keep_weights(act, g + 1)

        r.first_scalar(act)
        act.wait_ge(k.loaded[self.kind], 16 * k.loads[self.kind])
        run_routed(act, body, lambda: None)

    def vector(self, dve):
        k, s, past, NF, E = self.k, self.s, self.past, self.NF, self.E
        r = self.route

        def add(g, e):
            i = g * E + e
            dve.drain()
            dve.wait_ge(s["y"], past["y"] + i + 1)
            for c in range(TPG):
                x = k.X[:, bass.ds(g * TPG + c, 1), :]
                w = k.route8[:, bass.ds(g * TPG + c, 1), e:e + 1].rearrange("p a e -> p (a e)")
                last = dve.scalar_tensor_tensor(out=x, in0=k.bank[4 + e % 2][:, c * P:(c + 1) * P].unsqueeze(1),
                                                scalar=w, in1=x, op0=ALU.mult, op1=ALU.add)
            last.then_inc(s["X"], 1)

        def split_weights(e):
            split(dve, self.up_w[:, e, :], k.split_u, self.parts[0][:, e, :], self.parts[1][:, e, :])\
                .then_inc(s["wsplit"], 1)

        def split_tokens(n):
            dve.wait_ge(r.s["hT"], r.past["hT"] + n + 1)
            at = bass.ds(n * GT, GT)
            split(dve, k.hT[0][:, :], k.split_u, k.HThigh[:, at], k.HTlow[:, at]).then_inc(s["xsplit"], 1)

        def body(g, first, last):
            for e in range(E):
                i = g * E + e
                if first and e < E - 1:
                    split_weights(e + 1)
                if self.gated:
                    for f in range(NF):
                        dve.wait_ge(s["act"], past["act"] + i * NF + f + 1)
                        at_least(dve, s["y"], i - 1, past["y"])
                        dve.tensor_tensor(k.hid[e % 2][:, f, :], k.bank[2 + f][:, :], k.silu[:, f, :],
                                          ALU.mult).then_inc(s["hid"], 1)
                if e > 0:
                    add(g, e - 1)
                elif not first:
                    add(g - 1, E - 1)
                if not last:
                    if e == 0:
                        r.statistics(dve, g + 1)
                    elif e == 1:
                        r.normalise(dve, g + 1)
                    elif e == 3:
                        split_tokens(g + 1)
                    elif self.gated and e >= 4:
                        for step in ((0,), (1, 2), (3, 4), (5,))[e - 4]:
                            r.choose(dve, g + 1, step)
                    elif e >= 4:
                        for step in ((0, 1), (2,), (), (3,))[e - 4]:
                            r.choose(dve, g + 1, step)

        dve.wait_ge(k.loaded[self.kind], 16 * k.loads[self.kind])
        r.fill(dve)
        r.statistics(dve, 0)
        split_weights(0)
        r.normalise(dve, 0)
        split_tokens(0)
        r.first_choice(dve)
        run_routed(dve, body, lambda: add(GROUPS - 1, E - 1))

    def gpsimd(self, pool):
        self.route.gpsimd(pool)

    def sync(self, sp):
        pass


class Choices:


    def __init__(self, k):
        self.k = k
        self.s, self.past = k.signals(
            {n: GROUPS + 1 for n in ("stats", "rstd", "xn")} | {n: GROUPS for n in ("lnT", "hT", "lr", "lrT")}
            | {n: TILES for n in ("logits", "mid", "eq", "ranked", "peak", "picked", "relu", "hid", "pT", "hidT", "out",
                                  "X")})

    def tensor(self, pe):
        k, s, past = self.k, self.s, self.past
        ident = CONST(k.const, "ident")

        def front(n, np_):
            pe.wait_ge(s["xn"], past["xn"] + n + 1)
            at_least(pe, s["lrT"], n, past["lrT"])
            for c in range(TPG):
                last = pe.transpose(k.bank[0][:, c * P:(c + 1) * P], k.xn[:, c, :], ident)
            last.then_inc(s["lnT"], 1)
            pe.wait_ge(s["hT"], past["hT"] + n + 1)
            pe.matmul(k.bank[0][0:DL, :], k.m1, k.hT[np_][:, :], start=True, stop=True).then_inc(s["lr"], 1)

        def units(t, c, gp, g):
            pe.wait_ge(s["lrT"], past["lrT"] + g + 1)
            at_least(pe, s["hid"], t - 1, past["hid"])
            pe.matmul(k.bank[2 + c % 2][:, :], k.lrT[gp][:, c * P:(c + 1) * P], k.m2, start=True, stop=True)\
                .then_inc(s["logits"], 1)
            pe.matmul(k.bank[4 + c % 2][:, :], k.hT[gp][:, c * P:(c + 1) * P], k.w1c, start=True, stop=True)\
                .then_inc(s["mid"], 1)

        def turn(t, c):
            pe.wait_ge(s["hid"], past["hid"] + t + 1)
            at_least(pe, s["hidT"], t, past["hidT"])
            for f in range(4):
                last = pe.transpose(k.bank[6][:, f * P:(f + 1) * P], k.hidc[c % 2][:, f * P:(f + 1) * P], ident)
            last.then_inc(s["pT"], 1)

        def multiply(t, c):
            pe.wait_ge(s["hidT"], past["hidT"] + t + 1)
            at_least(pe, s["X"], t - 1, past["X"])
            for f in range(4):
                last = pe.matmul(k.bank[7 - 6 * (c % 2)][:, 0:P], k.hidcT[:, f * P:(f + 1) * P], k.w2c[:, f, :], start=(f == 0),
                                 stop=(f == 3))
            last.then_inc(s["out"], 1)

        def prologue():
            front(0, 0)
            units(0, 0, 0, 0)
            units(1, 1, 0, 0)

        def body(g, gp, first, last):
            for c in range(TPG):
                t = g * TPG + c
                if c < 2:
                    units(t + 2, c + 2, gp, g)
                elif not last:
                    units(t + 2, c - 2, 1 - gp, g + 1)
                turn(t, c)
                if c == 0 and not last:
                    front(g + 1, 1 - gp)
                multiply(t, c)

        pe.wait_ge(k.loaded["f2"], 16 * k.loads["f2"])
        run_groups(pe, prologue, body, lambda: None)

    def scalar(self, act):
        k, s, past = self.k, self.s, self.past

        def front(n, np_):
            act.wait_ge(s["lnT"], past["lnT"] + n + 1)
            act.activation(k.hT[np_][:, :], k.bank[0][:, :], ACT.Copy).then_inc(s["hT"], 1)
            act.wait_ge(s["lr"], past["lr"] + n + 1)
            act.activation(k.lrT[np_][0:DL, :], k.bank[0][0:DL, :], ACT.Copy).then_inc(s["lrT"], 1)

        def relu(t, c):
            act.wait_ge(s["mid"], past["mid"] + t + 1)
            at_least(act, s["hid"], t - 1, past["hid"])
            act.activation(k.relu[c % 2][:, :], k.bank[4 + c % 2][:, :], ACT.Relu).then_inc(s["relu"], 1)

        def prologue():
            front(0, 0)
            relu(0, 0)
            relu(1, 1)

        def body(g, gp, first, last):
            for c in range(TPG):
                t = g * TPG + c
                if c < 2 or not last:
                    relu(t + 2, c % 2)
                act.wait_ge(s["pT"], past["pT"] + t + 1)
                at_least(act, s["out"], t, past["out"])
                act.activation(k.hidcT[:, :], k.bank[6][:, :], ACT.Copy).then_inc(s["hidT"], 1)
                if c == 0 and not last:
                    front(g + 1, 1 - gp)

        for lr in k.lrT:
            act.activation(lr[DL:DL + 1, :], k.onesrow[DL:DL + 1, :], ACT.Copy)
        act.drain()
        run_groups(act, prologue, body, lambda: None)

    def vector(self, dve):
        k, s, past = self.k, self.s, self.past

        def normalise(n):
            dve.wait_ge(s["rstd"], past["rstd"] + n + 1)
            at_least(dve, s["lnT"], n, past["lnT"])
            for c in range(TPG):
                last = dve.tensor_scalar(k.xn[:, c, :], k.X[:, bass.ds(n * TPG + c, 1), :], k.mv[:, c, 0:1],
                                         k.rstd[:, c:c + 1], ALU.subtract, ALU.mult)
            last.then_inc(s["xn"], 1)

        def blocks(ap):
            return ap.rearrange("p (j y) -> p j y", j=D1)

        def largest(t, c):
            dve.wait_ge(s["logits"], past["logits"] + t + 1)
            dve.tensor_reduce(k.top[:, 0:D1], blocks(k.bank[2 + c % 2][:, :]), AX_X, ALU.max)
            dve.drain()
            dve.tensor_tensor(blocks(k.eq[c % 2][:, :]), blocks(k.bank[2 + c % 2][:, :]),
                              k.top[:, 0:D1].unsqueeze(2).broadcast_to([P, D1, D2]), ALU.is_equal)
            dve.drain().then_inc(s["eq"], 1)

        def peak(t, c):
            dve.wait_ge(s["ranked"], past["ranked"] + t + 1)
            dve.tensor_reduce(k.top[:, 16 + 8 * (c % 2):24 + 8 * (c % 2)], blocks(k.eq[c % 2][:, :]), AX_X, ALU.max)\
                .then_inc(s["peak"], 1)

        def keep(t, c):
            dve.wait_ge(s["picked"], past["picked"] + t + 1)
            dve.wait_ge(s["relu"], past["relu"] + t + 1)
            at_least(dve, s["pT"], t - 1, past["pT"])
            dve.scalar_tensor_tensor(out=k.hidc[c % 2][:, :], in0=k.eq[c % 2][:, :], scalar=0.0,
                                     in1=k.relu[c % 2][:, :], op0=ALU.is_equal, op1=ALU.mult).then_inc(s["hid"], 1)

        def add(t, c):
            dve.drain()
            dve.wait_ge(s["out"], past["out"] + t + 1)
            x = k.X[:, bass.ds(t, 1), :]
            dve.scalar_tensor_tensor(out=k.tmp[:, 0:P], in0=k.bank[7 - 6 * (c % 2)][:, 0:P], scalar=k.gates[:, 6:7], in1=k.b2c,
                                     op0=ALU.mult, op1=ALU.add)
            dve.drain().then_inc(s["X"], 1)
            dve.tensor_tensor(x, x, k.tmp[:, 0:P].unsqueeze(1), ALU.add)

        def prologue():
            layer_stats(dve, k, 0, s["stats"])
            normalise(0)
            largest(0, 0)
            layer_stats(dve, k, 1, s["stats"])
            peak(0, 0)
            largest(1, 1)
            keep(0, 0)
            normalise(1)
            peak(1, 1)

        def body(g, gp, first, last):
            for c in range(TPG):
                t = g * TPG + c
                if c < 2 or not last:
                    largest(t + 2, c % 2)
                if c < 3 or not last:
                    keep(t + 1, (c + 1) % 2)
                if c > 0 or not first:
                    add(t - 1, c + 1)
                if c < 2 or not last:
                    peak(t + 2, c % 2)
                if c == 1 and not last:
                    layer_stats(dve, k, g + 2, s["stats"])
                elif c == 2 and not last:
                    normalise(g + 2)

        run_groups(dve, prologue, body, lambda: add(TILES - 1, 1))

    def gpsimd(self, pool):
        k, s, past = self.k, self.s, self.past

        def rank(t, c):
            pool.wait_ge(s["eq"], past["eq"] + t + 1)
            eq = k.eq[c % 2][:, :].rearrange("p (j y) -> p j y", j=D1)
            pool.tensor_tensor(eq, eq, CONST(k.const, "first").unsqueeze(1).broadcast_to([P, D1, D2]), ALU.mult)\
                .then_inc(s["ranked"], 1)

        def pick(t, c):
            pool.wait_ge(s["peak"], past["peak"] + t + 1)
            eq = k.eq[c % 2][:, :].rearrange("p (j y) -> p j y", j=D1)
            top = k.top[:, 16 + 8 * (c % 2):24 + 8 * (c % 2)].unsqueeze(2).broadcast_to([P, D1, D2])
            pool.tensor_tensor(eq, eq, top, ALU.subtract).then_inc(s["picked"], 1)

        def prologue():
            layer_rstd(pool, k, 0, s, past)
            rank(0, 0)
            layer_rstd(pool, k, 1, s, past)
            pick(0, 0)
            rank(1, 1)
            pick(1, 1)

        def body(g, gp, first, last):
            for c in range(TPG):
                if c < 2 or not last:
                    rank(g * TPG + c + 2, c % 2)
                    pick(g * TPG + c + 2, c % 2)
                if c == 1 and not last:
                    layer_rstd(pool, k, g + 2, s, past)

        run_groups(pool, prologue, body, lambda: None)

    def sync(self, sp):
        pass


class Mixture:

    CHUNKS = len(CHUNKS3)

    def __init__(self, k):
        self.k = k
        self.s, self.past = k.signals(
            {n: TILES * self.CHUNKS for n in ("up", "silu", "hid", "pT", "hidT", "out")}
            | {"x": 2 * GROUPS, "X": TILES, "wsplit": self.CHUNKS})
        self.route = Route(k, "f3")
        self.chunks, at, block = [], 0, 0
        for _, _, groups, width in CHUNKS3:
            units = groups * width
            blocks = -(-units // P)
            self.chunks.append((at, k.w3d[:, block:block + blocks, :], units))
            at, block = at + units, block + blocks

    def tensor(self, pe):
        k, s, past = self.k, self.s, self.past
        r = self.route
        ident = CONST(k.const, "ident")

        def up(g, c, n, first):
            t = g * TPG + c
            i = t * self.CHUNKS + n
            at, _, width = self.chunks[n]
            if n == 0:
                pe.wait_ge(s["x"], past["x"] + 2 * g + 1 + c // 2)
            if first:
                pe.wait_ge(s["wsplit"], past["wsplit"] + n + 1)
            at_least(pe, s["hid"], i - 1, past["hid"])
            b = 2 * (n % 2)
            x = [v[:, c * P:(c + 1) * P] for v in k.hx]
            product(pe, k.bank[b][:, 0:width], x, [w[:, at:at + width] for w in k.w3g_parts])
            product(pe, k.bank[b + 1][:, 0:width], x, [w[:, at:at + width] for w in k.w3u_parts]).then_inc(s["up"], 1)

        def turn(t, n):
            i = t * self.CHUNKS + n
            width = self.chunks[n][2]
            pe.wait_ge(s["hid"], past["hid"] + i + 1)
            at_least(pe, s["hidT"], i - 1, past["hidT"])
            for f in range(-(-width // P)):
                last = pe.transpose(k.bank[4 + n % 2][:, f * P:(f + 1) * P], k.hid3[n % 2][:, f * P:(f + 1) * P],
                                    ident)
            last.then_inc(s["pT"], 1)

        def down(t, n):
            i = t * self.CHUNKS + n
            width = self.chunks[n][2]
            pe.wait_ge(s["hidT"], past["hidT"] + i + 1)
            if n == 0:
                at_least(pe, s["X"], t, past["X"])
            for f in range(-(-width // P)):
                last = pe.matmul(k.bank[6][:, 0:P], k.hid3T[n % 2][:, f * P:(f + 1) * P],
                                 self.chunks[n][1][:, f, :], start=(n == 0 and f == 0),
                                 stop=(n == self.CHUNKS - 1 and (f + 1) * P >= width))
            last.then_inc(s["out"], 1)

        def body(g, first, last):
            for u in range(TPG * self.CHUNKS):
                n = u % self.CHUNKS
                up(g, u // self.CHUNKS, n, first and u < self.CHUNKS)
                if u >= 1:
                    turn(g * TPG + (u - 1) // self.CHUNKS, (u - 1) % self.CHUNKS)
                elif not first:
                    turn(g * TPG - 1, self.CHUNKS - 1)
                if u >= 2:
                    down(g * TPG + (u - 2) // self.CHUNKS, (u - 2) % self.CHUNKS)
                elif not first:
                    down(g * TPG - 1, self.CHUNKS - 2 + u)
                if u == 4 and not last:
                    r.turn(pe, g + 1)
                elif u == 6 and not last:
                    r.logits(pe, g + 1)

        def tail():
            turn(TILES - 1, self.CHUNKS - 1)
            down(TILES - 1, self.CHUNKS - 2)
            down(TILES - 1, self.CHUNKS - 1)

        r.first_tensor(pe)
        pe.wait_ge(k.loaded["f3"], 16 * k.loads["f3"])
        run_routed(pe, body, tail)

    def scalar(self, act):
        k, s, past = self.k, self.s, self.past
        r = self.route

        def silu(t, n):
            i = t * self.CHUNKS + n
            width = self.chunks[n][2]
            act.wait_ge(s["up"], past["up"] + i + 1)
            at_least(act, s["hid"], i - 1, past["hid"])
            act.activation(k.silu3[n % 2][:, 0:width], k.bank[2 * (n % 2)][:, 0:width], ACT.Silu)\
                .then_inc(s["silu"], 1)

        def turned(t, n):
            i = t * self.CHUNKS + n
            cols = -(-self.chunks[n][2] // P) * P
            act.wait_ge(s["pT"], past["pT"] + i + 1)
            at_least(act, s["out"], i - 1, past["out"])
            act.activation(k.hid3T[n % 2][:, 0:cols], k.bank[4 + n % 2][:, 0:cols], ACT.Copy)\
                .then_inc(s["hidT"], 1)

        def body(g, first, last):
            for u in range(TPG * self.CHUNKS):
                silu(g * TPG + u // self.CHUNKS, u % self.CHUNKS)
                if u >= 1:
                    turned(g * TPG + (u - 1) // self.CHUNKS, (u - 1) % self.CHUNKS)
                elif not first:
                    turned(g * TPG - 1, self.CHUNKS - 1)
                if u == 4 and not last:
                    r.keep(act, g + 1)
                elif u == 8 and not last:
                    r.exps(act, g + 1)

        r.first_scalar(act)
        run_routed(act, body, lambda: turned(TILES - 1, self.CHUNKS - 1))

    def vector(self, dve):
        k, s, past = self.k, self.s, self.past
        r = self.route

        def weigh(t, n):
            i = t * self.CHUNKS + n
            width = self.chunks[n][2]
            dve.wait_ge(s["up"], past["up"] + i + 1)
            up = k.bank[2 * (n % 2) + 1][:, 0:width]
            part = k.up3[n % 2][:, 0:width]
            weights, lo, groups, _ = CHUNKS3[n]
            src = k.anchor if weights == "anchor" else k.route
            w = src[:, bass.ds(t, 1), lo:lo + groups].rearrange("p a e -> p (a e)").unsqueeze(2)\
                .broadcast_to([P, groups, width // groups])
            dve.tensor_tensor(part.rearrange("p (e i) -> p e i", e=groups), up.rearrange("p (e i) -> p e i", e=groups),
                              w, ALU.mult)
            dve.drain()
            dve.wait_ge(s["silu"], past["silu"] + i + 1)
            at_least(dve, s["pT"], i - 1, past["pT"])
            dve.tensor_tensor(k.hid3[n % 2][:, 0:width], part, k.silu3[n % 2][:, 0:width], ALU.mult)\
                .then_inc(s["hid"], 1)

        def add(t):
            dve.wait_ge(s["out"], past["out"] + (t + 1) * self.CHUNKS)
            x = k.X[:, bass.ds(t, 1), :]
            dve.tensor_tensor(x, k.bank[6][:, 0:P].unsqueeze(1), x, ALU.add).then_inc(s["X"], 1)

        def split_tokens(half):
            at = slice(half * GT // 2, (half + 1) * GT // 2)
            split(dve, k.hT[0][:, at], k.split_u3[:, 0:GT // 2], *(v[:, at] for v in k.hx)).then_inc(s["x"], 1)

        def split_weights(n):
            at, _, width = self.chunks[n]
            for w, parts in ((k.w3g, k.w3g_parts), (k.w3u, k.w3u_parts)):
                done = split(dve, w[:, at:at + width], k.split_u3[:, 0:width], *(p[:, at:at + width] for p in parts))
            done.then_inc(s["wsplit"], 1)

        def body(g, first, last):
            for u in range(TPG * self.CHUNKS):
                c, n = u // self.CHUNKS, u % self.CHUNKS
                t = g * TPG + c
                if first and u < self.CHUNKS - 1:
                    split_weights(n + 1)
                weigh(t, n)
                if n == 1 and not (first and c == 0):
                    add(t - 1)
                if u == 1:
                    split_tokens(1)
                if not last:
                    if u == 2:
                        r.statistics(dve, g + 1)
                    elif u == 3:
                        r.normalise(dve, g + 1)
                    elif u == 7:
                        r.choose(dve, g + 1, 0)
                    elif u == 12:
                        dve.wait_ge(r.s["hT"], r.past["hT"] + g + 2)
                        split_tokens(0)
                    elif u >= 9:
                        r.choose(dve, g + 1, u - 8 - (u > 12))

        dve.wait_ge(k.loaded["f3"], 16 * k.loads["f3"])
        dve.tensor_copy(k.route[:, :, E3:E3 + 1], k.gates[:, 7:8].unsqueeze(1).broadcast_to([P, TILES, 1]))
        dve.memset(k.hid3[1][:, :], 0.0)
        r.fill(dve)
        r.statistics(dve, 0)
        split_weights(0)
        r.normalise(dve, 0)
        dve.wait_ge(r.s["hT"], r.past["hT"] + 1)
        split_tokens(0)
        r.first_choice(dve)
        run_routed(dve, body, lambda: add(TILES - 1))

    def gpsimd(self, pool):
        self.route.gpsimd(pool)

    def sync(self, sp):
        pass


def build(nc, ins, out):
    with ExitStack() as ctx:
        k = Kernel(nc, ins, out, ctx)
        block = ctx.enter_context(nc.Block())

        @block.sync
        def _(sp):
            k.load(sp)
            for n, part in enumerate(k.program):
                if n:
                    sp.wait_ge(k.s_part, 4 * n)
                part.sync(sp)
                k.load_late(sp, n)
            sp.wait_ge(k.s_part, 4 * len(k.program))
            sp.dma_start(out, k.X[:, 0:TILES, :]).then_inc(k.s_out, 16)
            sp.wait_ge(k.s_out, 16)

        @block.tensor
        def _(pe):
            k.prepare_tensor(pe)
            for n, part in enumerate(k.program):
                k.enter(pe, n)
                part.tensor(pe)
                pe.drain().then_inc(k.s_part, 1)

        @block.scalar
        def _(act):
            k.prepare_scalar(act)
            for n, part in enumerate(k.program):
                k.enter(act, n)
                part.scalar(act)
                act.drain().then_inc(k.s_part, 1)

        @block.vector
        def _(dve):
            k.prepare_vector(dve)
            for n, part in enumerate(k.program):
                k.enter(dve, n)
                part.vector(dve)
                dve.drain().then_inc(k.s_part, 1)

        @block.gpsimd
        def _(pool):
            k.prepare_gpsimd(pool)
            for n, part in enumerate(k.program):
                k.enter(pool, n)
                part.gpsimd(pool)
                pool.drain().then_inc(k.s_part, 1)


def kernel_inputs(a):
    f = {n: np.asarray(v) for n, v in a.items()}
    x = f["x"].reshape(TILES, P, D).transpose(1, 0, 2)
    ctx = f["ctx_1024"].reshape(B * S, D)
    att = np.zeros((P, ATT_W.width), np.float32)

    def put(name, value):
        v = ATT_W(att, name)
        v[:] = np.asarray(value).reshape(v.shape)

    even_odd = np.arange(D).reshape(PAIRS, 2, DK).transpose(1, 0, 2).ravel()
    for n in ("wq", "wk", "wv", "wo"):
        cols = even_odd if n == "wv" else np.arange(D)
        put(f"{n}_x0", f["L0_xattn_" + n].T[:, cols])
        put(f"{n}_x1", f["L1_xattn_W" + n[1]][:, cols])
        put(f"{n}_x3", f["L3_xattn_W" + n[1]].T[:, cols])
    for n in ("bq", "bk", "bv"):
        for layer in (0, 1, 3):
            put(f"{n}_x{layer}", f[f"L{layer}_xattn_" + n])
    wqkv = f["L0_ffn_wqkv"]
    kv_rows = (np.arange(H)[:, None] // 4 * DK + np.arange(DK)[None]).ravel()
    swap = np.arange(D) // DK * DK + (np.arange(D) + DK // 2) % DK
    wq, wk, wv = wqkv[:H * DK], wqkv[H * DK:H * DK + 4 * DK][kv_rows], wqkv[H * DK + 4 * DK:][kv_rows]
    for n, w in (("wq_f0", wq), ("wqs_f0", wq[swap]), ("wk_f0", wk), ("wks_f0", wk[swap]), ("wv_f0", wv[even_odd]),
                 ("wo_f0", f["L0_ffn_wo"])):
        put(n, w.T)
    put("w1_x2", f["L2_xattn_W1"])
    put("w2t_x2", f["L2_xattn_W2"].T)
    put("b1_x2", f["L2_xattn_b1"])
    put("b2_x2", f["L2_xattn_b2"])
    put("ln1", f["L0_ffn_ln1_w"])
    put("ln2", f["L0_ffn_ln2_w"])
    put("mask", np.concatenate([f["fside_1xSxS2_0"][0]] * 2))
    put("gate0", f["L0_ffn_gate_w"].T)
    put("switch", f["L1_ffn_switch_w"])
    put("gate3", f["L3_ffn_gate_weight"].T)
    rows = np.zeros((1, ROWS.width), np.float32)
    for n, v in (("bo_x0", f["L0_xattn_bo"]), ("bo_x1", f["L1_xattn_bo"]), ("bo_x3", f["L3_xattn_bo"]),
                 ("b2_f2", f["L2_ffn_b2"]), ("g", np.concatenate([f["g_xattn"], f["g_ffn"]])),
                 ("decay", f["L0_xattn_time_decay"]), ("switch_b", f["L1_ffn_switch_b"]),
                 ("gate_bias", f["L3_ffn_gate_bias"])):
        ROWS(rows, n)[0] = v

    def down(w):
        return w.reshape(-1, P, D).transpose(1, 0, 2).reshape(P, -1)

    f0 = np.concatenate([f["L0_ffn_w13"].transpose(2, 0, 1).reshape(D, -1),
                         down(f["L0_ffn_w2"].transpose(0, 2, 1).reshape(-1, D))], 1)
    f1 = np.concatenate([f["L1_ffn_w1"].transpose(1, 0, 2).reshape(D, -1), down(f["L1_ffn_w2"].reshape(-1, D)),
                         f["L1_ffn_b1"].reshape(-1, P).T], 1)
    f2 = np.zeros((P, F2_W.width), np.float32)
    F2_W(f2, "m1")[:] = f["L2_ffn_m1"]
    F2_W(f2, "m2")[0:DL] = f["L2_ffn_m2"].reshape(DL, -1)
    F2_W(f2, "m2")[DL] = f["L2_ffn_mb"].ravel()
    F2_W(f2, "w1")[:] = f["L2_ffn_w1"].reshape(D, -1)
    F2_W(f2, "w2")[:] = down(f["L2_ffn_w2"].transpose(1, 0, 2).reshape(-1, D))

    def up3(which):
        return [f["L3_ffn_anchor_w_" + which].transpose(1, 0, 2).reshape(D, -1),
                f["L3_ffn_w_" + which].transpose(1, 0, 2).reshape(D, -1), f["L3_ffn_shared_w_" + which]]

    rows3 = {"anchor": f["L3_ffn_anchor_w_down"].reshape(-1, D),
             "route": np.concatenate([f["L3_ffn_w_down"].reshape(-1, D), f["L3_ffn_shared_w_down"]])}
    down3 = []
    for weights, lo, groups, width in CHUNKS3:
        r = rows3[weights][lo * width:(lo + groups) * width]
        down3.append(down(np.concatenate([r, np.zeros((-len(r) % P, D), np.float32)])))
    f3 = np.concatenate(up3("gate") + up3("up") + down3, 1)
    return {"x": x, "ctx_t": ctx.T, "ctx_n": ctx.reshape(B, S, D).transpose(1, 0, 2), "att_w": att, "rows": rows,
            "const": constants(), "f0_w": f0, "f1_w": f1, "f2_w": f2, "f3_w": f3, "b2e": f["L1_ffn_b2"]}


F2_W = Columns([("m1", DL), ("m2", D1 * D2), ("w1", D1 * D2), ("w2", D1 * D2)])
F0_COLS = E0 * 2 * F0 + E0 * F0 // P * D
F1_COLS = E1 * F1 + E1 * F1 // P * D + E1 * F1 // P
UP3 = E3 * I3 + L3 * A3 + I3
F3_COLS = 2 * UP3 + sum(-(-groups * width // P) for _, _, groups, width in CHUNKS3) * D
ATT_BUF = Columns([("probs0", H * S), ("probs1", H * S), ("PT0", H * S), ("PT1", H * S), ("Kblk0", 4 * H * S),
                   ("Kblk1", 4 * H * S), ("QT0", GT), ("QT1", GT), ("KT", GT), ("ctxT0", GT), ("ctxT1", GT),
                   ("attn0", GT), ("attn1", GT), ("aT", GT), ("soft0", TPG * S), ("soft1", TPG * S)])
X2_BUF = Columns([("skip", 4 * H * S), ("ctxN0", GB * D), ("ctxN1", GB * D)])
EXP_BUF = Columns([("route", TILES * E0), ("hid0", 4 * GT), ("hid1", 4 * GT), ("silu", 2 * GT), ("HThigh", B * S),
                   ("HTlow", B * S), ("w_low", max(E0 * 2 * F0, E1 * F1)), ("split_u", GT)])
F2_BUF = Columns([(n, GT) for n in ("lrT0", "lrT1", "relu0", "relu1", "hidc0", "hidc1", "eq0", "eq1", "hidcT")])
MIX_BUF = Columns([("route", TILES * (E3 + 1)), ("anchor", TILES * L3), ("split_u", GT), ("w_low", 2 * UP3)]
                  + [(n, GT) for n in ("silu30", "silu31", "up30", "up31", "hid30", "hid31", "hid3T0", "hid3T1")]
                  + [(n, GT) for n in ("hx_high", "hx_low")])


class Kernel:

    def __init__(self, nc, ins, out, ctx):
        self.nc, self.ins, self.ctx = nc, ins, ctx
        self.named, self.given = {n: self.sem(n) for n in ("X", "aTp")}, {"X": 2, "aTp": 2}

        def sb(name, shape):
            return ctx.enter_context(nc.sbuf_tensor(name, shape, F32))

        at = {}

        def shared(name, cols):
            tile = sb(name, [P, cols])
            at[name] = nc.sbuf_base - 4 * cols
            return tile

        def rounded(name, room, first, cols):
            return nc.alloc_sbuf_tensor_at(name, [P, cols], F32R, offset=at[room] + 4 * first)[:, :]

        self.X = sb("X", [P, TILES + TPG, D])
        self.att_w = sb("att_w", [P, ATT_W.width])
        self.rows = sb("rows", [P, ROWS.width])
        self.const = sb("const", [P, CONST.width])
        self.arena_a = shared("arena_a", max(F0_COLS, F3_COLS))
        self.arena_b = shared("arena_b", F1_COLS)
        self.f2_w = sb("f2_w", [P, F2_W.width])
        self.b2e = sb("b2e", [E1, D])
        self.XH = self.arena_b[:, 0:(TILES + TPG) * D].rearrange("p (t n) -> p t n", t=TILES + TPG)
        vcols = GB * PAIRS * 2 * VW + S - 2 * VW
        self.Vblk = [sb(f"Vblk{i}", [P, vcols]) for i in range(2)]
        self.xn = sb("xn", [P, TPG, D])
        self.hT = [sb(f"hT{i}", [P, GT]) for i in range(2)]
        self.tmp = sb("tmp", [P, GT])
        work = shared("work", max(b.width for b in (ATT_BUF, EXP_BUF, F2_BUF, MIX_BUF)))

        def att(name):
            return ATT_BUF(work, name)

        def exp(name):
            return EXP_BUF(work, name)

        def ffn(name):
            return F2_BUF(work, name)

        def mix(name):
            return MIX_BUF(work, name)

        self.probs = [att("probs0"), att("probs1")]
        self.PT = [att("PT0"), att("PT1")]
        self.Kblk = [att(f"Kblk{i}").rearrange("p (b h n) -> p b h n", b=4, h=H) for i in range(2)]
        self.QT, self.KT = [att("QT0"), att("QT1")], att("KT")
        self.ctxT = [att("ctxT0"), att("ctxT1")]
        self.attn = [att(f"attn{i}").rearrange("p (c n) -> p c n", c=TPG) for i in range(2)]
        self.aT = att("aT")
        self.soft = [att(f"soft{i}").rearrange("p (c n) -> p c n", c=TPG) for i in range(2)]
        self.ctxN = [X2_BUF(work, f"ctxN{i}")[0:S].rearrange("p (b n) -> p b n", b=GB) for i in range(2)]
        self.route = mix("route").rearrange("p (t e) -> p t e", t=TILES)
        self.anchor = mix("anchor").rearrange("p (t e) -> p t e", t=TILES)
        self.split_u3 = mix("split_u")
        self.route8 = exp("route").rearrange("p (t e) -> p t e", t=TILES)
        self.hid = [exp(f"hid{i}").rearrange("p (f n) -> p f n", f=4) for i in range(2)]
        self.silu = exp("silu").rearrange("p (f n) -> p f n", f=2)
        self.HThigh, self.HTlow, self.w_low = (
            rounded(n, "work", EXP_BUF.at[n][0], 4096) for n in ("HThigh", "HTlow", "w_low"))
        self.split_u = exp("split_u")
        self.lrT = [ffn("lrT0")[0:DL + 1], ffn("lrT1")[0:DL + 1]]
        self.relu = [ffn("relu0"), ffn("relu1")]
        self.hidc, self.eq, self.hidcT = [ffn("hidc0"), ffn("hidc1")], [ffn("eq0"), ffn("eq1")], ffn("hidcT")
        self.silu3, self.up3 = [mix("silu30"), mix("silu31")], [mix("up30"), mix("up31")]
        self.hid3, self.hid3T = [mix("hid30"), mix("hid31")], [mix("hid3T0"), mix("hid3T1")]
        self.hx = [rounded(n, "work", MIX_BUF.at[n][0], GT) for n in ("hx_high", "hx_low")]

        self.bn, self.mv = sb("bn", [P, TPG, 6]), sb("mv", [P, TPG, 2])
        self.veps, self.rstd, self.rms = (sb(n, [P, TPG]) for n in ("veps", "rstd", "rms"))
        self.minus_half, self.eps = sb("minus_half", [P, TPG]), sb("eps", [P, TPG])
        self.zero, self.gate, self.alpha = sb("zero", [P, 1]), sb("gate", [P, 4]), sb("alpha", [P, 1])
        self.onesrow = sb("onesrow", [P, GT])
        self.top, self.rsum = sb("top", [P, 2 * H]), sb("rsum", [P, H])
        self.gates, self.decay, self.b2c = sb("gates", [P, 8]), sb("decay", [P, S]), sb("b2c", [P, D])[:, :]
        self.bqs = {n: sb(f"bqs_{n}", [P, 1])[:, :] for n in ("x0", "x1", "x3")}
        self.wo = {n: sb(f"wo_{n}s", [P, D])[:, :] for n in ("x0", "x1", "x3")}
        self.bo = {n: sb(f"bo_{n}s", [P, D])[:, :] for n in ("x0", "x1", "x3")}
        self.wo["f0"] = ATT_W(self.att_w, "wo_f0")
        self.decay = self.decay[:, :]
        self.wc, self.bc = sb("wc", [P, D])[:, :], sb("bc", [P, 2])
        self.lg, self.taken = sb("lg", [P, TPG, 16]), sb("taken", [P, TPG, E3 + 8])
        self.cand, self.ex = sb("cand", [P, TPG, E3 + 8]), sb("ex", [P, TPG, E3])
        self.sg, self.sc = sb("sg", [P, TPG, E3]), sb("sc", [P, TPG, E3])
        self.t8, self.m8 = sb("t8", [P, TPG, 8]), sb("m8", [P, TPG, 8])
        self.g8, self.gm = sb("g8", [P, TPG, G3, 8]), sb("gm", [P, TPG, 2, G3])
        self.pk, self.wt = sb("pk", [P, 2, TPG, 8]), sb("wt", [P, TPG, E1])
        self.wtT, self.sm = sb("wtT", [E1, GT]), sb("sm", [P, 16])

        psum = ctx.enter_context(nc.psum_tensor("psum", [P, 8, GT], F32))
        self.bank = [psum[:, i, :] for i in range(8)]
        self.scores = [psum[:, 2 * i:2 * i + 2, :].rearrange("p a (h n) -> p (a h) n", n=S) for i in range(2)]

        a, b = self.arena_a, self.arena_b
        n0, n1 = E0 * 2 * F0, E1 * F1
        self.experts = {
            "f0": (a[:, 0:n0].rearrange("p (e f) -> p e f", e=E0),
                   a[:, n0:F0_COLS].rearrange("p (e f n) -> p e f n", e=E0, n=D)),
            "f1": (b[:, 0:n1].rearrange("p (e f) -> p e f", e=E1),
                   b[:, n1:2 * n1].rearrange("p (e f n) -> p e f n", e=E1, n=D))}
        self.b1e = b[:, 2 * n1:F1_COLS]
        self.w_high = {"f0": rounded("f0_high", "arena_a", 0, n0), "f1": rounded("f1_high", "arena_b", 0, n1)}
        self.w3g, self.w3u = a[:, 0:UP3], a[:, UP3:2 * UP3]
        high3 = rounded("f3_high", "arena_a", 0, 2 * UP3)
        low3 = rounded("f3_low", "work", MIX_BUF.at["w_low"][0], 2 * UP3)
        self.w3g_parts, self.w3u_parts = ([v[:, c:c + UP3] for v in (high3, low3)] for c in (0, UP3))
        self.w3d = a[:, 2 * UP3:F3_COLS].rearrange("p (c n) -> p c n", n=D)
        self.m1, self.m2, self.w1c = (F2_W(self.f2_w, n) for n in ("m1", "m2", "w1"))
        self.m2 = self.m2[0:DL + 1]
        self.w2c = F2_W(self.f2_w, "w2").rearrange("p (c n) -> p c n", n=D)

        self.ctxT_dram, self.ctxN_dram = ins["ctx_t"], ins["ctx_n"]
        self.loaded = {n: self.sem(f"loaded_{n}") for n in ("small", "x", "f0", "f1", "f2", "f3")}
        self.loads = {"f0": 2, "f1": 3, "f2": 1, "f3": 2}
        self.s_part, self.s_out = self.sem("part_done"), self.sem("out_stored")
        self.s_gates, self.s_fold, self.s_consts = self.sem("gates"), self.sem("fold"), self.sem("constants")
        self.s_prepared = self.sem("prepared")
        self.program = [Attention(self, "x0"), Attention(self, "f0"), Experts(self, "f0"), Attention(self, "x1"),
                        Experts(self, "f1"), WholeAttention(self), Choices(self), Attention(self, "x3"), Mixture(self)]

    def signals(self, times):
        past = {}
        for name, n in times.items():
            if name not in self.named:
                self.named[name] = self.sem(name)
            past[name] = self.given.get(name, 0)
            self.given[name] = past[name] + n
        return {name: self.named[name] for name in times}, past

    def sem(self, name):
        return self.ctx.enter_context(self.nc.semaphore("s_" + name))

    def load(self, sp):
        i, small = self.ins, self.loaded["small"]
        sp.dma_start(self.rows[:, :], i["rows"].rearrange("a n -> (a n)").partition_broadcast(P)).then_inc(small, 16)
        sp.dma_start(self.att_w[:, :], i["att_w"]).then_inc(small, 16)
        sp.dma_start(self.const[:, :], i["const"]).then_inc(small, 16)
        sp.dma_start(self.X[:, 0:TILES, :], i["x"]).then_inc(self.loaded["x"], 16)

    def load_expert(self, sp, name, tile, cols):
        src = self.ins[name + "_w"]
        half = cols // 2
        for a, b in ((0, half), (half, cols)):
            sp.dma_start(tile[:, a:b], src[:, a:b]).then_inc(self.loaded[name], 16)

    def load_late(self, sp, n):
        if n == 0:
            self.load_expert(sp, "f0", self.arena_a, F0_COLS)
            sp.dma_start(self.f2_w[:, :], self.ins["f2_w"]).then_inc(self.loaded["f2"], 16)
        if n == 3:
            self.load_expert(sp, "f1", self.arena_b, F1_COLS)
            sp.dma_start(self.b2e[:, :], self.ins["b2e"]).then_inc(self.loaded["f1"], 16)
            self.load_expert(sp, "f3", self.arena_a, F3_COLS)

    def enter(self, eng, n):
        if n:
            eng.wait_ge(self.s_part, 4 * n)
        else:
            eng.wait_ge(self.loaded["small"], 48)
            eng.wait_ge(self.loaded["x"], 16)
            eng.wait_ge(self.s_prepared, 2)

    def prepare_gpsimd(self, pool):
        pool.memset(self.minus_half[:, :], -0.5)
        pool.memset(self.eps[:, :], EPS)
        pool.memset(self.zero[:, :], 0.0)
        pool.memset(self.gate[:, :], 1.0)
        pool.memset(self.X[:, TILES:TILES + TPG, :], 0.0)
        pool.memset(self.onesrow[:, :], 1.0)
        for v in self.Vblk:
            pool.memset(v[:, :], 0.0)
        pool.drain()
        for v in self.Vblk:
            w = v[:, 0:GB * PAIRS * 2 * VW].rearrange("p (r x) -> p r x", r=GB * PAIRS)
            pool.memset(w[0:S, :, DK:DK + 1], 1.0)
            pool.memset(w[S:P, :, 2 * VW - 1:2 * VW], 1.0)
        pool.drain().then_inc(self.s_prepared, 1)

    def prepare_scalar(self, act):
        act.wait_ge(self.loaded["small"], 48)
        act.activation(self.gates[:, :], ROWS(self.rows, "g"), ACT.Tanh).then_inc(self.s_gates, 1)

    def prepare_tensor(self, pe):
        pe.wait_ge(self.loaded["small"], 48)
        for i, n in enumerate(("x0", "x1", "x3")):
            pe.matmul(self.bank[i][:, 0:D], ATT_W(self.att_w, f"bv_{n}").broadcast_to([P, P]),
                      ATT_W(self.att_w, f"wo_{n}"), start=True, stop=True)
        w1, w2t = ATT_W(self.att_w, "w1_x2"), ATT_W(self.att_w, "w2t_x2")
        pe.matmul(self.bank[3][:, 0:D], w1, w2t, start=True, stop=True)
        for _ in range(2):
            pe.drain().then_inc(self.named["aTp"], 1)
        pe.matmul(self.bank[4][:, 0:1], w2t, ATT_W(self.att_w, "b1_x2"), start=True, stop=True).then_inc(self.s_fold, 1)

    def prepare_vector(self, dve):
        for _ in range(2):
            dve.drain().then_inc(self.named["X"], 1)
        dve.wait_ge(self.s_gates, 1)
        dve.wait_ge(self.s_fold, 1)
        dve.memset(self.alpha[:, :], 0.1)
        dve.tensor_scalar(self.decay, CONST(self.const, "dist"), ROWS(self.rows, "decay"), None, ALU.mult)
        dve.tensor_scalar(self.b2c, ROWS(self.rows, "b2_f2"), self.gates[:, 6:7], None, ALU.mult)
        dve.tensor_copy(self.wc, self.bank[3][:, 0:D])
        dve.tensor_tensor(self.bc[:, 0:1], self.bank[4][:, 0:1], ATT_W(self.att_w, "b2_x2"), ALU.add)
        for i, (n, g) in enumerate((("x0", 0), ("x1", 1), ("x3", 3))):
            dve.tensor_scalar(self.bqs[n], ATT_W(self.att_w, f"bq_{n}"), DK ** -0.5, None, ALU.mult)
            dve.tensor_scalar(self.wo[n], ATT_W(self.att_w, f"wo_{n}"), self.gates[:, g:g + 1], None, ALU.mult)
            dve.tensor_tensor(self.bo[n], self.bank[i][:, 0:D], ROWS(self.rows, f"bo_{n}"), ALU.add)
        dve.drain()
        for n, g in (("x0", 0), ("x1", 1), ("x3", 3)):
            dve.tensor_scalar(self.bo[n], self.bo[n], self.gates[:, g:g + 1], None, ALU.mult)
        dve.tensor_scalar(self.bc[:, 1:2], self.bc[:, 0:1], D ** -0.5, None, ALU.mult)
        dve.tensor_scalar(self.alpha[:, :], self.alpha[:, :], self.gates[:, 7:8], None, ALU.mult)
        dve.drain().then_inc(self.s_prepared, 1)


def kernel(**inputs):
    import concourse.bacc as bacc
    from concourse.bass_utils import run_bass_kernel_spmd

    arrays = {n: np.ascontiguousarray(v) for n, v in kernel_inputs(inputs).items()}
    nc = bacc.Bacc("TRN2", target_bir_lowering=False, num_devices=1)
    ins = {n: nc.dram_tensor(n + "_dram", v.shape, mybir.dt.from_np(v.dtype), kind="ExternalInput").ap()
           for n, v in arrays.items()}
    out = nc.dram_tensor("out_dram", (P, TILES, D), F32, kind="ExternalOutput").ap()
    build(nc, ins, out)
    r = run_bass_kernel_spmd(nc, [{n + "_dram": v for n, v in arrays.items()}], core_ids=[0])
    return r.results[0]["out_dram"].transpose(1, 0, 2).reshape(B, S, D)
```
